# Optimizing a Trainium2 kernel written in Bass

```python
import numpy as np
import jax
import jax.numpy as jnp

def _softmax(x, axis=-1):
    return jax.nn.softmax(x, axis=axis)

def _gelu(x):
    return jax.nn.gelu(x, approximate=True)

def _silu(x):
    return jax.nn.silu(x)

def _sigmoid(x):
    return jax.nn.sigmoid(x)

def _layernorm(x, axis=-1, eps=1e-05):
    m = jnp.mean(x, axis=axis, keepdims=True)
    v = jnp.var(x, axis=axis, keepdims=True)
    return (x - m) / jnp.sqrt(v + eps)

def _scatter_add(tgt, idx, src, axis=0):
    return tgt.at[idx].add(src)

def _segment_sum(src, seg, n):
    return jax.ops.segment_sum(src, seg, n)
kernel_name = 'mk_decoder_postln_d1_seqx_r8_f287f1'

def setup_inputs(seed: int=0):
    np.random.seed(seed)
    _w = jnp.asarray

    def _rec_inputs():
        import jax
        import jax.numpy as jnp
        _rk = jax.random.key(seed)
        x = -0.0003929 + 0.9999 * jax.random.normal(jax.random.fold_in(_rk, 1), (32, 64, 128), jnp.float32)
        _lenS = 64 - jax.random.randint(jax.random.fold_in(_rk, 7), (32,), 0, max(1, 64 // 4) + 1, jnp.int32)
        _lenS2 = 64 - jax.random.randint(jax.random.fold_in(_rk, 8), (32,), 0, max(1, 64 // 4) + 1, jnp.int32)
        _ctx_1024P = jax.random.normal(jax.random.fold_in(_rk, 11), (32, 16, 128), jnp.float32)
        _ctx_1024c = jax.random.dirichlet(jax.random.fold_in(_rk, 511), 0.3 * jnp.ones((16,), jnp.float32), (32, 64))
        _ctx_1024t = jnp.einsum('bsk,bkd->bsd', _ctx_1024c, _ctx_1024P)
        _ctx_1024t = _ctx_1024t * jax.lax.rsqrt(jnp.mean(jnp.square(_ctx_1024t)) + 1e-12) * 0.953939
        ctx_1024 = 2.81802e-05 + 1.00001 * (_ctx_1024t + 0.3 * jax.random.normal(jax.random.fold_in(_rk, 611), (32, 64, 128), jnp.float32))
        return (x, ctx_1024)
    x, ctx_1024 = _rec_inputs()

    def _L0_attn_setup():
        import jax, jax.numpy as jnp
        import numpy as np
        B, T, D = (1, 256, 128)
        H = 16
        SEM_DIM, GEO_DIM, ATTN_DIM = (64, 64, 128)
        ROPE_BASE = 10000.0
        NEG = -1000000000.0

        def _heads(y, hd):
            b, t, _ = y.shape
            return y.reshape(b, t, H, hd).transpose(0, 2, 1, 3)

        def _rope(x, cos, sin):
            hd = x.shape[-1]
            x1, x2 = (x[..., :hd // 2], x[..., hd // 2:])
            c = cos[None, None]
            sn = sin[None, None]
            return jnp.concatenate([x1 * c - x2 * sn, x2 * c + x1 * sn], axis=-1)

        def _forward(x, wq_sem, wk_sem, wq_geo, wk_geo, wv, wo, k_sem_null, k_geo_null, v_null):
            b, t, _ = x.shape
            sem_hd = wq_sem.shape[1] // H
            geo_hd = wq_geo.shape[1] // H
            v_hd = wv.shape[1] // H
            sem_scale = 1.0 / np.sqrt(sem_hd)
            geo_scale = 1.0 / np.sqrt(geo_hd)
            qs = _heads(x @ wq_sem, sem_hd)
            ks = _heads(x @ wk_sem, sem_hd)
            qg = _heads(x @ wq_geo, geo_hd)
            kg = _heads(x @ wk_geo, geo_hd)
            v = _heads(x @ wv, v_hd)
            pos = jnp.arange(t, dtype=jnp.float32)
            inv_freq = 1.0 / ROPE_BASE ** (jnp.arange(0, geo_hd, 2, dtype=jnp.float32) / geo_hd)
            ang = pos[:, None] * inv_freq[None, :]
            cos, sin = (jnp.cos(ang), jnp.sin(ang))
            qg = _rope(qg, cos, sin)
            kg = _rope(kg, cos, sin)
            ksn = jnp.broadcast_to(k_sem_null.reshape(1, 1, H, sem_hd).transpose(0, 2, 1, 3), (b, H, 1, sem_hd))
            kgn = jnp.broadcast_to(k_geo_null.reshape(1, 1, H, geo_hd).transpose(0, 2, 1, 3), (b, H, 1, geo_hd))
            vn = jnp.broadcast_to(v_null.reshape(1, 1, H, v_hd).transpose(0, 2, 1, 3), (b, H, 1, v_hd))
            ks_full = jnp.concatenate([ksn, ks], axis=2)
            kg_full = jnp.concatenate([kgn, kg], axis=2)
            v_full = jnp.concatenate([vn, v], axis=2)
            scores = jnp.einsum('bhqd,bhkd->bhqk', qs, ks_full).astype(jnp.float32) * sem_scale + jnp.einsum('bhqd,bhkd->bhqk', qg, kg_full).astype(jnp.float32) * geo_scale
            causal = jnp.tril(jnp.ones((t, t), dtype=bool))
            mask = jnp.concatenate([jnp.ones((t, 1), dtype=bool), causal], axis=1)
            scores = jnp.where(mask[None, None], scores, NEG)
            probs = jax.nn.softmax(scores, axis=-1).astype(v.dtype)
            out = jnp.einsum('bhqk,bhkd->bhqd', probs, v_full)
            out = out.transpose(0, 2, 1, 3).reshape(b, t, H * v_hd)
            return out @ wo
        key = jax.random.key(seed)
        ks = jax.random.split(key, 10)
        s = 0.02
        return {'x': jax.random.normal(ks[0], (B, T, D), jnp.float32), 'wq_sem': jax.random.normal(ks[1], (D, SEM_DIM), jnp.float32) * s, 'wk_sem': jax.random.normal(ks[2], (D, SEM_DIM), jnp.float32) * s, 'wq_geo': jax.random.normal(ks[3], (D, GEO_DIM), jnp.float32) * s, 'wk_geo': jax.random.normal(ks[4], (D, GEO_DIM), jnp.float32) * s, 'wv': jax.random.normal(ks[5], (D, ATTN_DIM), jnp.float32) * s, 'wo': jax.random.normal(ks[6], (ATTN_DIM, D), jnp.float32) * s, 'k_sem_null': jax.random.normal(ks[7], (SEM_DIM,), jnp.float32) * s, 'k_geo_null': jax.random.normal(ks[8], (GEO_DIM,), jnp.float32) * s, 'v_null': jax.random.normal(ks[9], (ATTN_DIM,), jnp.float32) * s}
    _L0_attn_all = _L0_attn_setup()
    _L0_attn_in = {k: v for k, v in _L0_attn_all.items() if k in ('wq_sem', 'wk_sem', 'wq_geo', 'wk_geo', 'wv', 'wo', 'k_sem_null', 'k_geo_null', 'v_null')}
    del _L0_attn_all

    def _L0_xattn_setup():
        import jax, jax.numpy as jnp
        import numpy as np
        from functools import partial
        FACTOR = 5
        N_HEADS = 16

        def _time_delay_agg(values, corr):
            B, H, L, C = values.shape
            top_k = int(FACTOR * np.log(L + 1)) if L > 1 else 1
            top_k = max(1, min(top_k, L))
            mean_value = corr.mean(axis=1).mean(axis=1)
            mean_across_batch = mean_value.mean(axis=0)
            actual_k = min(top_k, C)
            _, indices = jax.lax.top_k(mean_across_batch, actual_k)
            selected = mean_value[:, indices]
            weights = jax.nn.softmax(selected, axis=-1)
            t = jnp.arange(L)

            def body(acc, inp):
                d, w = inp
                idx = (t + d) % L
                acc = acc + values[:, :, idx, :] * w[:, None, None, None]
                return (acc, None)
            agg, _ = jax.lax.scan(body, jnp.zeros_like(values), (indices, weights.T))
            return agg
        key = jax.random.key(seed)
        ks = jax.random.split(key, 8)
        B, L, D = (4, 512, 128)
        scale = 0.02
        return {'q': jax.random.normal(ks[0], (B, L, D), jnp.float32), 'k': jax.random.normal(ks[1], (B, L, D), jnp.float32), 'v': jax.random.normal(ks[2], (B, L, D), jnp.float32), 'Wq': jax.random.normal(ks[3], (D, D), jnp.float32) * scale, 'bq': jnp.zeros((D,), jnp.float32), 'Wk': jax.random.normal(ks[4], (D, D), jnp.float32) * scale, 'bk': jnp.zeros((D,), jnp.float32), 'Wv': jax.random.normal(ks[5], (D, D), jnp.float32) * scale, 'bv': jnp.zeros((D,), jnp.float32), 'Wo': jax.random.normal(ks[6], (D, D), jnp.float32) * scale, 'bo': jnp.zeros((D,), jnp.float32)}
    _L0_xattn_all = _L0_xattn_setup()
    _L0_xattn_in = {k: v for k, v in _L0_xattn_all.items() if k in ('Wq', 'bq', 'Wk', 'bk', 'Wv', 'bv', 'Wo', 'bo')}
    del _L0_xattn_all

    def _L0_ffn_setup():
        import jax, jax.numpy as jnp
        import numpy as np
        B, S, D, F, E = (4, 256, 128, 512, 8)
        key = jax.random.key(seed)
        ks = jax.random.split(key, 7)
        s1 = 1.0 / np.sqrt(D)
        s2 = 1.0 / np.sqrt(F)
        x = jax.random.normal(ks[0], (B, S, D), dtype=jnp.float32)
        W1 = jax.random.uniform(ks[1], (E, D, F), jnp.float32, -s1, s1)
        b1 = jax.random.uniform(ks[2], (E, F), jnp.float32, -s1, s1)
        W2 = jax.random.uniform(ks[3], (E, F, D), jnp.float32, -s2, s2)
        b2 = jax.random.uniform(ks[4], (E, D), jnp.float32, -s2, s2)
        Wr = jax.random.uniform(ks[5], (D, E), jnp.float32, -s1, s1)
        br = jax.random.uniform(ks[6], (E,), jnp.float32, -s1, s1)
        return {'x': x, 'W1': W1, 'b1': b1, 'W2': W2, 'b2': b2, 'Wr': Wr, 'br': br}
    _L0_ffn_all = _L0_ffn_setup()
    _L0_ffn_in = {k: v for k, v in _L0_ffn_all.items() if k in ('W1', 'b1', 'W2', 'b2', 'Wr', 'br')}
    del _L0_ffn_all
    return {'x': x, 'ctx_1024': ctx_1024, 'L0_attn_wq_sem': _L0_attn_in['wq_sem'], 'L0_attn_wk_sem': _L0_attn_in['wk_sem'], 'L0_attn_wq_geo': _L0_attn_in['wq_geo'], 'L0_attn_wk_geo': _L0_attn_in['wk_geo'], 'L0_attn_wv': _L0_attn_in['wv'], 'L0_attn_wo': _L0_attn_in['wo'], 'L0_attn_k_sem_null': _L0_attn_in['k_sem_null'], 'L0_attn_k_geo_null': _L0_attn_in['k_geo_null'], 'L0_attn_v_null': _L0_attn_in['v_null'], 'L0_xattn_Wq': _L0_xattn_in['Wq'], 'L0_xattn_bq': _L0_xattn_in['bq'], 'L0_xattn_Wk': _L0_xattn_in['Wk'], 'L0_xattn_bk': _L0_xattn_in['bk'], 'L0_xattn_Wv': _L0_xattn_in['Wv'], 'L0_xattn_bv': _L0_xattn_in['bv'], 'L0_xattn_Wo': _L0_xattn_in['Wo'], 'L0_xattn_bo': _L0_xattn_in['bo'], 'L0_ffn_W1': _L0_ffn_in['W1'], 'L0_ffn_b1': _L0_ffn_in['b1'], 'L0_ffn_W2': _L0_ffn_in['W2'], 'L0_ffn_b2': _L0_ffn_in['b2'], 'L0_ffn_Wr': _L0_ffn_in['Wr'], 'L0_ffn_br': _L0_ffn_in['br']}

def reference(x, ctx_1024, L0_attn_wq_sem, L0_attn_wk_sem, L0_attn_wq_geo, L0_attn_wk_geo, L0_attn_wv, L0_attn_wo, L0_attn_k_sem_null, L0_attn_k_geo_null, L0_attn_v_null, L0_xattn_Wq, L0_xattn_bq, L0_xattn_Wk, L0_xattn_bk, L0_xattn_Wv, L0_xattn_bv, L0_xattn_Wo, L0_xattn_bo, L0_ffn_W1, L0_ffn_b1, L0_ffn_W2, L0_ffn_b2, L0_ffn_Wr, L0_ffn_br):
    import jax
    import jax.numpy as jnp

    def _L0_attn_ref(x, wq_sem, wk_sem, wq_geo, wk_geo, wv, wo, k_sem_null, k_geo_null, v_null):
        import jax, jax.numpy as jnp
        import numpy as np
        B, T, D = (1, 256, 128)
        H = 16
        SEM_DIM, GEO_DIM, ATTN_DIM = (64, 64, 128)
        ROPE_BASE = 10000.0
        NEG = -1000000000.0

        def _heads(y, hd):
            b, t, _ = y.shape
            return y.reshape(b, t, H, hd).transpose(0, 2, 1, 3)

        def _rope(x, cos, sin):
            hd = x.shape[-1]
            x1, x2 = (x[..., :hd // 2], x[..., hd // 2:])
            c = cos[None, None]
            sn = sin[None, None]
            return jnp.concatenate([x1 * c - x2 * sn, x2 * c + x1 * sn], axis=-1)

        def _forward(x, wq_sem, wk_sem, wq_geo, wk_geo, wv, wo, k_sem_null, k_geo_null, v_null):
            b, t, _ = x.shape
            sem_hd = wq_sem.shape[1] // H
            geo_hd = wq_geo.shape[1] // H
            v_hd = wv.shape[1] // H
            sem_scale = 1.0 / np.sqrt(sem_hd)
            geo_scale = 1.0 / np.sqrt(geo_hd)
            qs = _heads(x @ wq_sem, sem_hd)
            ks = _heads(x @ wk_sem, sem_hd)
            qg = _heads(x @ wq_geo, geo_hd)
            kg = _heads(x @ wk_geo, geo_hd)
            v = _heads(x @ wv, v_hd)
            pos = jnp.arange(t, dtype=jnp.float32)
            inv_freq = 1.0 / ROPE_BASE ** (jnp.arange(0, geo_hd, 2, dtype=jnp.float32) / geo_hd)
            ang = pos[:, None] * inv_freq[None, :]
            cos, sin = (jnp.cos(ang), jnp.sin(ang))
            qg = _rope(qg, cos, sin)
            kg = _rope(kg, cos, sin)
            ksn = jnp.broadcast_to(k_sem_null.reshape(1, 1, H, sem_hd).transpose(0, 2, 1, 3), (b, H, 1, sem_hd))
            kgn = jnp.broadcast_to(k_geo_null.reshape(1, 1, H, geo_hd).transpose(0, 2, 1, 3), (b, H, 1, geo_hd))
            vn = jnp.broadcast_to(v_null.reshape(1, 1, H, v_hd).transpose(0, 2, 1, 3), (b, H, 1, v_hd))
            ks_full = jnp.concatenate([ksn, ks], axis=2)
            kg_full = jnp.concatenate([kgn, kg], axis=2)
            v_full = jnp.concatenate([vn, v], axis=2)
            scores = jnp.einsum('bhqd,bhkd->bhqk', qs, ks_full).astype(jnp.float32) * sem_scale + jnp.einsum('bhqd,bhkd->bhqk', qg, kg_full).astype(jnp.float32) * geo_scale
            causal = jnp.tril(jnp.ones((t, t), dtype=bool))
            mask = jnp.concatenate([jnp.ones((t, 1), dtype=bool), causal], axis=1)
            scores = jnp.where(mask[None, None], scores, NEG)
            probs = jax.nn.softmax(scores, axis=-1).astype(v.dtype)
            out = jnp.einsum('bhqk,bhkd->bhqd', probs, v_full)
            out = out.transpose(0, 2, 1, 3).reshape(b, t, H * v_hd)
            return out @ wo
        return _forward(x, wq_sem, wk_sem, wq_geo, wk_geo, wv, wo, k_sem_null, k_geo_null, v_null)

    def _L0_xattn_ref(q, k, v, Wq, bq, Wk, bk, Wv, bv, Wo, bo):
        import jax, jax.numpy as jnp
        import numpy as np
        from functools import partial
        FACTOR = 5
        N_HEADS = 16

        def _time_delay_agg(values, corr):
            B, H, L, C = values.shape
            top_k = int(FACTOR * np.log(L + 1)) if L > 1 else 1
            top_k = max(1, min(top_k, L))
            mean_value = corr.mean(axis=1).mean(axis=1)
            mean_across_batch = mean_value.mean(axis=0)
            actual_k = min(top_k, C)
            _, indices = jax.lax.top_k(mean_across_batch, actual_k)
            selected = mean_value[:, indices]
            weights = jax.nn.softmax(selected, axis=-1)
            t = jnp.arange(L)

            def body(acc, inp):
                d, w = inp
                idx = (t + d) % L
                acc = acc + values[:, :, idx, :] * w[:, None, None, None]
                return (acc, None)
            agg, _ = jax.lax.scan(body, jnp.zeros_like(values), (indices, weights.T))
            return agg
        B, L, D = q.shape
        H = N_HEADS
        dk = D // H

        def proj(x, W, b):
            y = x @ W.T + b
            return y.reshape(B, L, H, dk).transpose(0, 2, 1, 3)
        Q = proj(q, Wq, bq).astype(jnp.float32)
        K = proj(k, Wk, bk).astype(jnp.float32)
        V = proj(v, Wv, bv).astype(jnp.float32)
        Qf = jnp.fft.rfft(Q, axis=2)
        Kf = jnp.fft.rfft(K, axis=2)
        R = jnp.fft.irfft(Qf * jnp.conj(Kf), n=L, axis=2)
        V_agg = _time_delay_agg(V, R)
        V_agg = V_agg.transpose(0, 2, 1, 3).reshape(B, L, D)
        return V_agg @ Wo.T + bo

    def _L0_ffn_ref(x, W1, b1, W2, b2, Wr, br):
        import jax, jax.numpy as jnp
        import numpy as np
        B, S, D, F, E = (4, 256, 128, 512, 8)
        b, s, d = x.shape
        e = Wr.shape[1]
        logits = x @ Wr + br
        idx = jnp.argmax(logits, axis=-1)
        probs = jax.nn.softmax(logits, axis=-1)
        gates = jnp.take_along_axis(probs, idx[..., None], axis=-1)[..., 0]
        xf = x.reshape(-1, d)
        idxf = idx.reshape(-1)
        gf = gates.reshape(-1)
        out = jnp.zeros_like(xf)
        for ei in range(e):
            h = jax.nn.gelu(xf @ W1[ei] + b1[ei], approximate=False)
            y = h @ W2[ei] + b2[ei]
            mask = (idxf == ei).astype(xf.dtype)
            out = out + y * (gf * mask)[:, None]
        return out.reshape(b, s, d)
    x = _layernorm(x + _L0_attn_ref(x, L0_attn_wq_sem, L0_attn_wk_sem, L0_attn_wq_geo, L0_attn_wk_geo, L0_attn_wv, L0_attn_wo, L0_attn_k_sem_null, L0_attn_k_geo_null, L0_attn_v_null), axis=-1)
    x = _layernorm(x + _L0_xattn_ref(x, ctx_1024, ctx_1024, L0_xattn_Wq, L0_xattn_bq, L0_xattn_Wk, L0_xattn_bk, L0_xattn_Wv, L0_xattn_bv, L0_xattn_Wo, L0_xattn_bo), axis=-1)
    x = _layernorm(x + _L0_ffn_ref(x, L0_ffn_W1, L0_ffn_b1, L0_ffn_W2, L0_ffn_b2, L0_ffn_Wr, L0_ffn_br), axis=-1)
    return x

_drawn_inputs = setup_inputs


def setup_inputs(seed=0):
    import zlib

    import numpy as np

    out = dict(_drawn_inputs(seed))
    spreads = {'L0_xattn_bq': (0.0, 0.8),
     'L0_xattn_bk': (0.0, 0.8),
     'L0_xattn_bv': (0.0, 0.33),
     'L0_xattn_bo': (0.0, 0.1)}
    factors = {'L0_attn_wq_sem': 8.0,
     'L0_attn_wk_sem': 8.0,
     'L0_attn_wq_geo': 8.0,
     'L0_attn_wk_geo': 8.0,
     'L0_attn_wv': 4.664,
     'L0_attn_wo': 4.495,
     'L0_attn_k_sem_null': 63.442,
     'L0_attn_k_geo_null': 64.0,
     'L0_attn_v_null': 27.205,
     'L0_xattn_Wq': 25.61,
     'L0_xattn_Wk': 8.0,
     'L0_ffn_b1': 8.0,
     'L0_ffn_b2': 8.0,
     'L0_ffn_br': 3.978}
    for name, (base, spread) in spreads.items():
        noise = np.random.default_rng([zlib.crc32(name.encode()), seed]).standard_normal(out[name].shape)
        drawn = base * np.exp(spread * noise) if base else spread * noise
        out[name] = jnp.asarray(drawn.astype(out[name].dtype))
    for name, factor in factors.items():
        out[name] = (out[name] * factor).astype(out[name].dtype)
    return out
```

```python
from contextlib import ExitStack

import numpy as np
import concourse.bass as bass
from concourse import mybir

ALU = mybir.AluOpType
ACT = mybir.ActivationFunctionType
AX = mybir.AxisListType
F32 = mybir.dt.float32
BF16 = mybir.dt.bfloat16
I32 = mybir.dt.int32
U32 = mybir.dt.uint32

P = 128
B, T, D = 32, 64, 128
H, HD = 16, 8
E, F = 8, 512
NT = B * T // P
BPT = P // T
EPS = 1e-5
STRIPS, HPS = 4, 4
FC = F // P
SLOTS = (NT * P + E * (P - 1)) // P
ROW = D + 2
NO_TOKEN = 1 << 20
SCALE = 0.5
VW = P + 16

CONSTS = [("ident", 128), ("cos8", 8), ("sin4", 4), ("strip", 4), ("strip_head", 4), ("head16", 16), ("row_head", 128),
          ("den_ones", 64), ("chan8", 8), ("batch_rows", 128), ("batch_tile", 128), ("tap_of", 64),
          ("band", 128), ("batch_ind", 2), ("rev8", 8), ("thresholds", 16), ("before8", 64),
          ("slot_j", SLOTS), ("minus_half", 16), ("causal", T), ("earlier", P)]
COL, _at = {}, 0
for _n, _w in CONSTS:
    COL[_n] = (_at, _at + _w)
    _at += _w
NCONST = _at


class Tile:

    def __init__(self, c, i=None, U=1):
        self.c, self.i, self.U = c, i, U
        self.n = c if i is None else i * U + c

    def __add__(self, k):
        return Tile(self.c + k, self.i, self.U)

    def ring(self, size):
        return self.c % size

    def turn(self, size):
        return self.c // size if self.i is None else self.i * (self.U // size) + self.c // size


def run_steps(eng, step, total, U, tail):
    looped = (total - tail) // U
    with eng.Fori(0, looped) as i:
        for c in range(U):
            step(Tile(c, i, U), False)
    for n in range(looped * U, total):
        step(Tile(n), True)


def decoder_layer(nc, a, out):
    with ExitStack() as ctx:
        def sb(name, shape, dt=F32):
            return ctx.enter_context(nc.sbuf_tensor(name, shape, dt))

        def sem(name):
            return ctx.enter_context(nc.semaphore(name))

        rows_dram = nc.dram_tensor("token_rows", (SLOTS * P, ROW), F32, kind="Internal").ap()
        ps = ctx.enter_context(nc.psum_tensor("ps", [P, 8, 512], F32))
        consts = sb("consts", [P, NCONST])
        cb = sb("cb", [P, 128 + 512 + 128 + 128], BF16)
        wqk, wv, wo = sb("wqk", [P, 384]), sb("wv", [P, P]), sb("wo", [P, P])
        xattn_w = sb("xattn_w", [P, 4, P])
        cols = sb("cols", [P, 4])
        vnull_bc, bo_bc = sb("vnull_bc", [16, P]), sb("bo_bc", [P, P])
        wr, br_bc = sb("wr", [P, E]), sb("br_bc", [P, E])
        w1, w2 = sb("w1", [P, E * F]), sb("w2", [P, E * FC * D])
        b1_bc, b2_bc = sb("b1_bc", [P, E * F]), sb("b2_bc", [P, E * D])
        x_all, ctx_all = sb("x_all", [P, NT, D]), sb("ctx_all", [P, NT, D])
        pad_row = sb("pad_row", [P, ROW])
        token_ids = sb("token_ids", [P, NT], I32)

        def const(name, parts=P):
            lo, hi = COL[name]
            return consts[0:parts, lo:hi]

        ident = const("ident")
        ident_b, mask_b, tri_b, ones_b = cb[:, 0:128], cb[:, 128:640], cb[:, 640:768], cb[:, 768:896]

        knull, vnull = sb("knull", [P, H]), sb("vnull", [16, P])
        bv_bc, wvo, bvo = sb("bv_bc", [P, P]), sb("wvo", [P, P]), sb("bvo", [P, P])
        xT = sb("xT", [P, 2, P])
        roped, rope_b = sb("roped", [P, 2, 256]), sb("rope_b", [P, 2, 128])
        qkT, q_strips, k4 = sb("qkT", [P, 2, 2 * P]), sb("q_strips", [P, 2, STRIPS, P]), sb("k4", [P, 2, BPT, HPS, T])
        v_pad = sb("v_pad", [P, 2, 4 * VW])
        null_s = sb("null_s", [P, 2, H])
        row_max, row_max2 = sb("row_max", [P, 2, H]), sb("row_max2", [P, 2, H])
        probs = sb("probs", [P, 2, H * T + H])
        probsT, nullT = sb("probsT", [P, 2, 8, P]), sb("nullT", [16, 2, P])
        rden, attnT = sb("rden", [P, 2, P]), sb("attnT", [P, 2, P])
        y_all, y2_all = sb("y_all", [P, NT, D]), sb("y2_all", [P, NT, D])
        stats, mv, mv2 = sb("stats", [P, NT, 6]), sb("mv", [P, NT]), sb("mv2", [P, NT])
        stats2, mean_gap = sb("stats2", [P, NT, 6]), sb("mean_gap", [P, NT])
        var_eps, rstd = sb("var_eps", [P, 2, NT]), sb("rstd", [P, 2, NT])
        sumT, sqk = sb("sumT", [P, 2, B]), sb("sqk", [P, 3, B])
        wsm = sb("wsm", [B, 4, 8])
        wcol = sb("wcol", [B, 4])
        w_tiles, w_tok = sb("w_tiles", [B, P]), sb("w_tok", [P, P])
        w_taps, w_perm = sb("w_taps", [P, NT * 64]), sb("w_perm", [P, P])
        circ, ctx_in, ctxT, x1b = sb("circ", [P, 2, P]), sb("ctx_in", [P, 2, P]), sb("ctxT", [P, 2, P]), sb("x1b", [P, 2, P])
        x2_in, x2T = sb("x2_in", [P, 2, P]), sb("x2T", [P, 2, P])
        rows = sb("rows", [P, NT, ROW])
        lg, lmax, lex = sb("lg", [P, NT, E]), sb("lmax", [P, NT]), sb("lex", [P, NT, E])
        lsum, eqr, first, onehot = sb("lsum", [P, NT]), sb("eqr", [P, NT, E]), sb("first", [P, NT]), sb("onehot", [P, NT, E], BF16)
        slot_f, slot_a, slots = sb("slot_f", [P, NT, E]), sb("slot_a", [P, NT]), sb("slots", [P, NT], U32)
        cnt, over, ntile = sb("cnt", [P, E]), sb("over", [P, E, 16]), sb("ntile", [P, E])
        tmp64, start_t, end_t = sb("tmp64", [P, E, E]), sb("start_t", [P, E]), sb("end_t", [P, E])
        ge = sb("ge", [P, SLOTS, E])
        e_f, e_i = sb("e_f", [P, SLOTS]), sb("e_i", [P, SLOTS], I32)
        g_rows = sb("g_rows", [P, 4, ROW])
        gxT, hid, gel, gelT = sb("gxT", [P, 2, P]), sb("hid", [P, 2, F]), sb("gel", [P, 2, F]), sb("gelT", [P, 2, F])
        z, z_stats, z_mv, z_rstd = sb("z", [P, 2, D]), sb("z_stats", [P, 2, 6]), sb("z_mv", [P, 2, 2]), sb("z_rstd", [P, 2, 2])
        z_out = sb("z_out", [P, 4, D])

        S = {name: sem(name) for name in """
            consts_in weights_in attn_in x_in0 x_in1 x_all_in ctx_all_in ffn_in ids_in pad_row_in
            bf16_ready slots_empty pads_zero knull_ready vnull_ready bv_ready wvo_ready bvo_done bvo_ready
            proj_done rope_a rope_b_done rope_done v_done qkT_ready null_taken q_ready k4_ready v_ready
            scores_done null_done max_a max_done null_sub scores_used exp_done probsT_done probsT_a probsT_b null_ready
            attn_done attn_r attn_ready wo_done wo_used y_ready y_stats y_all_ready
            eps_ready rstd_ready x1_ready sums_k sums_ready sumT_k_ready sumT_ready sqk_done sk_ready sq_ready prod_ready
            mean_done m_max m_sub m_exp m_sum m_rec w_ready wt_ready wtok_done wtok_ready wtaps wperm_ready
            circ_ready ctx_in_ready x1b_ready ctxT_done ctxT_ready mix_done y2_ready y2_stats y2_all_ready
            eps2_ready rstd2_ready x2_ready rows_ready x2T_done x2T_ready logits_done
            lg_ready lmax_ready ld_ready lex_ready lsum_ready gate_ready eq_ready eqr_ready first_ready onehot_ready
            ranks_done slot1 slot2 slot3 slots_ready cnt_ready route scattered
            ge_ready ef_ready e_ready gathered0 gathered1 gathered2 gathered3 gxT_done gxT_ready up_done hid_ready gel_ready
            gelT_done gelT_ready down_done z_a z_b z_st z_agg z_eps z_rs z_ready row_used out_st0 out_st1 out_st2 out_st3
        """.split()}

        x_in = [S["x_in0"], S["x_in1"]]

        def count_first(eng, *values):
            values = [v if isinstance(v, int) else eng.to_reg(v) for v in values]
            eng.wait_ge(S["consts_in"], 16)
            return values if len(values) > 1 else values[0]
        gathered = [S[f"gathered{r}"] for r in range(4)]
        stored = [S[f"out_st{r}"] for r in range(4)]

        def scores_ps(r):
            return ps[:, 2 * r:2 * r + 2, :].rearrange("p a b -> p (a b)")

        probsT_ps = ps[:, 4:6, :].rearrange("p a b -> p (a b)")
        attn_ps, den_ps, wo_ps = ps[:, 6, 0:128], ps[:, 6, 128:256], ps[:, 6, 256:384]
        nullT_ps = ps[0:16, 6, 256:384]

        proj_ps, qkT_ps, v_ps, null_ps = ps[:, 7, 0:384], ps[:, 7, 0:256], ps[:, 7, 256:512], ps[:, 7, 0:H]

        block = ctx.enter_context(nc.Block())

        @block.sync
        def _(sp):
            sp.dma_start(wqk[:, :], a["wqk"]).then_inc(S["attn_in"], 16)
            sp.dma_start(consts[:, :], a["consts"]).then_inc(S["consts_in"], 16)

            def load_x(t):
                if t.i is not None or t.c >= 2:
                    sp.wait_ge(S["v_done"], t.n - 1)
                sp.dma_start(xT[:, t.ring(2), :], a["xT"][:, bass.ds(t.n * P, P)]).then_inc(x_in[t.ring(2)], 16)

            load_x(Tile(0))
            load_x(Tile(1))
            sp.dma_start(wv[:, :], a["wv"]).then_inc(S["attn_in"], 16)
            sp.dma_start(cols[:, :], a["cols"]).then_inc(S["attn_in"], 16)
            sp.dma_start(vnull_bc[:, :], a["v_null"].partition_broadcast(16)).then_inc(S["attn_in"], 16)
            sp.dma_start(wo[:, :], a["wo"]).then_inc(S["attn_in"], 16)
            sp.dma_start(x_all[:, :, :], a["x"].rearrange("(t p) d -> p t d", p=P)).then_inc(S["x_all_in"], 16)
            with sp.Fori(0, NT // 2 - 1) as i:
                load_x(Tile(2, i, 2))
                load_x(Tile(3, i, 2))

            def load_rows(t, static):
                r = t.ring(4)
                if not static or t.c >= 4:
                    sp.wait_ge(S["row_used"], t.n - 3)
                    sp.wait_ge(stored[r], t.turn(4) * 16)
                sp.dma_start(g_rows[:, r, :], rows_dram[bass.ds(t.n * P, P), :]).then_inc(gathered[r], 16)

            sp.wait_ge(S["scattered"], 16 * NT)
            for n in range(4):
                load_rows(Tile(n), True)
            n0 = (SLOTS - 4) // 4
            with sp.Fori(0, n0) as i:
                for c in range(4, 8):
                    load_rows(Tile(c, i, 4), False)
            for n in range(4 + 4 * n0, SLOTS):
                load_rows(Tile(n), True)

        @block.gpsimd
        def _(pool):
            nc.gpsimd.memset(v_pad[:, :, :], 0.0).then_inc(S["pads_zero"], 1)
            pool.dma_start(ctx_all[:, :, :], a["ctx"].rearrange("(t p) d -> p t d", p=P)).then_inc(S["ctx_all_in"], 16)
            pool.dma_start(xattn_w[:, :, :], a["xattn_w"]).then_inc(S["weights_in"], 16)
            pool.dma_start(bo_bc[:, :], a["bo"].partition_broadcast(P)).then_inc(S["weights_in"], 16)
            pool.dma_start(wr[:, :], a["wr"]).then_inc(S["weights_in"], 16)
            pool.dma_start(br_bc[:, :], a["br"].partition_broadcast(P)).then_inc(S["weights_in"], 16)
            pool.dma_start(token_ids[:, :], a["token_ids"]).then_inc(S["ids_in"], 16)
            pool.dma_start(pad_row[:, :], a["pad_row"].partition_broadcast(P)).then_inc(S["pad_row_in"], 16)
            pool.wait_ge(S["pad_row_in"], 16)
            pool.dma_start(rows_dram.rearrange("(j p) r -> p j r", p=P),
                           pad_row[:, :].unsqueeze(1).to_broadcast([P, SLOTS, ROW])).then_inc(S["slots_empty"], 16)
            pool.dma_start(w1[:, :], a["w1"]).then_inc(S["ffn_in"], 16)
            pool.dma_start(w2[:, :], a["w2"]).then_inc(S["ffn_in"], 16)
            pool.dma_start(b1_bc[:, :], a["b1"].partition_broadcast(P)).then_inc(S["ffn_in"], 16)
            pool.dma_start(b2_bc[:, :], a["b2"].partition_broadcast(P)).then_inc(S["ffn_in"], 16)
            pool.wait_ge(S["ids_in"], 16)
            nc.gpsimd.tensor_copy(rows[:, :, D + 1:D + 2].bitcast(I32).squeeze(2), token_ids[:, :])

            def q_blocks(t):
                turn = count_first(pool, t.n + 1)
                pool.wait_ge(S["qkT_ready"], turn)
                r = t.ring(2)
                nc.gpsimd.tensor_tensor(q_strips[:, r, :, :], qkT[:, r, 0:P].unsqueeze(1).to_broadcast([P, STRIPS, P]),
                                        const("strip").unsqueeze(2).to_broadcast([P, STRIPS, P]), ALU.mult).then_inc(S["q_ready"], 1)
                src = qkT[:, r, P:2 * P].rearrange("p (b k) -> p b k", b=BPT).unsqueeze(2).to_broadcast([P, BPT, HPS, T])
                m = const("strip_head").unsqueeze(1).unsqueeze(3).to_broadcast([P, BPT, HPS, T])
                nc.gpsimd.tensor_tensor(k4[:, r, :, :, :], src, m, ALU.mult).then_inc(S["k4_ready"], 1)

            pool.wait_ge(S["pads_zero"], 1)
            run_steps(pool, lambda t, _: q_blocks(t), NT, 2, 0)

            def inverse_std(k, ready, done):
                pool.wait_ge(S[ready], 1)
                nc.gpsimd.tensor_tensor(rstd[:, k, :], var_eps[:, k, :], const("minus_half"), ALU.pow).then_inc(S[done], 1)

            inverse_std(0, "eps_ready", "rstd_ready")

            pool.wait_ge(S["ctx_all_in"], 16)
            pool.wait_ge(S["x1_ready"], NT)
            pool.wait_ge(S["bvo_ready"], 1)

            def mix_inputs(t, _):
                r = t.ring(2)
                if t.i is not None and t.c >= 2 or t.i is None and t.c >= 2:
                    turn = count_first(pool, t.n - 1)
                    pool.wait_ge(S["y2_ready"], turn)
                nc.gpsimd.tensor_copy(ctx_in[:, r, :], ctx_all[:, bass.ds(t.n, 1), :].squeeze(1)).then_inc(S["ctx_in_ready"], 1)
                nc.gpsimd.tensor_tensor(x1b[:, r, :], y_all[:, bass.ds(t.n, 1), :].squeeze(1), bvo[:, :], ALU.add).then_inc(S["x1b_ready"], 1)

            mix_inputs(Tile(0), True)
            mix_inputs(Tile(1), True)
            with pool.Fori(0, NT // 2 - 1) as i:
                mix_inputs(Tile(2, i, 2), False)
                mix_inputs(Tile(3, i, 2), False)

            inverse_std(1, "eps2_ready", "rstd2_ready")

            def keep_rows(t, _):
                turn = count_first(pool, t.n + 1)
                pool.wait_ge(S["x2_ready"], turn)
                nc.gpsimd.tensor_copy(rows[:, bass.ds(t.n, 1), 0:D].squeeze(1), x2_in[:, t.ring(2), :]).then_inc(S["rows_ready"], 1)

            run_steps(pool, keep_rows, NT, 2, 0)

            pool.wait_ge(S["slots_ready"], 1)
            pool.wait_ge(S["gate_ready"], 1)
            pool.wait_ge(S["rows_ready"], NT)
            pool.wait_ge(S["slots_empty"], 16)
            for t in range(NT):
                pool.indirect_dma_start(out=rows_dram, out_offset=bass.IndirectOffsetOnAxis(ap=slots[:, t:t + 1], axis=0),
                                        in_=rows[:, t, :], in_offset=None, bounds_check=SLOTS * P - 1,
                                        oob_is_err=False).then_inc(S["scattered"], 16)
            def finish_tile(t, static):
                r, q = t.ring(2), t.ring(4)
                pool.wait_ge(S["z_eps"], t.n + 1)
                nc.gpsimd.tensor_tensor(z_rstd[:, r, 1:2], z_rstd[:, r, 0:1], const("minus_half")[:, 0:1], ALU.pow).then_inc(S["z_rs"], 1)
                turn = count_first(pool, t.n + 1)
                pool.wait_ge(S["z_ready"], turn)
                pool.indirect_dma_start(out=out, out_offset=bass.IndirectOffsetOnAxis(ap=g_rows[:, q, D + 1:D + 2].bitcast(U32), axis=0),
                                        in_=z_out[:, q, :], in_offset=None, bounds_check=NT * P - 1,
                                        oob_is_err=False).then_inc(stored[q], 16)

            run_steps(pool, lambda t, _: finish_tile(t, _), SLOTS, 4, 0)
            for r in range(4):
                pool.wait_ge(stored[r], 16 * ((SLOTS - 1 - r) // 4 + 1))

        @block.tensor
        def _(pe):
            def project(t):
                pe.wait_ge(x_in[t.ring(2)], (t.turn(2) + 1) * 16)
                if t.i is not None or t.c >= 1:
                    pe.wait_ge(S["null_taken"], t.n)
                nc.tensor.matmul(proj_ps, xT[:, t.ring(2), :], wqk[:, :], start=True, stop=True).then_inc(S["proj_done"], 1)

            def turn_qk(t):
                r = t.ring(2)
                pe.wait_ge(S["rope_done"], t.n + 1)
                nc.tensor.transpose(qkT_ps[:, 0:128], roped[:, r, 0:128], ident)
                nc.tensor.transpose(qkT_ps[:, 128:256], roped[:, r, 128:256], ident)
                for b in range(BPT):
                    for half in range(2):
                        last = nc.tensor.matmul(v_ps[64 * half:64 * half + 64, b * P:(b + 1) * P], xT[:, r, b * T:(b + 1) * T],
                                                wv[:, :], start=True, stop=True)
                last.then_inc(S["v_done"], 1)

            def scores(t):
                r = t.ring(2)
                pe.wait_ge(S["q_ready"], t.n + 1)
                pe.wait_ge(S["k4_ready"], t.n + 1)
                if t.i is not None or t.c >= 2:
                    pe.wait_ge(S["scores_used"], t.n - 1)
                pe.wait_ge(S["v_ready"], t.n + 1)
                nc.tensor.matmul(null_ps, qkT[:, r, 0:P], knull[:, :], start=True, stop=True).then_inc(S["null_done"], 1)
                sc = scores_ps(r)
                for bank in range(2):
                    nc.tensor.matmul(sc[:, 512 * bank:512 * bank + 512], ident_b, mask_b, start=True, stop=False, skip_group_check=True)
                for s in range(STRIPS):
                    for b in range(BPT):
                        last = nc.tensor.matmul(sc[b * T:(b + 1) * T, 256 * s:256 * s + 256], q_strips[:, r, s, b * T:(b + 1) * T],
                                         k4[:, r, b, :, :], start=False, stop=True, skip_group_check=True)
                last.then_inc(S["scores_done"], 1)

            def turn_probs(t):
                r = t.ring(2)
                pe.wait_ge(S["exp_done"], t.n + 1)
                if t.i is not None or t.c >= 1:
                    pe.wait_ge(S["wo_used"], t.n)
                    pe.wait_ge(S["probsT_a"], t.n)
                    pe.wait_ge(S["probsT_b"], t.n)
                for c in range(8):
                    nc.tensor.transpose(probsT_ps[:, c * P:(c + 1) * P], probs[:, r, c * P:(c + 1) * P], ident)
                nc.tensor.transpose(nullT_ps, probs[:, r, H * T:H * T + H], ident).then_inc(S["probsT_done"], 1)

            def mix_values(t):
                r = t.ring(2)
                pe.wait_ge(S["null_ready"], t.n + 1)
                pe.wait_ge(S["probsT_a"], t.n + 1)
                pe.wait_ge(S["probsT_b"], t.n + 1)
                pe.wait_ge(S["v_ready"], t.n + 1)
                nc.tensor.matmul(attn_ps, vnull[:, :], nullT[:, r, :], start=True, stop=False, skip_group_check=True)
                for ab in range(2):
                    for b in range(BPT):
                        for s in range(STRIPS):
                            at = 2 * VW * b + P * ab + 32 * s
                            nc.tensor.matmul(attn_ps[32 * s:32 * s + 32, b * T:(b + 1) * T], v_pad[:, r, at:at + 32],
                                             probsT[:, r, 4 * ab + s, b * T:(b + 1) * T], start=False, stop=(ab == 1),
                                             skip_group_check=True)
                nc.tensor.matmul(den_ps, const("row_head", 16), nullT[:, r, :], start=True, stop=False, skip_group_check=True)
                for ab in range(2):
                    for s in range(STRIPS):
                        last = nc.tensor.matmul(den_ps[32 * s:32 * s + 32, :], const("den_ones")[:, 32 * ab:32 * ab + 32],
                                                probsT[:, r, 4 * ab + s, :], start=False, stop=(ab == 1), skip_group_check=True)
                last.then_inc(S["attn_done"], 1)

            def project_out(t):
                pe.wait_ge(S["attn_ready"], t.n + 1)
                nc.tensor.matmul(wo_ps, attnT[:, t.ring(2), :], wo[:, :], start=True, stop=True).then_inc(S["wo_done"], 1)

            pe.wait_ge(S["attn_in"], 16 * 5)
            pe.wait_ge(S["consts_in"], 16)
            project(Tile(0))
            turn_qk(Tile(0))
            pe.wait_ge(S["bf16_ready"], 1)
            pe.wait_ge(S["knull_ready"], 1)
            pe.wait_ge(S["vnull_ready"], 1)
            scores(Tile(0))
            project(Tile(1))
            turn_qk(Tile(1))

            def attn_step(t, static):
                if not static or t.c + 1 < NT:
                    scores(t + 1)
                turn_probs(t)
                if not static or t.c + 2 < NT:
                    project(t + 2)
                mix_values(t)
                if not static or t.c + 2 < NT:
                    turn_qk(t + 2)
                project_out(t)

            run_steps(pe, attn_step, NT, 2, 2)

            sums_ps = ps[:, 0, 0:2 * B]
            pe.wait_ge(S["ctx_all_in"], 16)
            pe.wait_ge(S["weights_in"], 64)
            for t in range(NT):
                last = nc.tensor.matmul(sums_ps[:, BPT * t:BPT * (t + 1)], ctx_all[:, t, :], const("batch_ind"), start=True, stop=True)
            last.then_inc(S["sums_k"], 1)
            nc.tensor.matmul(ps[:, 1, 0:128], xattn_w[:, 2, :], xattn_w[:, 3, :], start=True, stop=True)
            pe.wait_ge(S["bv_ready"], 1)
            nc.tensor.matmul(ps[:, 1, 128:256], bv_bc[:, :], xattn_w[:, 3, :], start=True, stop=True).then_inc(S["bvo_done"], 1)
            pe.wait_ge(S["x1_ready"], NT)
            for t in range(NT):
                last = nc.tensor.matmul(sums_ps[:, B + BPT * t:B + BPT * (t + 1)], y_all[:, t, :], const("batch_ind"), start=True, stop=True)
            last.then_inc(S["sums_ready"], 1)
            pe.wait_ge(S["sumT_ready"], 1)
            nc.tensor.matmul(ps[:, 2, 0:B], xattn_w[:, 1, :], sumT[:, 0, :], start=True, stop=True)
            nc.tensor.matmul(ps[:, 2, B:2 * B], xattn_w[:, 0, :], sumT[:, 1, :], start=True, stop=True).then_inc(S["sqk_done"], 1)
            pe.wait_ge(S["prod_ready"], 1)
            nc.tensor.matmul(ps[0:B, 3, 0:8], sqk[:, 2, :], const("chan8"), start=True, stop=True).then_inc(S["mean_done"], 1)
            pe.wait_ge(S["wt_ready"], 1)
            nc.tensor.matmul(ps[:, 3, 128:256], const("batch_rows", B), w_tiles[:, :], start=True, stop=True).then_inc(S["wtok_done"], 1)

            def ctx_ps(r):
                return ps[:, 4 + r, 0:128]

            def mix_ps(r):
                return ps[:, 6 + r, 0:128]

            def aggregate(t):
                r = t.ring(2)
                pe.wait_ge(S["ctx_in_ready"], t.n + 1)
                pe.wait_ge(S["circ_ready"], t.n + 1)
                if t.i is not None or t.c >= 2:
                    pe.wait_ge(S["ctxT_ready"], t.n - 1)
                nc.tensor.matmul(ctx_ps(r), ctx_in[:, r, :], circ[:, r, :], start=True, stop=True).then_inc(S["ctxT_done"], 1)

            pe.wait_ge(S["wvo_ready"], 1)

            def mix_step(t, static):
                if not static or t.c + 1 < NT:
                    aggregate(t + 1)
                r = t.ring(2)
                pe.wait_ge(S["ctxT_ready"], t.n + 1)
                nc.tensor.matmul(mix_ps(r), ctxT[:, r, :], wvo[:, :], start=True, stop=True).then_inc(S["mix_done"], 1)

            def mix_step_w(t, static):
                if not static or t.c >= 2:
                    pe.wait_ge(S["y2_ready"], t.n - 1)
                mix_step(t, static)

            aggregate(Tile(0))
            mix_step_w(Tile(0), True)
            mix_step_w(Tile(1), True)
            with pe.Fori(0, NT // 2 - 2) as i:
                mix_step_w(Tile(2, i, 2), False)
                mix_step_w(Tile(3, i, 2), False)
            mix_step_w(Tile(NT - 2), True)
            mix_step_w(Tile(NT - 1), True)

            lg_ps = ps[:, 0, 0:NT * E]

            def x2T_ps(r):
                return ps[:, 4 + r, 0:128]

            def turn_x2(t):
                r = t.ring(2)
                pe.wait_ge(S["x2_ready"], t.n + 1)
                nc.tensor.transpose(x2T_ps(r), x2_in[:, r, :], ident).then_inc(S["x2T_done"], 1)

            def router_step(t, static):
                if not static or t.c + 1 < NT:
                    turn_x2(t + 1)
                pe.wait_ge(S["x2T_ready"], t.n + 1)
                nc.tensor.matmul(lg_ps[:, bass.ds(t.n * E, E)], x2T[:, t.ring(2), :], wr[:, :], start=True, stop=True).then_inc(S["logits_done"], 1)

            turn_x2(Tile(0))
            run_steps(pe, router_step, NT, 2, 2)

            pe.wait_ge(S["onehot_ready"], 1)
            oh = onehot[:, :, :].rearrange("p t e -> p (t e)")
            nc.tensor.matmul(ps[:, 1, 0:128], tri_b, oh, start=True, stop=False, skip_group_check=True)
            for s in range(1, NT):
                nc.tensor.matmul(ps[:, 1, E * s:128], ones_b, oh[:, 0:128 - E * s], start=False, stop=(s == NT - 1), skip_group_check=True)
            for t in range(NT):
                last = nc.tensor.matmul(ps[:, 2, 0:E], ones_b, oh[:, E * t:E * (t + 1)], start=(t == 0), stop=(t == NT - 1))
            last.then_inc(S["ranks_done"], 1)

            def gxT_ps(r):
                return ps[:, 4 + r, 0:P]

            def y_ps(r):
                return ps[:, 6 + r, 0:D]

            def turn_rows(t):
                pe.wait_ge(gathered[t.ring(4)], (t.turn(4) + 1) * 16)
                nc.tensor.transpose(gxT_ps(t.ring(2)), g_rows[:, t.ring(4), 0:D], ident).then_inc(S["gxT_done"], 1)

            def up(t):
                r = t.ring(2)
                e = pe.value_load(e_i[0:1, bass.ds(t.n, 1)], min_val=0, max_val=E - 1)
                pe.wait_ge(S["gxT_ready"], t.n + 1)
                if t.i is not None or t.c >= 2:
                    pe.wait_ge(S["hid_ready"], t.n - 1)
                nc.tensor.matmul(ps[:, r, :], gxT[:, r, :], w1[:, bass.ds(e * F, F)], start=True, stop=True).then_inc(S["up_done"], 1)

            def turn_hidden(t):
                r = t.ring(2)
                pe.wait_ge(S["gel_ready"], t.n + 1)
                for c in range(FC):
                    last = nc.tensor.transpose(ps[:, 2 + r, c * P:(c + 1) * P], gel[:, r, c * P:(c + 1) * P], ident)
                last.then_inc(S["gelT_done"], 1)

            def down(t, static):
                r = t.ring(2)
                e = pe.value_load(e_i[0:1, bass.ds(t.n, 1)], min_val=0, max_val=E - 1)
                pe.wait_ge(S["gelT_ready"], t.n + 1)
                if not static or t.c >= 2:
                    pe.wait_ge(S["z_a"], t.n - 1)
                for c in range(FC):
                    last = nc.tensor.matmul(y_ps(r), gelT[:, r, c * P:(c + 1) * P], w2[:, bass.ds(e * (FC * D) + c * D, D)],
                                            start=(c == 0), stop=(c == FC - 1))
                last.then_inc(S["down_done"], 1)

            pe.wait_ge(S["e_ready"], 1)
            pe.wait_ge(S["ffn_in"], 64)
            turn_rows(Tile(0))
            turn_rows(Tile(1))
            up(Tile(0))
            up(Tile(1))

            def expert_step(t, static):
                turn_hidden(t)
                if not static or t.c + 2 < SLOTS:
                    turn_rows(t + 2)
                    up(t + 2)
                down(t, static)

            expert_step(Tile(0), True)
            expert_step(Tile(1), True)
            n0 = (SLOTS - 4) // 4
            with pe.Fori(0, n0) as i:
                for c in range(2, 6):
                    expert_step(Tile(c, i, 4), False)
            for n in range(2 + 4 * n0, SLOTS):
                expert_step(Tile(n), True)

        @block.scalar
        def _(act):
            def copy(o, i):
                return nc.scalar.activation(o, i, ACT.Copy)

            def take_probsT(t):
                act.wait_ge(S["probsT_done"], t.n + 1)
                copy(probsT[:, t.ring(2), 0:4, :].rearrange("p a b -> p (a b)"), probsT_ps[:, 0:512]).then_inc(S["probsT_a"], 1)

            def take_qv(t):
                r = t.ring(2)
                act.wait_ge(S["v_done"], t.n + 1)
                copy(qkT[:, r, :], qkT_ps).then_inc(S["qkT_ready"], 1)
                for half in range(2):
                    rows_h = slice(64 * half, 64 * half + 64)
                    dst = v_pad[rows_h, r, :].rearrange("p (g w) -> p g w", w=VW)[:, :, 0:P].rearrange("p g (s c) -> p g s c", c=32)
                    src = v_ps[rows_h, :].rearrange("p (g s c) -> p g s c", g=4, s=4)
                    last = copy(dst[:, :, :, 8 * half:8 * half + 8], src[:, :, :, 8 * half:8 * half + 8])
                last.then_inc(S["v_ready"], 1)

            def exponent(t):
                act.wait_ge(S["null_sub"], t.n + 1)
                act.wait_ge(S["scores_used"], t.n + 1)
                nc.scalar.activation(probs[:, t.ring(2), :], probs[:, t.ring(2), :], ACT.Exp, scale=SCALE).then_inc(S["exp_done"], 1)

            act.wait_ge(S["pads_zero"], 1)
            take_qv(Tile(0))
            take_qv(Tile(1))
            exponent(Tile(0))

            def attn_step(t, static):
                take_probsT(t)
                if not static or t.c + 1 < NT:
                    exponent(t + 1)
                if not static or t.c + 2 < NT:
                    take_qv(t + 2)

            run_steps(act, attn_step, NT, 2, 2)
            act.wait_ge(S["m_sub"], 1)
            nc.scalar.activation(wsm[:, 1, :], wsm[:, 0, :], ACT.Exp).then_inc(S["m_exp"], 1)

            def take_ctx(t, _):
                act.wait_ge(S["ctxT_done"], t.n + 1)
                copy(ctxT[:, t.ring(2), :], ps[:, 4 + t.ring(2), 0:128]).then_inc(S["ctxT_ready"], 1)

            run_steps(act, take_ctx, NT, 2, 0)

            def take_x2(t, _):
                act.wait_ge(S["x2T_done"], t.n + 1)
                copy(x2T[:, t.ring(2), :], ps[:, 4 + t.ring(2), 0:128]).then_inc(S["x2T_ready"], 1)

            run_steps(act, take_x2, NT, 2, 0)
            act.wait_ge(S["ld_ready"], 1)
            nc.scalar.activation(lex[:, :, :], lg[:, :, :], ACT.Exp).then_inc(S["lex_ready"], 1)

            def take_rows(t):
                act.wait_ge(S["gxT_done"], t.n + 1)
                copy(gxT[:, t.ring(2), :], ps[:, 4 + t.ring(2), 0:P]).then_inc(S["gxT_ready"], 1)

            def gelu(t):
                r = t.ring(2)
                act.wait_ge(S["hid_ready"], t.n + 1)
                nc.scalar.activation(gel[:, r, :], hid[:, r, :], ACT.Gelu).then_inc(S["gel_ready"], 1)

            def take_hidden(t):
                r = t.ring(2)
                act.wait_ge(S["gelT_done"], t.n + 1)
                copy(gelT[:, r, :], ps[:, 2 + r, :]).then_inc(S["gelT_ready"], 1)

            take_rows(Tile(0))
            take_rows(Tile(1))
            gelu(Tile(0))

            def expert_step(t, static):
                take_hidden(t)
                if not static or t.c + 2 < SLOTS:
                    take_rows(t + 2)
                if not static or t.c + 1 < SLOTS:
                    gelu(t + 1)

            run_steps(act, expert_step, SLOTS, 4, 2)

        @block.vector
        def _(dve):
            v = nc.vector
            route_step = [0]

            def chained(ins, name="route"):
                route_step[0] += 1
                ins.then_inc(S["route"], 1)
                dve.wait_ge(S["route"], route_step[0])

            def rope(t):
                r = t.ring(2)
                dve.wait_ge(S["proj_done"], t.n + 1)
                main = proj_ps[:, 0:256].rearrange("p (h c) -> p h c", c=HD)
                swapped = proj_ps[:, 256:384].rearrange("p (h c) -> p h c", c=4)
                ra = roped[:, r, :].rearrange("p (h c) -> p h c", c=HD)
                rb = rope_b[:, r, :].rearrange("p (h c) -> p h c", c=4)
                v.tensor_tensor(ra, main, const("cos8").unsqueeze(1).to_broadcast([P, 2 * H, HD]), ALU.mult).then_inc(S["rope_a"], 1)
                v.tensor_tensor(rb, swapped, const("sin4").unsqueeze(1).to_broadcast([P, 2 * H, 4]), ALU.mult).then_inc(S["rope_b_done"], 1)
                dve.wait_ge(S["rope_a"], t.n + 1)
                dve.wait_ge(S["rope_b_done"], t.n + 1)
                v.tensor_tensor(ra[:, :, 0:4], ra[:, :, 0:4], rb, ALU.add).then_inc(S["rope_done"], 1)

            def maximum(t):
                r = t.ring(2)
                dve.wait_ge(S["null_done"], t.n + 1)
                v.tensor_copy(null_s[:, r, :], null_ps).then_inc(S["null_taken"], 1)
                dve.wait_ge(S["scores_done"], t.n + 1)
                v.tensor_reduce(row_max[:, r, :], scores_ps(r).rearrange("p (h k) -> p h k", k=T), AX.X, ALU.max).then_inc(S["max_a"], 1)
                dve.wait_ge(S["max_a"], t.n + 1)
                dve.wait_ge(S["null_taken"], t.n + 1)
                v.tensor_tensor(row_max2[:, r, :], row_max[:, r, :], null_s[:, r, :], ALU.max).then_inc(S["max_done"], 1)

            def subtract(t):
                r = t.ring(2)
                dve.wait_ge(S["max_done"], t.n + 1)
                v.tensor_tensor(probs[:, r, H * T:H * T + H], null_s[:, r, :], row_max2[:, r, :], ALU.subtract).then_inc(S["null_sub"], 1)
                v.tensor_tensor(probs[:, r, 0:H * T].rearrange("p (h k) -> p h k", k=T), scores_ps(r).rearrange("p (h k) -> p h k", k=T),
                                row_max2[:, r, :].unsqueeze(2).to_broadcast([P, H, T]), ALU.subtract).then_inc(S["scores_used"], 1)

            def take_probsT(t):
                r = t.ring(2)
                dve.wait_ge(S["probsT_done"], t.n + 1)
                v.tensor_copy(nullT[:, r, :], nullT_ps).then_inc(S["null_ready"], 1)
                v.tensor_copy(probsT[:, r, 4:8, :].rearrange("p a b -> p (a b)"), probsT_ps[:, 512:1024]).then_inc(S["probsT_b"], 1)

            def normalize(t):
                r = t.ring(2)
                dve.wait_ge(S["attn_done"], t.n + 1)
                v.reciprocal(rden[:, r, :], den_ps).then_inc(S["attn_r"], 1)
                dve.wait_ge(S["attn_r"], t.n + 1)
                v.tensor_tensor(attnT[:, r, :], attn_ps, rden[:, r, :], ALU.mult).then_inc(S["attn_ready"], 1)

            def residual(t):
                r = t.ring(2)
                y = y_all[:, bass.ds(t.n, 1), :].squeeze(1)
                dve.wait_ge(S["wo_done"], t.n + 1)
                v.tensor_tensor(y, wo_ps, x_all[:, bass.ds(t.n, 1), :].squeeze(1), ALU.add).then_inc(S["wo_used"], 1)
                turn = count_first(dve, t.n + 1)
                dve.wait_ge(S["wo_used"], turn)
                v.bn_stats(stats[:, bass.ds(t.n, 1), :].squeeze(1), y).then_inc(S["y_all_ready"], 1)

            dve.wait_ge(S["consts_in"], 16)
            dve.wait_ge(S["attn_in"], 80)
            v.tensor_copy(ident_b, ident)
            v.tensor_copy(mask_b.rearrange("p (h k) -> p h k", k=T), const("causal").unsqueeze(1).to_broadcast([P, 8, T]))
            v.tensor_copy(tri_b, const("earlier"))
            v.memset(ones_b, 1.0).then_inc(S["bf16_ready"], 1)
            v.tensor_scalar(knull[:, :], const("head16"), cols[:, 0:1], None, ALU.mult).then_inc(S["knull_ready"], 1)
            v.tensor_tensor(vnull[:, :], const("row_head", 16), vnull_bc[:, :], ALU.mult).then_inc(S["vnull_ready"], 1)
            v.tensor_scalar(bv_bc[:, :], ident, 0.0, cols[:, 3:4], ALU.mult, ALU.add).then_inc(S["bv_ready"], 1)
            rope(Tile(0))
            maximum(Tile(0))
            rope(Tile(1))
            subtract(Tile(0))
            dve.wait_ge(S["x_all_in"], 16)

            def attn_step(t, static):
                if not static or t.c + 1 < NT:
                    maximum(t + 1)
                take_probsT(t)
                if not static or t.c + 1 < NT:
                    subtract(t + 1)
                if not static or t.c + 2 < NT:
                    rope(t + 2)
                normalize(t)
                residual(t)

            run_steps(dve, attn_step, NT, 2, 2)

            def mean_and_variance(k, st, mean, done):
                even, m2e, odd, m2o = (st[:, :, j:j + 1].squeeze(2) for j in (1, 2, 4, 5))
                chained(v.tensor_tensor(mean_gap[:, :], even, odd, ALU.subtract))
                chained(v.tensor_tensor(mean[:, :], even, odd, ALU.add))
                chained(v.tensor_scalar(mean[:, :], mean[:, :], 0.5, None, ALU.mult))
                chained(v.tensor_tensor(var_eps[:, k, :], m2e, m2o, ALU.add))
                chained(v.tensor_tensor(mean_gap[:, :], mean_gap[:, :], mean_gap[:, :], ALU.mult))
                chained(v.tensor_scalar(var_eps[:, k, :], var_eps[:, k, :], 1.0 / D, EPS, ALU.mult, ALU.add))
                v.scalar_tensor_tensor(var_eps[:, k, :], mean_gap[:, :], 0.25, var_eps[:, k, :], ALU.mult, ALU.add).then_inc(S[done], 1)

            def normed(k, mean_var, source, target, ready, done):
                dve.wait_ge(S[ready], 1)

                def one(t, _):
                    target_ap = target(t)
                    v.tensor_scalar(target_ap, source[:, bass.ds(t.n, 1), :].squeeze(1), mean_var[:, bass.ds(t.n, 1)],
                                    rstd[:, k, bass.ds(t.n, 1)], ALU.subtract, ALU.mult).then_inc(S[done], 1)
                return one

            dve.wait_ge(S["y_all_ready"], NT)
            mean_and_variance(0, stats, mv, "eps_ready")
            dve.wait_ge(S["bvo_done"], 1)
            dve.wait_ge(S["weights_in"], 64)
            v.tensor_copy(wvo[:, :], ps[:, 1, 0:128]).then_inc(S["wvo_ready"], 1)
            v.tensor_tensor(bvo[:, :], ps[:, 1, 128:256], bo_bc[:, :], ALU.add).then_inc(S["bvo_ready"], 1)
            one = normed(0, mv, y_all, lambda t: y_all[:, bass.ds(t.n, 1), :].squeeze(1), "rstd_ready", "x1_ready")
            run_steps(dve, one, NT, 2, 0)

            dve.wait_ge(S["sums_ready"], 1)
            v.tensor_copy(sumT[:, :, :].rearrange("p a b -> p (a b)"), ps[:, 0, 0:2 * B]).then_inc(S["sumT_ready"], 1)
            v.tensor_scalar(cols[:, 1:3], cols[:, 1:3], float(T), None, ALU.mult).then_inc(S["sk_ready"], 1)
            dve.wait_ge(S["sqk_done"], 1)
            dve.wait_ge(S["sk_ready"], 1)
            v.tensor_scalar(sqk[:, 0, :], ps[:, 2, 0:B], cols[:, 2:3], 1.0 / (H * T), ALU.add, ALU.mult).then_inc(S["sq_ready"], 1)
            dve.wait_ge(S["sq_ready"], 1)
            v.scalar_tensor_tensor(sqk[:, 2, :], ps[:, 2, B:2 * B], cols[:, 1:2], sqk[:, 0, :], ALU.add, ALU.mult).then_inc(S["prod_ready"], 1)
            dve.wait_ge(S["mean_done"], 1)
            mean = ps[0:B, 3, 0:8]
            v.tensor_reduce(wcol[:, 0:1], mean, AX.X, ALU.max).then_inc(S["m_max"], 1)
            dve.wait_ge(S["m_max"], 1)
            v.tensor_scalar(wsm[:, 0, :], mean, wcol[:, 0:1], None, ALU.subtract).then_inc(S["m_sub"], 1)
            dve.wait_ge(S["m_exp"], 1)
            v.tensor_reduce(wcol[:, 1:2], wsm[:, 1, :], AX.X, ALU.add).then_inc(S["m_sum"], 1)
            dve.wait_ge(S["m_sum"], 1)
            v.reciprocal(wcol[:, 2:3], wcol[:, 1:2]).then_inc(S["m_rec"], 1)
            dve.wait_ge(S["m_rec"], 1)
            v.tensor_scalar(wsm[:, 2, :], wsm[:, 1, :], wcol[:, 2:3], None, ALU.mult).then_inc(S["w_ready"], 1)
            dve.wait_ge(S["w_ready"], 1)
            v.tensor_tensor(w_tiles[:, :].rearrange("p (t c) -> p t c", c=8), const("batch_tile", B).rearrange("p (t c) -> p t c", c=8),
                            wsm[:, 2, :].unsqueeze(1).to_broadcast([B, NT, 8]), ALU.mult).then_inc(S["wt_ready"], 1)
            dve.wait_ge(S["wtok_done"], 1)
            v.tensor_copy(w_tok[:, :], ps[:, 3, 128:256]).then_inc(S["wtok_ready"], 1)
            dve.wait_ge(S["wtok_ready"], 1)
            taps = w_taps[:, :].rearrange("p (t r c) -> p t r c", r=8, c=8)
            v.tensor_tensor(taps, w_tok[:, :].rearrange("p (t c) -> p t c", c=8).unsqueeze(2).to_broadcast([P, NT, 8, 8]),
                            const("tap_of").rearrange("p (r c) -> p r c", c=8).unsqueeze(1).to_broadcast([P, NT, 8, 8]),
                            ALU.mult).then_inc(S["wtaps"], 1)
            dve.wait_ge(S["wtaps"], 1)
            v.tensor_reduce(w_perm[:, :].rearrange("p (t r) -> p t r", r=8), taps, AX.X, ALU.add).then_inc(S["wperm_ready"], 1)
            dve.wait_ge(S["wperm_ready"], 1)

            def circulant(t):
                r = t.ring(2)
                if t.i is not None or t.c >= 2:
                    dve.wait_ge(S["ctxT_done"], t.n - 1)
                v.tensor_tensor(circ[:, r, :].rearrange("p (a r) -> p a r", r=8), const("band").rearrange("p (a r) -> p a r", r=8),
                                w_perm[:, bass.ds(t.n * 8, 8)].unsqueeze(1).to_broadcast([P, 16, 8]), ALU.mult).then_inc(S["circ_ready"], 1)

            def mix_step(t, static):
                r = t.ring(2)
                if not static or t.c + 2 < NT:
                    circulant(t + 2)
                y2 = y2_all[:, bass.ds(t.n, 1), :].squeeze(1)
                dve.wait_ge(S["mix_done"], t.n + 1)
                dve.wait_ge(S["x1b_ready"], t.n + 1)
                v.tensor_tensor(y2, ps[:, 6 + r, 0:128], x1b[:, r, :], ALU.add).then_inc(S["y2_ready"], 1)
                turn = count_first(dve, t.n + 1)
                dve.wait_ge(S["y2_ready"], turn)
                v.bn_stats(stats2[:, bass.ds(t.n, 1), :].squeeze(1), y2).then_inc(S["y2_all_ready"], 1)

            circulant(Tile(0))
            circulant(Tile(1))
            run_steps(dve, mix_step, NT, 2, 2)

            dve.wait_ge(S["y2_all_ready"], NT)
            mean_and_variance(1, stats2, mv2, "eps2_ready")
            one2 = normed(1, mv2, y2_all, lambda t: x2_in[:, t.ring(2), :], "rstd2_ready", "x2_ready")

            def norm2(t, static):
                if t.i is not None or t.c >= 2:
                    dve.wait_ge(S["x2T_done"], t.n - 1)
                    dve.wait_ge(S["rows_ready"], t.n - 1)
                one2(t, static)

            norm2(Tile(0), True)
            norm2(Tile(1), True)
            with dve.Fori(0, NT // 2 - 1) as i:
                norm2(Tile(2, i, 2), False)
                norm2(Tile(3, i, 2), False)

            dve.wait_ge(S["logits_done"], NT)
            per_tile = [P, NT, E]
            v.tensor_tensor(lg[:, :, :], ps[:, 0, 0:NT * E].rearrange("p (t e) -> p t e", e=E),
                            br_bc[:, :].unsqueeze(1).to_broadcast(per_tile), ALU.add).then_inc(S["lg_ready"], 1)
            dve.wait_ge(S["lg_ready"], 1)
            v.tensor_reduce(lmax[:, :], lg[:, :, :], AX.X, ALU.max).then_inc(S["lmax_ready"], 1)
            dve.wait_ge(S["lmax_ready"], 1)
            v.tensor_tensor(lg[:, :, :], lg[:, :, :], lmax[:, :].unsqueeze(2).to_broadcast(per_tile), ALU.subtract).then_inc(S["ld_ready"], 1)
            dve.wait_ge(S["ld_ready"], 1)
            v.tensor_scalar(eqr[:, :, :], lg[:, :, :], 0.0, None, ALU.is_equal).then_inc(S["eq_ready"], 1)
            dve.wait_ge(S["eq_ready"], 1)
            v.tensor_tensor(eqr[:, :, :], eqr[:, :, :], const("rev8").unsqueeze(1).to_broadcast(per_tile), ALU.mult).then_inc(S["eqr_ready"], 1)
            dve.wait_ge(S["eqr_ready"], 1)
            v.tensor_reduce(first[:, :], eqr[:, :, :], AX.X, ALU.max).then_inc(S["first_ready"], 1)
            dve.wait_ge(S["first_ready"], 1)
            v.tensor_tensor(onehot[:, :, :], eqr[:, :, :], first[:, :].unsqueeze(2).to_broadcast(per_tile), ALU.is_equal).then_inc(S["onehot_ready"], 1)
            dve.wait_ge(S["lex_ready"], 1)
            v.tensor_reduce(lsum[:, :], lex[:, :, :], AX.X, ALU.add).then_inc(S["lsum_ready"], 1)
            dve.wait_ge(S["lsum_ready"], 1)
            v.reciprocal(rows[:, :, D:D + 1].squeeze(2), lsum[:, :]).then_inc(S["gate_ready"], 1)
            dve.wait_ge(S["ranks_done"], 1)

            chained(v.tensor_copy(cnt[:, :], ps[:, 2, 0:E]))
            chained(v.tensor_tensor(over[:, :, :], cnt[:, :].unsqueeze(2).to_broadcast([P, E, 16]),
                                    const("thresholds").unsqueeze(1).to_broadcast([P, E, 16]), ALU.is_gt))
            chained(v.tensor_reduce(ntile[:, :], over[:, :, :], AX.X, ALU.add))
            chained(v.tensor_tensor(tmp64[:, :, :], const("before8").rearrange("p (a b) -> p a b", b=E),
                                    ntile[:, :].unsqueeze(1).to_broadcast([P, E, E]), ALU.mult))
            chained(v.tensor_reduce(start_t[:, :], tmp64[:, :, :], AX.X, ALU.add))
            chained(v.tensor_tensor(end_t[:, :], start_t[:, :], ntile[:, :], ALU.add))
            chained(v.tensor_scalar(start_t[:, :], start_t[:, :], float(P), None, ALU.mult))
            v.tensor_tensor(slot_f[:, :, :], ps[:, 1, 0:NT * E].rearrange("p (t e) -> p t e", e=E),
                            start_t[:, :].unsqueeze(1).to_broadcast(per_tile), ALU.add).then_inc(S["slot1"], 1)
            dve.wait_ge(S["slot1"], 1)
            v.tensor_tensor(slot_f[:, :, :], slot_f[:, :, :], onehot[:, :, :], ALU.mult).then_inc(S["slot2"], 1)
            dve.wait_ge(S["slot2"], 1)
            v.tensor_reduce(slot_a[:, :], slot_f[:, :, :], AX.X, ALU.add).then_inc(S["slot3"], 1)
            dve.wait_ge(S["slot3"], 1)
            v.tensor_copy(slots[:, :], slot_a[:, :]).then_inc(S["slots_ready"], 1)
            v.tensor_tensor(ge[:, :, :], const("slot_j").unsqueeze(2).to_broadcast([P, SLOTS, E]),
                            end_t[:, :].unsqueeze(1).to_broadcast([P, SLOTS, E]), ALU.is_ge).then_inc(S["ge_ready"], 1)
            dve.wait_ge(S["ge_ready"], 1)
            v.tensor_reduce(e_f[:, :], ge[:, :, :], AX.X, ALU.add).then_inc(S["ef_ready"], 1)
            dve.wait_ge(S["ef_ready"], 1)
            v.tensor_scalar(e_i[:, :], e_f[:, :], float(E - 1), None, ALU.min).then_inc(S["e_ready"], 1)

            def add_b1(t):
                r = t.ring(2)
                e = dve.value_load(e_i[0:1, bass.ds(t.n, 1)], min_val=0, max_val=E - 1)
                dve.wait_ge(S["up_done"], t.n + 1)
                v.tensor_tensor(hid[:, r, :], ps[:, r, :], b1_bc[:, bass.ds(e * F, F)], ALU.add).then_inc(S["hid_ready"], 1)

            def finish(t, static):
                r, q = t.ring(2), t.ring(4)
                e = dve.value_load(e_i[0:1, bass.ds(t.n, 1)], min_val=0, max_val=E - 1)
                dve.wait_ge(gathered[q], (t.turn(4) + 1) * 16)
                if not static or t.c >= 4:
                    dve.wait_ge(stored[q], t.turn(4) * 16)
                dve.wait_ge(S["down_done"], t.n + 1)
                v.tensor_tensor(z[:, r, :], ps[:, 6 + r, 0:D], b2_bc[:, bass.ds(e * D, D)], ALU.add).then_inc(S["z_a"], 1)
                dve.wait_ge(S["z_a"], t.n + 1)
                v.scalar_tensor_tensor(z[:, r, :], z[:, r, :], g_rows[:, q, D:D + 1], g_rows[:, q, 0:D], ALU.mult, ALU.add).then_inc(S["row_used"], 1)
                turn = count_first(dve, t.n + 1)
                dve.wait_ge(S["row_used"], turn)
                v.bn_stats(z_stats[:, r, :], z[:, r, :]).then_inc(S["z_st"], 1)
                turn = count_first(dve, t.n + 1)
                dve.wait_ge(S["z_st"], turn)
                v.bn_aggr(z_mv[:, r, :], z_stats[:, r, :]).then_inc(S["z_agg"], 1)
                dve.wait_ge(S["z_agg"], t.n + 1)
                v.tensor_scalar(z_rstd[:, r, 0:1], z_mv[:, r, 1:2], EPS, None, ALU.add).then_inc(S["z_eps"], 1)

            def norm_out(t):
                r, q = t.ring(2), t.ring(4)
                dve.wait_ge(S["z_rs"], t.n + 1)
                v.tensor_scalar(z_out[:, q, :], z[:, r, :], z_mv[:, r, 0:1], z_rstd[:, r, 1:2], ALU.subtract, ALU.mult).then_inc(S["z_ready"], 1)

            dve.wait_ge(S["e_ready"], 1)
            dve.wait_ge(S["ffn_in"], 64)
            add_b1(Tile(0))
            add_b1(Tile(1))

            def expert_step(t, static):
                q = t.ring(4)
                if not static or t.c + 2 < SLOTS:
                    add_b1(t + 2)
                finish(t, static)
                norm_out(t)

            for n in range(4):
                expert_step(Tile(n), True)
            n0 = (SLOTS - 4 - 2) // 4
            with dve.Fori(0, n0) as i:
                for c in range(4, 8):
                    expert_step(Tile(c, i, 4), False)
            for n in range(4 + 4 * n0, SLOTS):
                expert_step(Tile(n), True)


def shape_constants():
    c = {}
    p = np.arange(P)
    c["ident"] = np.eye(P)
    ang = (p % T).astype(np.float32)[:, None] * (1.0 / 10000.0 ** (np.arange(0, 4, 2, dtype=np.float32) / 4)).astype(np.float32)[None]
    cos, sin = np.cos(ang), np.sin(ang)
    c["cos8"] = np.concatenate([cos, cos, np.ones((P, 4))], 1)
    c["sin4"] = np.concatenate([-sin, sin], 1)
    c["strip"] = (p[:, None] // 32 == np.arange(STRIPS)[None])
    c["strip_head"] = (p[:, None] // HD % HPS == np.arange(HPS)[None])
    c["head16"] = (p[:, None] // HD == np.arange(H)[None])
    rh = value_rows() // HD
    c["row_head"] = np.arange(P)[:, None] == rh[None]
    c["den_ones"] = np.concatenate([np.arange(32)[None] // 8 == 2 * ab + p[:, None] // T for ab in range(2)], 1)
    c["chan8"] = (p[:, None] % HD == np.arange(8)[None])
    c["batch_rows"] = (p[:, None] % BPT == p[None] // T)
    c["batch_tile"] = (p[:, None] // BPT == p[None] // 8)
    c["tap_of"] = ((p[:, None, None] - np.arange(8)[None, :, None]) % 8 == np.arange(8)[None, None]).reshape(P, 64)
    c["band"] = (p[:, None] // T == p[None] // T) & ((p[:, None] - p[None]) % T < 8)
    c["batch_ind"] = (p[:, None] // T == np.arange(BPT)[None])
    c["rev8"] = np.broadcast_to(8 - np.arange(8)[None], (P, 8))
    c["thresholds"] = np.broadcast_to(P * np.arange(16)[None], (P, 16))
    c["before8"] = np.broadcast_to((np.arange(8)[None] < np.arange(8)[:, None]).reshape(1, 64), (P, 64))
    c["slot_j"] = np.broadcast_to(np.arange(SLOTS)[None], (P, SLOTS))
    c["minus_half"] = np.full((P, 16), -0.5)
    c["causal"] = np.where(np.arange(T)[None] <= (p % T)[:, None], 0.0, -1e30)
    c["earlier"] = p[:, None] < p[None]
    f32 = np.concatenate([c[n].astype(np.float32) for n, _ in CONSTS], 1)
    ids = (P * np.arange(NT)[None] + p[:, None]).astype(np.int32)
    pad = np.zeros(ROW, np.int32)
    pad[D + 1] = NO_TOKEN
    return f32, ids, pad.view(np.float32)


def value_rows():
    r = np.arange(P)
    s, ab, half, d = r // 32, r // 16 % 2, r // 8 % 2, r % 8
    return 64 * ab + 16 * s + 8 * half + d


def kernel(**inputs):
    import concourse.bacc as bacc
    from concourse.bass_utils import run_bass_kernel_spmd

    g = {k: np.asarray(v) for k, v in inputs.items()}
    x = g["x"].reshape(B * T, D)
    L = "L0_attn_"

    def headed(geo, sem):
        return np.concatenate([geo.reshape(-1, H, 4), sem.reshape(-1, H, 4)], 2).reshape(-1, P)

    def swapped(geo):
        return geo.reshape(-1, H, 2, 2)[:, :, ::-1].reshape(-1, H * 4)

    f32, ids, pad = shape_constants()
    A = "L0_xattn_"
    M = "L0_ffn_"
    knull = headed(g[L + "k_geo_null"][None], g[L + "k_sem_null"][None])[0]
    arrays = {
        "consts": f32, "token_ids": ids, "pad_row": pad,
        "x": x, "xT": x.T, "ctx": g["ctx_1024"].reshape(B * T, D),
        "wqk": np.concatenate([headed(g[L + "wq_geo"], g[L + "wq_sem"]), headed(g[L + "wk_geo"], g[L + "wk_sem"]),
                               swapped(g[L + "wq_geo"]), swapped(g[L + "wk_geo"])], 1),
        "wv": g[L + "wv"], "wo": g[L + "wo"][value_rows()], "v_null": g[L + "v_null"][value_rows()],
        "cols": np.stack([knull, g[A + "bq"], g[A + "bk"], g[A + "bv"]], 1),
        "xattn_w": np.stack([g[A + "Wq"].T, g[A + "Wk"].T, g[A + "Wv"], g[A + "Wo"].T], 1),
        "bo": g[A + "bo"], "wr": g[M + "Wr"], "br": g[M + "br"],
        "w1": g[M + "W1"].transpose(1, 0, 2).reshape(P, E * F),
        "w2": g[M + "W2"].reshape(E, FC, P, D).transpose(2, 0, 1, 3).reshape(P, E * FC * D),
        "b1": g[M + "b1"].reshape(-1), "b2": g[M + "b2"].reshape(-1),
    }
    nc = bacc.Bacc("TRN2", target_bir_lowering=False, num_devices=1)
    arrays = {k: np.ascontiguousarray(v) for k, v in arrays.items()}
    aps = {k: nc.dram_tensor("in_" + k, v.shape, mybir.dt.from_np(v.dtype), kind="ExternalInput").ap() for k, v in arrays.items()}
    out = nc.dram_tensor("out_0", (B * T, D), F32, kind="ExternalOutput").ap()
    decoder_layer(nc, aps, out)
    r = run_bass_kernel_spmd(nc, [{"in_" + k: v for k, v in arrays.items()}], core_ids=[0])
    return r.results[0]["out_0"].reshape(B, T, D)
```

```python
from contextlib import ExitStack

import numpy as np
import concourse.bass as bass
from concourse import mybir

ALU = mybir.AluOpType
ACT = mybir.ActivationFunctionType
AX = mybir.AxisListType
F32 = mybir.dt.float32
BF16 = mybir.dt.bfloat16
I32 = mybir.dt.int32
U32 = mybir.dt.uint32

P = 128
B, T, D = 32, 64, 128
H, HD = 16, 8
E, F = 8, 512
NT = B * T // P
BPT = P // T
EPS = 1e-5
STRIPS, HPS = 4, 4
FC = F // P
SLOTS = (NT * P + E * (P - 1)) // P
ROW = D + 2
NO_TOKEN = 1 << 20
SCALE = 0.5
RING = 6
VW = P + 16

CONSTS = [("ident", 128), ("cos8", 8), ("sin4", 4), ("strip", 4), ("strip_head", 4), ("head16", 16), ("row_head", 128),
          ("den_ones", 64), ("chan8", 8), ("batch_rows", 128), ("batch_tile", 128), ("tap_of", 64),
          ("band", 128), ("batch_ind", 2), ("rev8", 8), ("thresholds", 16), ("before8", 64),
          ("slot_j", SLOTS), ("minus_half", 16), ("causal", T), ("earlier", P)]
COL, _at = {}, 0
for _n, _w in CONSTS:
    COL[_n] = (_at, _at + _w)
    _at += _w
NCONST = _at


class Tile:

    def __init__(self, c, i=None, U=1):
        self.c, self.i, self.U = c, i, U
        self.n = c if i is None else i * U + c

    def __add__(self, k):
        return Tile(self.c + k, self.i, self.U)

    def ring(self, size):
        return self.c % size

    def turn(self, size):
        return self.c // size if self.i is None else self.i * (self.U // size) + self.c // size


def run_steps(eng, step, total, U, tail):
    looped = (total - tail) // U
    with eng.Fori(0, looped) as i:
        for c in range(U):
            step(Tile(c, i, U), False)
    for n in range(looped * U, total):
        step(Tile(n), True)


def decoder_layer(nc, a, out):
    with ExitStack() as ctx:
        def sb(name, shape, dt=F32):
            return ctx.enter_context(nc.sbuf_tensor(name, shape, dt))

        def sem(name):
            return ctx.enter_context(nc.semaphore(name))

        rows_dram = nc.dram_tensor("token_rows", (SLOTS * P, ROW), F32, kind="Internal").ap()
        ps = ctx.enter_context(nc.psum_tensor("ps", [P, 8, 512], F32))
        consts = sb("consts", [P, NCONST])
        cb = sb("cb", [P, 128 + 512 + 128 + 128], BF16)
        wqk, wv, wo = sb("wqk", [P, 384]), sb("wv", [P, P]), sb("wo", [P, P])
        xattn_w = sb("xattn_w", [P, 4, P])
        cols = sb("cols", [P, 4])
        vnull_bc, bo_bc = sb("vnull_bc", [16, P]), sb("bo_bc", [P, P])
        wr, br_bc = sb("wr", [P, E]), sb("br_bc", [P, E])
        w1, w2 = sb("w1", [P, E * F]), sb("w2", [P, E * FC * D])
        b1_bc, b2_bc = sb("b1_bc", [P, E * F]), sb("b2_bc", [P, E * D])
        x_all, ctx_all = sb("x_all", [P, NT, D]), sb("ctx_all", [P, NT, D])
        pad_row = sb("pad_row", [P, ROW])
        token_ids = sb("token_ids", [P, NT], I32)

        def const(name, parts=P):
            lo, hi = COL[name]
            return consts[0:parts, lo:hi]

        ident = const("ident")
        ident_b, mask_b, tri_b, ones_b = cb[:, 0:128], cb[:, 128:640], cb[:, 640:768], cb[:, 768:896]

        knull, vnull = sb("knull", [P, H]), sb("vnull", [16, P])
        bv_bc, wvo, bvo = sb("bv_bc", [P, P]), sb("wvo", [P, P]), sb("bvo", [P, P])
        xT = sb("xT", [P, 4, P])
        roped, rope_b = sb("roped", [P, 2, 256]), sb("rope_b", [P, 2, 128])
        qkT, q_strips, k4 = sb("qkT", [P, 2, 2 * P]), sb("q_strips", [P, 2, STRIPS, P]), sb("k4", [P, 2, BPT, HPS, T])
        v_pad = sb("v_pad", [P, 4, 4 * VW])
        null_s = sb("null_s", [P, 2, H])
        row_max, row_max2 = sb("row_max", [P, 2, H]), sb("row_max2", [P, 2, H])
        probs = sb("probs", [P, 2, H * T + H])
        probsT, nullT = sb("probsT", [P, 2, 8, P]), sb("nullT", [16, 2, P])
        rden, attnT = sb("rden", [P, 2, P]), sb("attnT", [P, 2, P])
        y_all, y2_all = sb("y_all", [P, NT, D]), sb("y2_all", [P, NT, D])
        stats, mv, mv2 = sb("stats", [P, NT, 6]), sb("mv", [P, NT]), sb("mv2", [P, NT])
        stats2, mean_gap = sb("stats2", [P, NT, 6]), sb("mean_gap", [P, NT])
        var_eps, rstd = sb("var_eps", [P, 2, NT]), sb("rstd", [P, 2, NT])
        sumT, sqk = sb("sumT", [P, 2, B]), sb("sqk", [P, 3, B])
        wsm = sb("wsm", [B, 4, 8])
        wcol = sb("wcol", [B, 4])
        w_tiles, w_tok = sb("w_tiles", [B, P]), sb("w_tok", [P, P])
        w_taps, w_perm = sb("w_taps", [P, NT * 64]), sb("w_perm", [P, P])
        circ, ctx_in, ctxT, x1b = sb("circ", [P, 2, P]), sb("ctx_in", [P, 2, P]), sb("ctxT", [P, 2, P]), sb("x1b", [P, 2, P])
        x2_in, x2T = sb("x2_in", [P, 2, P]), sb("x2T", [P, 2, P])
        rows = sb("rows", [P, NT, ROW])
        lg, lmax, lex = sb("lg", [P, NT, E]), sb("lmax", [P, NT]), sb("lex", [P, NT, E])
        lsum, eqr, first, onehot = sb("lsum", [P, NT]), sb("eqr", [P, NT, E]), sb("first", [P, NT]), sb("onehot", [P, NT, E], BF16)
        slot_f, slot_a, slots = sb("slot_f", [P, NT, E]), sb("slot_a", [P, NT]), sb("slots", [P, NT], U32)
        cnt, over, ntile = sb("cnt", [P, E]), sb("over", [P, E, 16]), sb("ntile", [P, E])
        tmp64, start_t, end_t = sb("tmp64", [P, E, E]), sb("start_t", [P, E]), sb("end_t", [P, E])
        ge = sb("ge", [P, SLOTS, E])
        e_f, e_i = sb("e_f", [P, SLOTS]), sb("e_i", [P, SLOTS], I32)
        g_rows = sb("g_rows", [P, RING, ROW])
        z_token = sb("z_token", [P, RING, 1], I32)
        gxT, hid, gel, gelT = sb("gxT", [P, 2, P]), sb("hid", [P, 2, F]), sb("gel", [P, 2, F]), sb("gelT", [P, 2, F])
        z, z_stats, z_mv, z_rstd = sb("z", [P, 2, D]), sb("z_stats", [P, 2, 6]), sb("z_mv", [P, 2, 2]), sb("z_rstd", [P, 2, 2])
        z_out = sb("z_out", [P, RING, D])

        S = {name: sem(name) for name in """
            consts_in weights_in attn_in x_in0 x_in1 x_in2 x_in3 x_all_in ctx_all_in ffn_in ids_in pad_row_in
            bf16_ready slots_empty pads_zero knull_ready vnull_ready bv_ready wvo_ready bvo_done bvo_ready
            proj_done rope_b_done rope_done v_done qkT_ready null_taken q_ready k4_ready v_ready
            null_done null_sub exp0 exp1 scored0 scored1 used0 used1 max_a0 max_a1 max0 max1 probsT_done probsT_ready null_ready
            attn_done attn_r attn_ready wo_done wo_used y_ready y_stats y_all_ready
            eps_ready rstd_ready x1_ready sums_k sums_ready sumT_k_ready sumT_ready sqk_done sk_ready sq_ready prod_ready
            mean_done m_max m_sub m_exp m_sum m_rec w_ready wt_ready wtok_done wtok_ready wtaps wperm_ready
            circ_ready ctx_in_ready x1b_ready ctxT_done ctxT_ready mix_done y2_ready y2_stats y2_all_ready
            eps2_ready rstd2_ready x2_ready rows_ready x2T_done x2T_ready logits_done
            lg_ready lmax_ready ld_ready lex_ready lsum_ready gate_ready eq_ready eqr_ready first_ready onehot_ready
            ranks_done slot1 slot2 slot3 slots_ready cnt_ready route scattered
            ge_ready ef_ready e_ready gathered0 gathered1 gathered2 gathered3 gathered4 gathered5 token_taken gxT_done gxT_ready up_done hid_ready gel_ready
            gelT_done gelT_ready down_done z_a z_b z_st z_agg z_eps z_rs z_ready row_used out_st0 out_st1 out_st2 out_st3 out_st4 out_st5
        """.split()}

        x_in = [S[f"x_in{r}"] for r in range(4)]

        def count_first(eng, *values):
            values = [v if isinstance(v, int) else eng.to_reg(v) for v in values]
            eng.wait_ge(S["consts_in"], 16)
            return values if len(values) > 1 else values[0]
        scored, used, max_a, maxed, exped = ([S[f"{k}{half}"] for half in range(2)] for k in ("scored", "used", "max_a", "max", "exp"))
        gathered = [S[f"gathered{r}"] for r in range(RING)]
        stored = [S[f"out_st{r}"] for r in range(RING)]

        scores_ps = [ps[:, half, :].rearrange("p (h k) -> p h k", k=T) for half in range(2)]
        nullT_ps, null_ps, wo_ps = ps[0:16, 2, 0:P], ps[:, 3, 0:H], ps[:, 3, 128:256]
        probsT_ps = [ps[:, 4 + half, :] for half in range(2)]
        attn_ps, den_ps = ps[:, 6, 0:128], ps[:, 6, 128:256]
        proj_ps, qkT_ps, v_ps = ps[:, 7, 0:384], ps[:, 7, 0:256], ps[:, 7, 256:512]

        block = ctx.enter_context(nc.Block())

        @block.sync
        def _(sp):
            sp.dma_start(wqk[:, :], a["wqk"]).then_inc(S["attn_in"], 16)
            sp.dma_start(consts[:, :], a["consts"]).then_inc(S["consts_in"], 16)

            def load_x(t):
                if t.i is not None or t.c >= 4:
                    sp.wait_ge(S["v_done"], t.n - 3)
                sp.dma_start(xT[:, t.ring(4), :], a["xT"][:, bass.ds(t.n * P, P)]).then_inc(x_in[t.ring(4)], 16)

            for n in range(4):
                load_x(Tile(n))
            sp.dma_start(wv[:, :], a["wv"]).then_inc(S["attn_in"], 16)
            sp.dma_start(cols[:, :], a["cols"]).then_inc(S["attn_in"], 16)
            sp.dma_start(vnull_bc[:, :], a["v_null"].partition_broadcast(16)).then_inc(S["attn_in"], 16)
            sp.dma_start(wo[:, :], a["wo"]).then_inc(S["attn_in"], 16)
            sp.dma_start(x_all[:, :, :], a["x"].rearrange("(t p) d -> p t d", p=P)).then_inc(S["x_all_in"], 16)
            with sp.Fori(0, NT // 4 - 1) as i:
                for c in range(4, 8):
                    load_x(Tile(c, i, 4))

            def load_rows(t, static):
                r = t.ring(RING)
                if not static or t.c >= RING:
                    sp.wait_ge(S["token_taken"], t.n - (RING - 1))
                sp.dma_start(g_rows[:, r, :], rows_dram[bass.ds(t.n * P, P), :]).then_inc(gathered[r], 16)

            sp.wait_ge(S["scattered"], 16 * NT)
            for n in range(RING):
                load_rows(Tile(n), True)
            n0 = (SLOTS - RING) // RING
            with sp.Fori(0, n0) as i:
                for c in range(RING, 2 * RING):
                    load_rows(Tile(c, i, RING), False)
            for n in range(RING + RING * n0, SLOTS):
                load_rows(Tile(n), True)

        @block.gpsimd
        def _(pool):
            nc.gpsimd.memset(v_pad[:, :, :], 0.0).then_inc(S["pads_zero"], 1)
            pool.dma_start(ctx_all[:, :, :], a["ctx"].rearrange("(t p) d -> p t d", p=P)).then_inc(S["ctx_all_in"], 16)
            pool.dma_start(xattn_w[:, :, :], a["xattn_w"]).then_inc(S["weights_in"], 16)
            pool.dma_start(bo_bc[:, :], a["bo"].partition_broadcast(P)).then_inc(S["weights_in"], 16)
            pool.dma_start(wr[:, :], a["wr"]).then_inc(S["weights_in"], 16)
            pool.dma_start(br_bc[:, :], a["br"].partition_broadcast(P)).then_inc(S["weights_in"], 16)
            pool.dma_start(token_ids[:, :], a["token_ids"]).then_inc(S["ids_in"], 16)
            pool.dma_start(pad_row[:, :], a["pad_row"].partition_broadcast(P)).then_inc(S["pad_row_in"], 16)
            pool.wait_ge(S["pad_row_in"], 16)
            pool.dma_start(rows_dram.rearrange("(j p) r -> p j r", p=P),
                           pad_row[:, :].unsqueeze(1).to_broadcast([P, SLOTS, ROW])).then_inc(S["slots_empty"], 16)
            pool.dma_start(w1[:, :], a["w1"]).then_inc(S["ffn_in"], 16)
            pool.dma_start(w2[:, :], a["w2"]).then_inc(S["ffn_in"], 16)
            pool.dma_start(b1_bc[:, :], a["b1"].partition_broadcast(P)).then_inc(S["ffn_in"], 16)
            pool.dma_start(b2_bc[:, :], a["b2"].partition_broadcast(P)).then_inc(S["ffn_in"], 16)
            pool.wait_ge(S["ids_in"], 16)
            nc.gpsimd.tensor_copy(rows[:, :, D + 1:D + 2].bitcast(I32).squeeze(2), token_ids[:, :])

            def rope_add(t):
                turn = count_first(pool, t.n + 1)
                pool.wait_ge(S["rope_b_done"], turn)
                r = t.ring(2)
                ra = roped[:, r, :].rearrange("p (h c) -> p h c", c=HD)[:, :, 0:4]
                nc.gpsimd.tensor_tensor(ra, ra, rope_b[:, r, :].rearrange("p (h c) -> p h c", c=4), ALU.add).then_inc(S["rope_done"], 1)

            def qk_blocks(t):
                turn = count_first(pool, t.n + 1)
                pool.wait_ge(S["qkT_ready"], turn)
                r = t.ring(2)
                nc.gpsimd.tensor_tensor(q_strips[:, r, :, :], qkT[:, r, 0:P].unsqueeze(1).to_broadcast([P, STRIPS, P]),
                                        const("strip").unsqueeze(2).to_broadcast([P, STRIPS, P]), ALU.mult)
                src = qkT[:, r, P:2 * P].rearrange("p (b k) -> p b k", b=BPT).unsqueeze(2).to_broadcast([P, BPT, HPS, T])
                m = const("strip_head").unsqueeze(1).unsqueeze(3).to_broadcast([P, BPT, HPS, T])
                nc.gpsimd.tensor_tensor(k4[:, r, :, :, :], src, m, ALU.mult).then_inc(S["k4_ready"], 1)

            pool.wait_ge(S["pads_zero"], 1)
            rope_add(Tile(0))
            qk_blocks(Tile(0))
            rope_add(Tile(1))
            qk_blocks(Tile(1))
            rope_add(Tile(2))

            def attn_step(t, static):
                qk_blocks(t + 2)
                if not static or t.c + 3 < NT:
                    rope_add(t + 3)

            run_steps(pool, attn_step, NT - 2, 4, 2)

            def inverse_std(k, ready, done):
                pool.wait_ge(S[ready], 1)
                nc.gpsimd.tensor_tensor(rstd[:, k, :], var_eps[:, k, :], const("minus_half"), ALU.pow).then_inc(S[done], 1)

            inverse_std(0, "eps_ready", "rstd_ready")

            pool.wait_ge(S["ctx_all_in"], 16)
            pool.wait_ge(S["x1_ready"], NT)
            pool.wait_ge(S["bvo_ready"], 1)

            def mix_inputs(t, _):
                r = t.ring(2)
                if t.i is not None and t.c >= 2 or t.i is None and t.c >= 2:
                    turn = count_first(pool, t.n - 1)
                    pool.wait_ge(S["y2_ready"], turn)
                nc.gpsimd.tensor_copy(ctx_in[:, r, :], ctx_all[:, bass.ds(t.n, 1), :].squeeze(1)).then_inc(S["ctx_in_ready"], 1)
                nc.gpsimd.tensor_tensor(x1b[:, r, :], y_all[:, bass.ds(t.n, 1), :].squeeze(1), bvo[:, :], ALU.add).then_inc(S["x1b_ready"], 1)

            mix_inputs(Tile(0), True)
            mix_inputs(Tile(1), True)
            with pool.Fori(0, NT // 2 - 1) as i:
                mix_inputs(Tile(2, i, 2), False)
                mix_inputs(Tile(3, i, 2), False)

            inverse_std(1, "eps2_ready", "rstd2_ready")

            def keep_rows(t, _):
                turn = count_first(pool, t.n + 1)
                pool.wait_ge(S["x2_ready"], turn)
                nc.gpsimd.tensor_copy(rows[:, bass.ds(t.n, 1), 0:D].squeeze(1), x2_in[:, t.ring(2), :]).then_inc(S["rows_ready"], 1)

            run_steps(pool, keep_rows, NT, 2, 0)

            pool.wait_ge(S["slots_ready"], 1)
            pool.wait_ge(S["gate_ready"], 1)
            pool.wait_ge(S["rows_ready"], NT)
            pool.wait_ge(S["slots_empty"], 16)
            for t in range(NT):
                pool.indirect_dma_start(out=rows_dram, out_offset=bass.IndirectOffsetOnAxis(ap=slots[:, t:t + 1], axis=0),
                                        in_=rows[:, t, :], in_offset=None, bounds_check=SLOTS * P - 1,
                                        oob_is_err=False).then_inc(S["scattered"], 16)
            def finish_tile(t, static):
                r, q = t.ring(2), t.ring(RING)
                pool.wait_ge(S["z_eps"], t.n + 1)
                nc.gpsimd.tensor_tensor(z_rstd[:, r, 1:2], z_rstd[:, r, 0:1], const("minus_half")[:, 0:1], ALU.pow).then_inc(S["z_rs"], 1)
                turn, lap = count_first(pool, t.n + 1, t.turn(RING) * 16)
                pool.wait_ge(S["z_rs"], turn)
                if not static or t.c >= RING:
                    pool.wait_ge(stored[q], lap)
                nc.gpsimd.tensor_scalar(z_out[:, q, :], z[:, r, :], z_mv[:, r, 0:1], z_rstd[:, r, 1:2], ALU.subtract, ALU.mult).then_inc(S["z_ready"], 1)
                turn = count_first(pool, t.n + 1)
                pool.wait_ge(S["z_ready"], turn)
                pool.indirect_dma_start(out=out, out_offset=bass.IndirectOffsetOnAxis(ap=z_token[:, q, :].bitcast(U32), axis=0),
                                        in_=z_out[:, q, :], in_offset=None, bounds_check=NT * P - 1,
                                        oob_is_err=False).then_inc(stored[q], 16)

            for n in range(RING):
                finish_tile(Tile(n), True)
            n0 = (SLOTS - RING) // RING
            with pool.Fori(0, n0) as i:
                for c in range(RING, 2 * RING):
                    finish_tile(Tile(c, i, RING), False)
            for n in range(RING + RING * n0, SLOTS):
                finish_tile(Tile(n), True)
            for r in range(RING):
                pool.wait_ge(stored[r], 16 * ((SLOTS - 1 - r) // RING + 1))

        @block.tensor
        def _(pe):
            def project(t):
                pe.wait_ge(x_in[t.ring(4)], (t.turn(4) + 1) * 16)
                if t.i is not None or t.c >= 1:
                    pe.wait_ge(S["v_ready"], t.n)
                nc.tensor.matmul(proj_ps, xT[:, t.ring(4), :], wqk[:, :], start=True, stop=True).then_inc(S["proj_done"], 1)

            def turn_qk(t):
                r = t.ring(2)
                pe.wait_ge(S["rope_done"], t.n + 1)
                nc.tensor.transpose(qkT_ps[:, 0:128], roped[:, r, 0:128], ident)
                nc.tensor.transpose(qkT_ps[:, 128:256], roped[:, r, 128:256], ident)
                for b in range(BPT):
                    for half in range(2):
                        last = nc.tensor.matmul(v_ps[64 * half:64 * half + 64, b * P:(b + 1) * P], xT[:, t.ring(4), b * T:(b + 1) * T],
                                                wv[:, :], start=True, stop=True)
                last.then_inc(S["v_done"], 1)

            def scores(t):
                r = t.ring(2)
                pe.wait_ge(S["k4_ready"], t.n + 1)
                if t.i is not None or t.c >= 3:
                    pe.wait_ge(S["wo_used"], t.n - 2)
                nc.tensor.matmul(null_ps, qkT[:, r, 0:P], knull[:, :], start=True, stop=True).then_inc(S["null_done"], 1)
                for half in range(2):
                    if t.i is not None or t.c >= 1:
                        pe.wait_ge(used[half], t.n)
                    nc.tensor.matmul(ps[:, half, :], ident_b, mask_b, start=True, stop=False, skip_group_check=True)
                    for s in range(2):
                        for b in range(BPT):
                            last = nc.tensor.matmul(ps[b * T:(b + 1) * T, half, 256 * s:256 * s + 256],
                                                    q_strips[:, r, 2 * half + s, b * T:(b + 1) * T],
                                                    k4[:, r, b, :, :], start=False, stop=True, skip_group_check=True)
                    last.then_inc(scored[half], 1)

            def turn_probs(t):
                r = t.ring(2)
                if t.i is not None or t.c >= 1:
                    pe.wait_ge(S["null_ready"], t.n)
                for half in range(2):
                    pe.wait_ge(exped[half], t.n + 1)
                    for c in range(4 * half, 4 * half + 4):
                        nc.tensor.transpose(probsT_ps[half][:, (c % 4) * P:(c % 4 + 1) * P], probs[:, r, c * P:(c + 1) * P], ident)
                nc.tensor.transpose(nullT_ps, probs[:, r, H * T:H * T + H], ident).then_inc(S["probsT_done"], 1)

            def mix_values(t):
                r = t.ring(2)
                pe.wait_ge(S["null_ready"], t.n + 1)
                pe.wait_ge(S["probsT_ready"], t.n + 1)
                pe.wait_ge(S["v_ready"], t.n + 1)
                if t.i is not None or t.c >= 1:
                    pe.wait_ge(S["attn_ready"], t.n)
                nc.tensor.matmul(attn_ps, vnull[:, :], nullT[:, r, :], start=True, stop=False, skip_group_check=True)
                for ab in range(2):
                    for b in range(BPT):
                        for s in range(STRIPS):
                            at = 2 * VW * b + P * ab + 32 * s
                            nc.tensor.matmul(attn_ps[32 * s:32 * s + 32, b * T:(b + 1) * T], v_pad[:, t.ring(4), at:at + 32],
                                             probsT[:, r, 4 * ab + s, b * T:(b + 1) * T], start=False, stop=(ab == 1),
                                             skip_group_check=True)
                nc.tensor.matmul(den_ps, const("row_head", 16), nullT[:, r, :], start=True, stop=False, skip_group_check=True)
                for ab in range(2):
                    for s in range(STRIPS):
                        last = nc.tensor.matmul(den_ps[32 * s:32 * s + 32, :], const("den_ones")[:, 32 * ab:32 * ab + 32],
                                                probsT[:, r, 4 * ab + s, :], start=False, stop=(ab == 1), skip_group_check=True)
                last.then_inc(S["attn_done"], 1)

            def project_out(t, null_too):
                pe.wait_ge(S["attn_ready"], t.n + 1)
                if null_too:
                    pe.wait_ge(S["null_taken"], t.n + 3)
                nc.tensor.matmul(wo_ps, attnT[:, t.ring(2), :], wo[:, :], start=True, stop=True).then_inc(S["wo_done"], 1)

            pe.wait_ge(S["attn_in"], 16 * 5)
            pe.wait_ge(S["consts_in"], 16)
            project(Tile(0))
            turn_qk(Tile(0))
            pe.wait_ge(S["bf16_ready"], 1)
            pe.wait_ge(S["knull_ready"], 1)
            pe.wait_ge(S["vnull_ready"], 1)
            project(Tile(1))
            turn_qk(Tile(1))
            scores(Tile(0))
            project(Tile(2))

            def attn_step(t, static):
                turn_probs(t)
                if not static or t.c + 2 < NT:
                    turn_qk(t + 2)
                if not static or t.c + 1 < NT:
                    scores(t + 1)
                if not static or t.c + 3 < NT:
                    project(t + 3)
                if not static or t.c >= 1:
                    project_out(t + -1, not static or t.c + 1 < NT)
                mix_values(t)

            for n in range(4):
                attn_step(Tile(n), True)
            with pe.Fori(0, (NT - 8) // 4) as i:
                for c in range(4, 8):
                    attn_step(Tile(c, i, 4), False)
            for n in range(NT - 4, NT):
                attn_step(Tile(n), True)
            project_out(Tile(NT - 1), False)

            sums_ps = ps[:, 0, 0:2 * B]
            pe.wait_ge(S["ctx_all_in"], 16)
            pe.wait_ge(S["weights_in"], 64)
            for t in range(NT):
                last = nc.tensor.matmul(sums_ps[:, BPT * t:BPT * (t + 1)], ctx_all[:, t, :], const("batch_ind"), start=True, stop=True)
            last.then_inc(S["sums_k"], 1)
            nc.tensor.matmul(ps[:, 1, 0:128], xattn_w[:, 2, :], xattn_w[:, 3, :], start=True, stop=True)
            pe.wait_ge(S["bv_ready"], 1)
            nc.tensor.matmul(ps[:, 1, 128:256], bv_bc[:, :], xattn_w[:, 3, :], start=True, stop=True).then_inc(S["bvo_done"], 1)
            pe.wait_ge(S["x1_ready"], NT)
            for t in range(NT):
                last = nc.tensor.matmul(sums_ps[:, B + BPT * t:B + BPT * (t + 1)], y_all[:, t, :], const("batch_ind"), start=True, stop=True)
            last.then_inc(S["sums_ready"], 1)
            pe.wait_ge(S["sumT_ready"], 1)
            nc.tensor.matmul(ps[:, 2, 0:B], xattn_w[:, 1, :], sumT[:, 0, :], start=True, stop=True)
            nc.tensor.matmul(ps[:, 2, B:2 * B], xattn_w[:, 0, :], sumT[:, 1, :], start=True, stop=True).then_inc(S["sqk_done"], 1)
            pe.wait_ge(S["prod_ready"], 1)
            nc.tensor.matmul(ps[0:B, 3, 0:8], sqk[:, 2, :], const("chan8"), start=True, stop=True).then_inc(S["mean_done"], 1)
            pe.wait_ge(S["wt_ready"], 1)
            nc.tensor.matmul(ps[:, 3, 128:256], const("batch_rows", B), w_tiles[:, :], start=True, stop=True).then_inc(S["wtok_done"], 1)

            def ctx_ps(r):
                return ps[:, 4 + r, 0:128]

            def mix_ps(r):
                return ps[:, 6 + r, 0:128]

            def aggregate(t):
                r = t.ring(2)
                pe.wait_ge(S["ctx_in_ready"], t.n + 1)
                pe.wait_ge(S["circ_ready"], t.n + 1)
                if t.i is not None or t.c >= 2:
                    pe.wait_ge(S["ctxT_ready"], t.n - 1)
                nc.tensor.matmul(ctx_ps(r), ctx_in[:, r, :], circ[:, r, :], start=True, stop=True).then_inc(S["ctxT_done"], 1)

            pe.wait_ge(S["wvo_ready"], 1)

            def mix_step(t, static):
                if not static or t.c + 1 < NT:
                    aggregate(t + 1)
                r = t.ring(2)
                pe.wait_ge(S["ctxT_ready"], t.n + 1)
                nc.tensor.matmul(mix_ps(r), ctxT[:, r, :], wvo[:, :], start=True, stop=True).then_inc(S["mix_done"], 1)

            def mix_step_w(t, static):
                if not static or t.c >= 2:
                    pe.wait_ge(S["y2_ready"], t.n - 1)
                mix_step(t, static)

            aggregate(Tile(0))
            mix_step_w(Tile(0), True)
            mix_step_w(Tile(1), True)
            with pe.Fori(0, NT // 2 - 2) as i:
                mix_step_w(Tile(2, i, 2), False)
                mix_step_w(Tile(3, i, 2), False)
            mix_step_w(Tile(NT - 2), True)
            mix_step_w(Tile(NT - 1), True)

            lg_ps = ps[:, 0, 0:NT * E]

            def x2T_ps(r):
                return ps[:, 4 + r, 0:128]

            def turn_x2(t):
                r = t.ring(2)
                pe.wait_ge(S["x2_ready"], t.n + 1)
                nc.tensor.transpose(x2T_ps(r), x2_in[:, r, :], ident).then_inc(S["x2T_done"], 1)

            def router_step(t, static):
                if not static or t.c + 1 < NT:
                    turn_x2(t + 1)
                pe.wait_ge(S["x2T_ready"], t.n + 1)
                nc.tensor.matmul(lg_ps[:, bass.ds(t.n * E, E)], x2T[:, t.ring(2), :], wr[:, :], start=True, stop=True).then_inc(S["logits_done"], 1)

            turn_x2(Tile(0))
            run_steps(pe, router_step, NT, 2, 2)

            pe.wait_ge(S["onehot_ready"], 1)
            oh = onehot[:, :, :].rearrange("p t e -> p (t e)")
            nc.tensor.matmul(ps[:, 1, 0:128], tri_b, oh, start=True, stop=False, skip_group_check=True)
            for s in range(1, NT):
                nc.tensor.matmul(ps[:, 1, E * s:128], ones_b, oh[:, 0:128 - E * s], start=False, stop=(s == NT - 1), skip_group_check=True)
            for t in range(NT):
                last = nc.tensor.matmul(ps[:, 2, 0:E], ones_b, oh[:, E * t:E * (t + 1)], start=(t == 0), stop=(t == NT - 1))
            last.then_inc(S["ranks_done"], 1)

            def gxT_ps(r):
                return ps[:, 4 + r, 0:P]

            def y_ps(r):
                return ps[:, 6 + r, 0:D]

            def turn_rows(t):
                pe.wait_ge(gathered[t.ring(RING)], (t.turn(RING) + 1) * 16)
                nc.tensor.transpose(gxT_ps(t.ring(2)), g_rows[:, t.ring(RING), 0:D], ident).then_inc(S["gxT_done"], 1)

            def up(t):
                r = t.ring(2)
                e = pe.value_load(e_i[0:1, bass.ds(t.n, 1)], min_val=0, max_val=E - 1)
                pe.wait_ge(S["gxT_ready"], t.n + 1)
                if t.i is not None or t.c >= 2:
                    pe.wait_ge(S["hid_ready"], t.n - 1)
                nc.tensor.matmul(ps[:, r, :], gxT[:, r, :], w1[:, bass.ds(e * F, F)], start=True, stop=True).then_inc(S["up_done"], 1)

            def turn_hidden(t):
                r = t.ring(2)
                pe.wait_ge(S["gel_ready"], t.n + 1)
                for c in range(FC):
                    last = nc.tensor.transpose(ps[:, 2 + r, c * P:(c + 1) * P], gel[:, r, c * P:(c + 1) * P], ident)
                last.then_inc(S["gelT_done"], 1)

            def down(t, static):
                r = t.ring(2)
                e = pe.value_load(e_i[0:1, bass.ds(t.n, 1)], min_val=0, max_val=E - 1)
                pe.wait_ge(S["gelT_ready"], t.n + 1)
                if not static or t.c >= 2:
                    pe.wait_ge(S["z_a"], t.n - 1)
                for c in range(FC):
                    last = nc.tensor.matmul(y_ps(r), gelT[:, r, c * P:(c + 1) * P], w2[:, bass.ds(e * (FC * D) + c * D, D)],
                                            start=(c == 0), stop=(c == FC - 1))
                last.then_inc(S["down_done"], 1)

            pe.wait_ge(S["e_ready"], 1)
            pe.wait_ge(S["ffn_in"], 64)
            turn_rows(Tile(0))
            turn_rows(Tile(1))
            up(Tile(0))
            turn_rows(Tile(2))
            up(Tile(1))

            def expert_step(t, static):
                turn_hidden(t)
                if not static or t.c + 2 < SLOTS:
                    up(t + 2)
                if not static or t.c + 3 < SLOTS:
                    turn_rows(t + 3)
                down(t, static)

            expert_step(Tile(0), True)
            expert_step(Tile(1), True)
            n0 = (SLOTS - 2 - 3) // RING
            with pe.Fori(0, n0) as i:
                for c in range(2, 2 + RING):
                    expert_step(Tile(c, i, RING), False)
            for n in range(2 + RING * n0, SLOTS):
                expert_step(Tile(n), True)

        @block.scalar
        def _(act):
            def copy(o, i):
                return nc.scalar.activation(o, i, ACT.Copy)

            def take_probsT(t):
                r = t.ring(2)
                act.wait_ge(S["probsT_done"], t.n + 1)
                copy(probsT[:, r, 0:4, :].rearrange("p a b -> p (a b)"), probsT_ps[0])
                copy(probsT[:, r, 4:8, :].rearrange("p a b -> p (a b)"), probsT_ps[1]).then_inc(S["probsT_ready"], 1)

            def take_qv(t):
                r = t.ring(2)
                act.wait_ge(S["v_done"], t.n + 1)
                copy(qkT[:, r, :], qkT_ps).then_inc(S["qkT_ready"], 1)
                for half in range(2):
                    rows_h = slice(64 * half, 64 * half + 64)
                    dst = v_pad[rows_h, t.ring(4), :].rearrange("p (g w) -> p g w", w=VW)[:, :, 0:P].rearrange("p g (s c) -> p g s c", c=32)
                    src = v_ps[rows_h, :].rearrange("p (g s c) -> p g s c", g=4, s=4)
                    last = copy(dst[:, :, :, 8 * half:8 * half + 8], src[:, :, :, 8 * half:8 * half + 8])
                last.then_inc(S["v_ready"], 1)

            def exponent(t):
                r = t.ring(2)
                for half, cols_h in enumerate((slice(0, 512), slice(512, H * T + H))):
                    act.wait_ge(used[half], t.n + 1)
                    nc.scalar.activation(probs[:, r, cols_h], probs[:, r, cols_h], ACT.Exp, scale=SCALE).then_inc(exped[half], 1)

            act.wait_ge(S["pads_zero"], 1)
            take_qv(Tile(0))
            take_qv(Tile(1))
            exponent(Tile(0))

            def attn_step(t, static):
                take_probsT(t)
                if not static or t.c + 2 < NT:
                    take_qv(t + 2)
                if not static or t.c + 1 < NT:
                    exponent(t + 1)

            run_steps(act, attn_step, NT, 4, 4)
            act.wait_ge(S["m_sub"], 1)
            nc.scalar.activation(wsm[:, 1, :], wsm[:, 0, :], ACT.Exp).then_inc(S["m_exp"], 1)

            def take_ctx(t, _):
                act.wait_ge(S["ctxT_done"], t.n + 1)
                copy(ctxT[:, t.ring(2), :], ps[:, 4 + t.ring(2), 0:128]).then_inc(S["ctxT_ready"], 1)

            run_steps(act, take_ctx, NT, 2, 0)

            def take_x2(t, _):
                act.wait_ge(S["x2T_done"], t.n + 1)
                copy(x2T[:, t.ring(2), :], ps[:, 4 + t.ring(2), 0:128]).then_inc(S["x2T_ready"], 1)

            run_steps(act, take_x2, NT, 2, 0)
            act.wait_ge(S["ld_ready"], 1)
            nc.scalar.activation(lex[:, :, :], lg[:, :, :], ACT.Exp).then_inc(S["lex_ready"], 1)

            def take_rows(t):
                act.wait_ge(S["gxT_done"], t.n + 1)
                copy(gxT[:, t.ring(2), :], ps[:, 4 + t.ring(2), 0:P]).then_inc(S["gxT_ready"], 1)

            def gelu(t):
                r = t.ring(2)
                act.wait_ge(S["hid_ready"], t.n + 1)
                nc.scalar.activation(gel[:, r, :], hid[:, r, :], ACT.Gelu).then_inc(S["gel_ready"], 1)

            def take_hidden(t):
                r = t.ring(2)
                act.wait_ge(S["gelT_done"], t.n + 1)
                copy(gelT[:, r, :], ps[:, 2 + r, :]).then_inc(S["gelT_ready"], 1)

            take_rows(Tile(0))
            take_rows(Tile(1))
            take_rows(Tile(2))
            gelu(Tile(0))

            def expert_step(t, static):
                take_hidden(t)
                if not static or t.c + 1 < SLOTS:
                    gelu(t + 1)
                if not static or t.c + 3 < SLOTS:
                    take_rows(t + 3)

            run_steps(act, expert_step, SLOTS, RING, 3)

        @block.vector
        def _(dve):
            v = nc.vector
            route_step = [0]

            def chained(ins, name="route"):
                route_step[0] += 1
                ins.then_inc(S["route"], 1)
                dve.wait_ge(S["route"], route_step[0])

            def rope(t):
                r = t.ring(2)
                dve.wait_ge(S["proj_done"], t.n + 1)
                main = proj_ps[:, 0:256].rearrange("p (h c) -> p h c", c=HD)
                swapped = proj_ps[:, 256:384].rearrange("p (h c) -> p h c", c=4)
                ra = roped[:, r, :].rearrange("p (h c) -> p h c", c=HD)
                rb = rope_b[:, r, :].rearrange("p (h c) -> p h c", c=4)
                v.tensor_tensor(ra, main, const("cos8").unsqueeze(1).to_broadcast([P, 2 * H, HD]), ALU.mult)
                v.tensor_tensor(rb, swapped, const("sin4").unsqueeze(1).to_broadcast([P, 2 * H, 4]), ALU.mult).then_inc(S["rope_b_done"], 1)

            def take_null(t):
                dve.wait_ge(S["null_done"], t.n + 1)
                v.tensor_copy(null_s[:, t.ring(2), :], null_ps).then_inc(S["null_taken"], 1)

            def subtract_max(t):
                r = t.ring(2)
                for half in range(2):
                    heads = slice(8 * half, 8 * half + 8)
                    dve.wait_ge(scored[half], t.n + 1)
                    v.tensor_reduce(row_max[:, r, heads], scores_ps[half], AX.X, ALU.max).then_inc(max_a[half], 1)
                    dve.wait_ge(max_a[half], t.n + 1)
                    dve.wait_ge(S["null_taken"], t.n + 1)
                    v.tensor_tensor(row_max2[:, r, heads], row_max[:, r, heads], null_s[:, r, heads], ALU.max).then_inc(maxed[half], 1)
                    dve.wait_ge(maxed[half], t.n + 1)
                    if half == 1:
                        v.tensor_tensor(probs[:, r, H * T:H * T + H], null_s[:, r, :], row_max2[:, r, :], ALU.subtract)
                    v.tensor_tensor(probs[:, r, 512 * half:512 * half + 512].rearrange("p (h k) -> p h k", k=T), scores_ps[half],
                                    row_max2[:, r, heads].unsqueeze(2).to_broadcast([P, 8, T]), ALU.subtract).then_inc(used[half], 1)

            def take_nullT(t):
                dve.wait_ge(S["probsT_done"], t.n + 1)
                v.tensor_copy(nullT[:, t.ring(2), :], nullT_ps).then_inc(S["null_ready"], 1)

            def normalize(t):
                r = t.ring(2)
                dve.wait_ge(S["attn_done"], t.n + 1)
                v.reciprocal(rden[:, r, :], den_ps).then_inc(S["attn_r"], 1)
                dve.wait_ge(S["attn_r"], t.n + 1)
                v.tensor_tensor(attnT[:, r, :], attn_ps, rden[:, r, :], ALU.mult).then_inc(S["attn_ready"], 1)

            def residual(t):
                y = y_all[:, bass.ds(t.n, 1), :].squeeze(1)
                dve.wait_ge(S["wo_done"], t.n + 1)
                v.tensor_tensor(y, wo_ps, x_all[:, bass.ds(t.n, 1), :].squeeze(1), ALU.add).then_inc(S["wo_used"], 1)

            def statistics(t):
                turn = count_first(dve, t.n + 1)
                dve.wait_ge(S["wo_used"], turn)
                v.bn_stats(stats[:, bass.ds(t.n, 1), :].squeeze(1), y_all[:, bass.ds(t.n, 1), :].squeeze(1)).then_inc(S["y_all_ready"], 1)

            dve.wait_ge(S["consts_in"], 16)
            dve.wait_ge(S["attn_in"], 80)
            v.tensor_copy(ident_b, ident)
            v.tensor_copy(mask_b.rearrange("p (h k) -> p h k", k=T), const("causal").unsqueeze(1).to_broadcast([P, 8, T]))
            v.tensor_copy(tri_b, const("earlier"))
            v.memset(ones_b, 1.0).then_inc(S["bf16_ready"], 1)
            v.tensor_scalar(knull[:, :], const("head16"), cols[:, 0:1], None, ALU.mult).then_inc(S["knull_ready"], 1)
            v.tensor_tensor(vnull[:, :], const("row_head", 16), vnull_bc[:, :], ALU.mult).then_inc(S["vnull_ready"], 1)
            v.tensor_scalar(bv_bc[:, :], ident, 0.0, cols[:, 3:4], ALU.mult, ALU.add).then_inc(S["bv_ready"], 1)
            rope(Tile(0))
            rope(Tile(1))
            take_null(Tile(0))
            subtract_max(Tile(0))
            rope(Tile(2))
            dve.wait_ge(S["x_all_in"], 16)

            def attn_step(t, static):
                take_nullT(t)
                if not static or t.c >= 1:
                    normalize(t + -1)
                if not static or t.c + 1 < NT:
                    take_null(t + 1)
                    subtract_max(t + 1)
                if not static or t.c >= 1:
                    residual(t + -1)
                if not static or t.c + 3 < NT:
                    rope(t + 3)
                if not static or t.c >= 1:
                    statistics(t + -1)

            for n in range(4):
                attn_step(Tile(n), True)
            with dve.Fori(0, (NT - 8) // 4) as i:
                for c in range(4, 8):
                    attn_step(Tile(c, i, 4), False)
            for n in range(NT - 4, NT):
                attn_step(Tile(n), True)
            normalize(Tile(NT - 1))
            residual(Tile(NT - 1))
            statistics(Tile(NT - 1))

            def mean_and_variance(k, st, mean, done):
                even, m2e, odd, m2o = (st[:, :, j:j + 1].squeeze(2) for j in (1, 2, 4, 5))
                chained(v.tensor_tensor(mean_gap[:, :], even, odd, ALU.subtract))
                chained(v.tensor_tensor(mean[:, :], even, odd, ALU.add))
                chained(v.tensor_scalar(mean[:, :], mean[:, :], 0.5, None, ALU.mult))
                chained(v.tensor_tensor(var_eps[:, k, :], m2e, m2o, ALU.add))
                chained(v.tensor_tensor(mean_gap[:, :], mean_gap[:, :], mean_gap[:, :], ALU.mult))
                chained(v.tensor_scalar(var_eps[:, k, :], var_eps[:, k, :], 1.0 / D, EPS, ALU.mult, ALU.add))
                v.scalar_tensor_tensor(var_eps[:, k, :], mean_gap[:, :], 0.25, var_eps[:, k, :], ALU.mult, ALU.add).then_inc(S[done], 1)

            def normed(k, mean_var, source, target, ready, done):
                dve.wait_ge(S[ready], 1)

                def one(t, _):
                    target_ap = target(t)
                    v.tensor_scalar(target_ap, source[:, bass.ds(t.n, 1), :].squeeze(1), mean_var[:, bass.ds(t.n, 1)],
                                    rstd[:, k, bass.ds(t.n, 1)], ALU.subtract, ALU.mult).then_inc(S[done], 1)
                return one

            dve.wait_ge(S["y_all_ready"], NT)
            mean_and_variance(0, stats, mv, "eps_ready")
            dve.wait_ge(S["bvo_done"], 1)
            dve.wait_ge(S["weights_in"], 64)
            v.tensor_copy(wvo[:, :], ps[:, 1, 0:128]).then_inc(S["wvo_ready"], 1)
            v.tensor_tensor(bvo[:, :], ps[:, 1, 128:256], bo_bc[:, :], ALU.add).then_inc(S["bvo_ready"], 1)
            one = normed(0, mv, y_all, lambda t: y_all[:, bass.ds(t.n, 1), :].squeeze(1), "rstd_ready", "x1_ready")
            run_steps(dve, one, NT, 2, 0)

            dve.wait_ge(S["sums_ready"], 1)
            v.tensor_copy(sumT[:, :, :].rearrange("p a b -> p (a b)"), ps[:, 0, 0:2 * B]).then_inc(S["sumT_ready"], 1)
            v.tensor_scalar(cols[:, 1:3], cols[:, 1:3], float(T), None, ALU.mult).then_inc(S["sk_ready"], 1)
            dve.wait_ge(S["sqk_done"], 1)
            dve.wait_ge(S["sk_ready"], 1)
            v.tensor_scalar(sqk[:, 0, :], ps[:, 2, 0:B], cols[:, 2:3], 1.0 / (H * T), ALU.add, ALU.mult).then_inc(S["sq_ready"], 1)
            dve.wait_ge(S["sq_ready"], 1)
            v.scalar_tensor_tensor(sqk[:, 2, :], ps[:, 2, B:2 * B], cols[:, 1:2], sqk[:, 0, :], ALU.add, ALU.mult).then_inc(S["prod_ready"], 1)
            dve.wait_ge(S["mean_done"], 1)
            mean = ps[0:B, 3, 0:8]
            v.tensor_reduce(wcol[:, 0:1], mean, AX.X, ALU.max).then_inc(S["m_max"], 1)
            dve.wait_ge(S["m_max"], 1)
            v.tensor_scalar(wsm[:, 0, :], mean, wcol[:, 0:1], None, ALU.subtract).then_inc(S["m_sub"], 1)
            dve.wait_ge(S["m_exp"], 1)
            v.tensor_reduce(wcol[:, 1:2], wsm[:, 1, :], AX.X, ALU.add).then_inc(S["m_sum"], 1)
            dve.wait_ge(S["m_sum"], 1)
            v.reciprocal(wcol[:, 2:3], wcol[:, 1:2]).then_inc(S["m_rec"], 1)
            dve.wait_ge(S["m_rec"], 1)
            v.tensor_scalar(wsm[:, 2, :], wsm[:, 1, :], wcol[:, 2:3], None, ALU.mult).then_inc(S["w_ready"], 1)
            dve.wait_ge(S["w_ready"], 1)
            v.tensor_tensor(w_tiles[:, :].rearrange("p (t c) -> p t c", c=8), const("batch_tile", B).rearrange("p (t c) -> p t c", c=8),
                            wsm[:, 2, :].unsqueeze(1).to_broadcast([B, NT, 8]), ALU.mult).then_inc(S["wt_ready"], 1)
            dve.wait_ge(S["wtok_done"], 1)
            v.tensor_copy(w_tok[:, :], ps[:, 3, 128:256]).then_inc(S["wtok_ready"], 1)
            dve.wait_ge(S["wtok_ready"], 1)
            taps = w_taps[:, :].rearrange("p (t r c) -> p t r c", r=8, c=8)
            v.tensor_tensor(taps, w_tok[:, :].rearrange("p (t c) -> p t c", c=8).unsqueeze(2).to_broadcast([P, NT, 8, 8]),
                            const("tap_of").rearrange("p (r c) -> p r c", c=8).unsqueeze(1).to_broadcast([P, NT, 8, 8]),
                            ALU.mult).then_inc(S["wtaps"], 1)
            dve.wait_ge(S["wtaps"], 1)
            v.tensor_reduce(w_perm[:, :].rearrange("p (t r) -> p t r", r=8), taps, AX.X, ALU.add).then_inc(S["wperm_ready"], 1)
            dve.wait_ge(S["wperm_ready"], 1)

            def circulant(t):
                r = t.ring(2)
                if t.i is not None or t.c >= 2:
                    dve.wait_ge(S["ctxT_done"], t.n - 1)
                v.tensor_tensor(circ[:, r, :].rearrange("p (a r) -> p a r", r=8), const("band").rearrange("p (a r) -> p a r", r=8),
                                w_perm[:, bass.ds(t.n * 8, 8)].unsqueeze(1).to_broadcast([P, 16, 8]), ALU.mult).then_inc(S["circ_ready"], 1)

            def mix_step(t, static):
                r = t.ring(2)
                if not static or t.c + 2 < NT:
                    circulant(t + 2)
                y2 = y2_all[:, bass.ds(t.n, 1), :].squeeze(1)
                dve.wait_ge(S["mix_done"], t.n + 1)
                dve.wait_ge(S["x1b_ready"], t.n + 1)
                v.tensor_tensor(y2, ps[:, 6 + r, 0:128], x1b[:, r, :], ALU.add).then_inc(S["y2_ready"], 1)
                turn = count_first(dve, t.n + 1)
                dve.wait_ge(S["y2_ready"], turn)
                v.bn_stats(stats2[:, bass.ds(t.n, 1), :].squeeze(1), y2).then_inc(S["y2_all_ready"], 1)

            circulant(Tile(0))
            circulant(Tile(1))
            run_steps(dve, mix_step, NT, 2, 2)

            dve.wait_ge(S["y2_all_ready"], NT)
            mean_and_variance(1, stats2, mv2, "eps2_ready")
            one2 = normed(1, mv2, y2_all, lambda t: x2_in[:, t.ring(2), :], "rstd2_ready", "x2_ready")

            def norm2(t, static):
                if t.i is not None or t.c >= 2:
                    dve.wait_ge(S["x2T_done"], t.n - 1)
                    dve.wait_ge(S["rows_ready"], t.n - 1)
                one2(t, static)

            norm2(Tile(0), True)
            norm2(Tile(1), True)
            with dve.Fori(0, NT // 2 - 1) as i:
                norm2(Tile(2, i, 2), False)
                norm2(Tile(3, i, 2), False)

            dve.wait_ge(S["logits_done"], NT)
            per_tile = [P, NT, E]
            v.tensor_tensor(lg[:, :, :], ps[:, 0, 0:NT * E].rearrange("p (t e) -> p t e", e=E),
                            br_bc[:, :].unsqueeze(1).to_broadcast(per_tile), ALU.add).then_inc(S["lg_ready"], 1)
            dve.wait_ge(S["lg_ready"], 1)
            v.tensor_reduce(lmax[:, :], lg[:, :, :], AX.X, ALU.max).then_inc(S["lmax_ready"], 1)
            dve.wait_ge(S["lmax_ready"], 1)
            v.tensor_tensor(lg[:, :, :], lg[:, :, :], lmax[:, :].unsqueeze(2).to_broadcast(per_tile), ALU.subtract).then_inc(S["ld_ready"], 1)
            dve.wait_ge(S["ld_ready"], 1)
            v.tensor_scalar(eqr[:, :, :], lg[:, :, :], 0.0, None, ALU.is_equal).then_inc(S["eq_ready"], 1)
            dve.wait_ge(S["eq_ready"], 1)
            v.tensor_tensor(eqr[:, :, :], eqr[:, :, :], const("rev8").unsqueeze(1).to_broadcast(per_tile), ALU.mult).then_inc(S["eqr_ready"], 1)
            dve.wait_ge(S["eqr_ready"], 1)
            v.tensor_reduce(first[:, :], eqr[:, :, :], AX.X, ALU.max).then_inc(S["first_ready"], 1)
            dve.wait_ge(S["first_ready"], 1)
            v.tensor_tensor(onehot[:, :, :], eqr[:, :, :], first[:, :].unsqueeze(2).to_broadcast(per_tile), ALU.is_equal).then_inc(S["onehot_ready"], 1)
            dve.wait_ge(S["lex_ready"], 1)
            v.tensor_reduce(lsum[:, :], lex[:, :, :], AX.X, ALU.add).then_inc(S["lsum_ready"], 1)
            dve.wait_ge(S["lsum_ready"], 1)
            v.reciprocal(rows[:, :, D:D + 1].squeeze(2), lsum[:, :]).then_inc(S["gate_ready"], 1)
            dve.wait_ge(S["ranks_done"], 1)

            chained(v.tensor_copy(cnt[:, :], ps[:, 2, 0:E]))
            chained(v.tensor_tensor(over[:, :, :], cnt[:, :].unsqueeze(2).to_broadcast([P, E, 16]),
                                    const("thresholds").unsqueeze(1).to_broadcast([P, E, 16]), ALU.is_gt))
            chained(v.tensor_reduce(ntile[:, :], over[:, :, :], AX.X, ALU.add))
            chained(v.tensor_tensor(tmp64[:, :, :], const("before8").rearrange("p (a b) -> p a b", b=E),
                                    ntile[:, :].unsqueeze(1).to_broadcast([P, E, E]), ALU.mult))
            chained(v.tensor_reduce(start_t[:, :], tmp64[:, :, :], AX.X, ALU.add))
            chained(v.tensor_tensor(end_t[:, :], start_t[:, :], ntile[:, :], ALU.add))
            chained(v.tensor_scalar(start_t[:, :], start_t[:, :], float(P), None, ALU.mult))
            v.tensor_tensor(slot_f[:, :, :], ps[:, 1, 0:NT * E].rearrange("p (t e) -> p t e", e=E),
                            start_t[:, :].unsqueeze(1).to_broadcast(per_tile), ALU.add).then_inc(S["slot1"], 1)
            dve.wait_ge(S["slot1"], 1)
            v.tensor_tensor(slot_f[:, :, :], slot_f[:, :, :], onehot[:, :, :], ALU.mult).then_inc(S["slot2"], 1)
            dve.wait_ge(S["slot2"], 1)
            v.tensor_reduce(slot_a[:, :], slot_f[:, :, :], AX.X, ALU.add).then_inc(S["slot3"], 1)
            dve.wait_ge(S["slot3"], 1)
            v.tensor_copy(slots[:, :], slot_a[:, :]).then_inc(S["slots_ready"], 1)
            v.tensor_tensor(ge[:, :, :], const("slot_j").unsqueeze(2).to_broadcast([P, SLOTS, E]),
                            end_t[:, :].unsqueeze(1).to_broadcast([P, SLOTS, E]), ALU.is_ge).then_inc(S["ge_ready"], 1)
            dve.wait_ge(S["ge_ready"], 1)
            v.tensor_reduce(e_f[:, :], ge[:, :, :], AX.X, ALU.add).then_inc(S["ef_ready"], 1)
            dve.wait_ge(S["ef_ready"], 1)
            v.tensor_scalar(e_i[:, :], e_f[:, :], float(E - 1), None, ALU.min).then_inc(S["e_ready"], 1)

            def add_b1(t):
                r = t.ring(2)
                e = dve.value_load(e_i[0:1, bass.ds(t.n, 1)], min_val=0, max_val=E - 1)
                dve.wait_ge(S["up_done"], t.n + 1)
                v.tensor_tensor(hid[:, r, :], ps[:, r, :], b1_bc[:, bass.ds(e * F, F)], ALU.add).then_inc(S["hid_ready"], 1)

            def combine(t, static):
                r, q = t.ring(2), t.ring(RING)
                e = dve.value_load(e_i[0:1, bass.ds(t.n, 1)], min_val=0, max_val=E - 1)
                if not static or t.c >= RING:
                    dve.wait_ge(stored[q], t.turn(RING) * 16)
                if not static or t.c >= 2:
                    dve.wait_ge(S["z_ready"], t.n - 1)
                dve.wait_ge(S["down_done"], t.n + 1)
                v.tensor_tensor(z[:, r, :], ps[:, 6 + r, 0:D], b2_bc[:, bass.ds(e * D, D)], ALU.add).then_inc(S["z_a"], 1)
                dve.wait_ge(S["z_a"], t.n + 1)
                dve.wait_ge(gathered[q], (t.turn(RING) + 1) * 16)
                v.scalar_tensor_tensor(z[:, r, :], z[:, r, :], g_rows[:, q, D:D + 1], g_rows[:, q, 0:D], ALU.mult, ALU.add).then_inc(S["row_used"], 1)
                v.tensor_copy(z_token[:, q, :], g_rows[:, q, D + 1:D + 2].bitcast(I32)).then_inc(S["token_taken"], 1)

            def z_statistics(t):
                r = t.ring(2)
                turn = count_first(dve, t.n + 1)
                dve.wait_ge(S["row_used"], turn)
                v.bn_stats(z_stats[:, r, :], z[:, r, :]).then_inc(S["z_st"], 1)
                turn = count_first(dve, t.n + 1)
                dve.wait_ge(S["z_st"], turn)
                v.bn_aggr(z_mv[:, r, :], z_stats[:, r, :]).then_inc(S["z_agg"], 1)
                dve.wait_ge(S["z_agg"], t.n + 1)
                v.tensor_scalar(z_rstd[:, r, 0:1], z_mv[:, r, 1:2], EPS, None, ALU.add).then_inc(S["z_eps"], 1)

            dve.wait_ge(S["e_ready"], 1)
            dve.wait_ge(S["ffn_in"], 64)
            add_b1(Tile(0))
            add_b1(Tile(1))

            def expert_step(t, static):
                if not static or t.c + 2 < SLOTS:
                    add_b1(t + 2)
                combine(t, static)
                z_statistics(t)

            for n in range(RING):
                expert_step(Tile(n), True)
            n0 = (SLOTS - RING - 2) // RING
            with dve.Fori(0, n0) as i:
                for c in range(RING, 2 * RING):
                    expert_step(Tile(c, i, RING), False)
            for n in range(RING + RING * n0, SLOTS):
                expert_step(Tile(n), True)


def shape_constants():
    c = {}
    p = np.arange(P)
    c["ident"] = np.eye(P)
    ang = (p % T).astype(np.float32)[:, None] * (1.0 / 10000.0 ** (np.arange(0, 4, 2, dtype=np.float32) / 4)).astype(np.float32)[None]
    cos, sin = np.cos(ang), np.sin(ang)
    c["cos8"] = np.concatenate([cos, cos, np.ones((P, 4))], 1)
    c["sin4"] = np.concatenate([-sin, sin], 1)
    c["strip"] = (p[:, None] // 32 == np.arange(STRIPS)[None])
    c["strip_head"] = (p[:, None] // HD % HPS == np.arange(HPS)[None])
    c["head16"] = (p[:, None] // HD == np.arange(H)[None])
    rh = value_rows() // HD
    c["row_head"] = np.arange(P)[:, None] == rh[None]
    c["den_ones"] = np.concatenate([np.arange(32)[None] // 8 == 2 * ab + p[:, None] // T for ab in range(2)], 1)
    c["chan8"] = (p[:, None] % HD == np.arange(8)[None])
    c["batch_rows"] = (p[:, None] % BPT == p[None] // T)
    c["batch_tile"] = (p[:, None] // BPT == p[None] // 8)
    c["tap_of"] = ((p[:, None, None] - np.arange(8)[None, :, None]) % 8 == np.arange(8)[None, None]).reshape(P, 64)
    c["band"] = (p[:, None] // T == p[None] // T) & ((p[:, None] - p[None]) % T < 8)
    c["batch_ind"] = (p[:, None] // T == np.arange(BPT)[None])
    c["rev8"] = np.broadcast_to(8 - np.arange(8)[None], (P, 8))
    c["thresholds"] = np.broadcast_to(P * np.arange(16)[None], (P, 16))
    c["before8"] = np.broadcast_to((np.arange(8)[None] < np.arange(8)[:, None]).reshape(1, 64), (P, 64))
    c["slot_j"] = np.broadcast_to(np.arange(SLOTS)[None], (P, SLOTS))
    c["minus_half"] = np.full((P, 16), -0.5)
    c["causal"] = np.where(np.arange(T)[None] <= (p % T)[:, None], 0.0, -1e30)
    c["earlier"] = p[:, None] < p[None]
    f32 = np.concatenate([c[n].astype(np.float32) for n, _ in CONSTS], 1)
    ids = (P * np.arange(NT)[None] + p[:, None]).astype(np.int32)
    pad = np.zeros(ROW, np.int32)
    pad[D + 1] = NO_TOKEN
    return f32, ids, pad.view(np.float32)


def value_rows():
    r = np.arange(P)
    s, ab, half, d = r // 32, r // 16 % 2, r // 8 % 2, r % 8
    return 64 * ab + 16 * s + 8 * half + d


def kernel(**inputs):
    import concourse.bacc as bacc
    from concourse.bass_utils import run_bass_kernel_spmd

    g = {k: np.asarray(v) for k, v in inputs.items()}
    x = g["x"].reshape(B * T, D)
    L = "L0_attn_"

    def headed(geo, sem):
        return np.concatenate([geo.reshape(-1, H, 4), sem.reshape(-1, H, 4)], 2).reshape(-1, P)

    def swapped(geo):
        return geo.reshape(-1, H, 2, 2)[:, :, ::-1].reshape(-1, H * 4)

    f32, ids, pad = shape_constants()
    A = "L0_xattn_"
    M = "L0_ffn_"
    knull = headed(g[L + "k_geo_null"][None], g[L + "k_sem_null"][None])[0]
    arrays = {
        "consts": f32, "token_ids": ids, "pad_row": pad,
        "x": x, "xT": x.T, "ctx": g["ctx_1024"].reshape(B * T, D),
        "wqk": np.concatenate([headed(g[L + "wq_geo"], g[L + "wq_sem"]), headed(g[L + "wk_geo"], g[L + "wk_sem"]),
                               swapped(g[L + "wq_geo"]), swapped(g[L + "wk_geo"])], 1),
        "wv": g[L + "wv"], "wo": g[L + "wo"][value_rows()], "v_null": g[L + "v_null"][value_rows()],
        "cols": np.stack([knull, g[A + "bq"], g[A + "bk"], g[A + "bv"]], 1),
        "xattn_w": np.stack([g[A + "Wq"].T, g[A + "Wk"].T, g[A + "Wv"], g[A + "Wo"].T], 1),
        "bo": g[A + "bo"], "wr": g[M + "Wr"], "br": g[M + "br"],
        "w1": g[M + "W1"].transpose(1, 0, 2).reshape(P, E * F),
        "w2": g[M + "W2"].reshape(E, FC, P, D).transpose(2, 0, 1, 3).reshape(P, E * FC * D),
        "b1": g[M + "b1"].reshape(-1), "b2": g[M + "b2"].reshape(-1),
    }
    nc = bacc.Bacc("TRN2", target_bir_lowering=False, num_devices=1)
    arrays = {k: np.ascontiguousarray(v) for k, v in arrays.items()}
    aps = {k: nc.dram_tensor("in_" + k, v.shape, mybir.dt.from_np(v.dtype), kind="ExternalInput").ap() for k, v in arrays.items()}
    out = nc.dram_tensor("out_0", (B * T, D), F32, kind="ExternalOutput").ap()
    decoder_layer(nc, aps, out)
    r = run_bass_kernel_spmd(nc, [{"in_" + k: v for k, v in arrays.items()}], core_ids=[0])
    return r.results[0]["out_0"].reshape(B, T, D)
```

```python
from contextlib import ExitStack

import numpy as np
import concourse.bass as bass
from concourse import mybir

ALU = mybir.AluOpType
ACT = mybir.ActivationFunctionType
AX = mybir.AxisListType
F32 = mybir.dt.float32
BF16 = mybir.dt.bfloat16
I32 = mybir.dt.int32
U32 = mybir.dt.uint32

P = 128
B, T, D = 32, 64, 128
H, HD = 16, 8
E, F = 8, 512
NT = B * T // P
BPT = P // T
EPS = 1e-5
STRIPS, HPS = 4, 4
FC = F // P
SLOTS = (NT * P + E * (P - 1)) // P
REGION = NT * P + P
ROW = D + 2
NO_TOKEN = 1 << 20
SCALE = 0.5
RING = 6
GROUPS = NT // 4
PAIR = 2 * (HD + 1)

CONSTS = [("ident", 128), ("cos8", 8), ("sin4", 4), ("strip", 4), ("strip_head", 4), ("head16", 16), ("causal", T),
          ("same_pos", T), ("chan8", 8), ("batch_rows", 128), ("batch_tile", 128), ("tap_of", 64),
          ("band", 128), ("batch_ind", 2), ("rev8", 8), ("thresholds", 16), ("upto8", 64), ("region_at", E), ("slot_row", SLOTS),
          ("slot_j", SLOTS), ("minus_half", 16), ("earlier", P)]
COL, _at = {}, 0
for _n, _w in CONSTS:
    COL[_n] = (_at, _at + _w)
    _at += _w
NCONST = _at
FIRST_CONSTS = COL["chan8"][0]


class Tile:

    def __init__(self, c, i=None, U=1):
        self.c, self.i, self.U = c, i, U
        self.n = c if i is None else i * U + c

    def __add__(self, k):
        return Tile(self.c + k, self.i, self.U)

    def ring(self, size):
        return self.c % size

    def turn(self, size):
        return self.c // size if self.i is None else self.i * (self.U // size) + self.c // size


def run_steps(eng, step, total, U, tail):
    looped = (total - tail) // U
    with eng.Fori(0, looped) as i:
        for c in range(U):
            step(Tile(c, i, U), False)
    for n in range(looped * U, total):
        step(Tile(n), True)


def decoder_layer(nc, a, out):
    with ExitStack() as ctx:
        def sb(name, shape, dt=F32):
            return ctx.enter_context(nc.sbuf_tensor(name, shape, dt))

        def sem(name):
            return ctx.enter_context(nc.semaphore(name))

        rows_dram = nc.dram_tensor("token_rows", (E * REGION + P, ROW), F32, kind="Internal").ap()
        ps = ctx.enter_context(nc.psum_tensor("ps", [P, 8, 512], F32))
        consts = sb("consts", [P, NCONST])
        cb = sb("cb", [P, 2 * P], BF16)
        wqk, wv, wo = sb("wqk", [P, 256]), sb("wv", [P, P]), sb("wo", [P, P])
        xattn_w = sb("xattn_w", [P, 4, P])
        cols = sb("cols", [P, 4])
        vnull_bc, bo_bc = sb("vnull_bc", [16, P]), sb("bo_bc", [P, P])
        wr, br_bc = sb("wr", [P, E]), sb("br_bc", [P, E])
        w1, w2 = sb("w1", [P, E * F]), sb("w2", [P, E * FC * D])
        b1_bc, b2_bc = sb("b1_bc", [P, E * F]), sb("b2_bc", [P, E * D])
        x_all, ctxT = sb("x_all", [P, NT, D]), sb("ctxT", [P, B * T])
        pad_row = sb("pad_row", [P, ROW])
        token_ids = sb("token_ids", [P, NT], I32)

        def const(name, parts=P):
            lo, hi = COL[name]
            return consts[0:parts, lo:hi]

        ident = const("ident")
        tri_b, ones_b = cb[:, 0:P], cb[:, P:2 * P]

        knull, vnull = sb("knull", [P, H]), sb("vnull", [H, H * (HD + 1)])
        bv_bc, wvo, bvo = sb("bv_bc", [P, P]), sb("wvo", [P, P]), sb("bvo", [P, P])
        xT = sb("xT", [P, 4, P])
        roped, rope_b = sb("roped", [P, 2, 256]), sb("rope_b", [P, 2, 128])
        qkT, q_strips, k4 = sb("qkT", [P, 2, 2 * P]), sb("q_strips", [P, 2, STRIPS, P]), sb("k4", [P, 2, 2, BPT, HPS, T])
        v_blocks = sb("v_blocks", [P, 4, BPT * 8 * PAIR])
        null_s = sb("null_s", [P, 2, H])
        row_max, row_max2 = sb("row_max", [P, 2, H]), sb("row_max2", [P, 2, H])
        probs = sb("probs", [P, 2, H * T + H])
        probsT, nullT = sb("probsT", [P, 2, 8, P]), sb("nullT", [16, 2, P])
        rden, attn, attnT = sb("rden", [P, 2, H]), sb("attn", [P, 2, P]), sb("attnT", [P, 2, P])
        y_all, y2_all = sb("y_all", [P, NT, D]), sb("y2_all", [P, NT, D])
        stats, mv, mv2 = sb("stats", [P, NT, 6]), sb("mv", [P, NT, 2]), sb("mv2", [P, NT, 2])
        stats2 = sb("stats2", [P, NT, 6])
        var_eps, rstd = sb("var_eps", [P, 2, NT]), sb("rstd", [P, 2, NT])
        sumT, sqk = sb("sumT", [P, 2, B]), sb("sqk", [P, 3, B])
        wsm = sb("wsm", [B, 4, 8])
        wcol = sb("wcol", [B, 4])
        w_tiles, w_tok = sb("w_tiles", [B, P]), sb("w_tok", [P, P])
        w_taps, w_perm = sb("w_taps", [P, NT * 64]), sb("w_perm", [P, P])
        circ, cw = sb("circ", [P, NT, P]), sb("cw", [P, NT, D])
        x2T = sb("x2T", [P, NT, P])
        rows = sb("rows", [P, NT, ROW])
        lg, lmax, lex = sb("lg", [P, NT, E]), sb("lmax", [P, NT]), sb("lex", [P, NT, E])
        lsum, eqr, first, onehot = sb("lsum", [P, NT]), sb("eqr", [P, NT, E]), sb("first", [P, NT]), sb("onehot", [P, NT, E], BF16)
        slot_f, slot_a, slots = sb("slot_f", [P, NT, E]), sb("slot_a", [P, NT]), sb("slots", [P, NT], U32)
        cnt, over, ntile = sb("cnt", [P, E]), sb("over", [P, E, 16]), sb("ntile", [P, E])
        cnt_i, tmp64, end_t = sb("cnt_i", [P, E], I32), sb("tmp64", [P, E, E]), sb("end_t", [P, E])
        jump, jumps, row_f, row_at = sb("jump", [P, E]), sb("jumps", [P, SLOTS, E]), sb("row_f", [P, SLOTS]), sb("row_at", [P, SLOTS], I32)
        ge = sb("ge", [P, SLOTS, E])
        e_f, e_i = sb("e_f", [P, SLOTS]), sb("e_i", [P, SLOTS], I32)
        gelu_first = sb("gelu_first", [P, 1])
        g_rows = sb("g_rows", [P, RING, ROW])
        z_token = sb("z_token", [P, RING, 1], I32)
        gxT, hid, gel, gelT = sb("gxT", [P, 2, P]), sb("hid", [P, 2, F]), sb("gel", [P, 2, F]), sb("gelT", [P, 2, F])
        z, z_stats, z_mv, z_rstd = sb("z", [P, 2, D]), sb("z_stats", [P, 2, 6]), sb("z_mv", [P, 2, 2]), sb("z_rstd", [P, 2, 2])
        z_out = sb("z_out", [P, RING, D])

        S = {name: sem(name) for name in """
            wqk_in consts_in late_consts_in router_in weights_in attn_in x_in0 x_in1 x_in2 x_in3 x_all_in ctxT_in
            ffn_in ids_in pad_row_in mask_ready blocks_clear blocks_zero knull_ready vnull_ready bv_ready
            wvo_ready bvo_done bvo_ready proj_done rope_b_done rope_done v_done qkT_ready null_taken k4_ready
            v_ready null_done exp0 exp1 scored0 scored1 used0 used1 max_a0 max_a1 max0 max1 probsT_done0
            probsT_done1 probsT_ready attn_done attn_r attn_ready attnT_done attnT_ready wo_done wo_used
            y_all_ready agg_ready eps_ready rstd_ready x1_ready sums_ready sumT_ready sqk_done sk_ready sq_ready
            prod_ready mean_done m_max m_sub m_exp m_sum m_rec w_ready wt_ready wtok_done wtok_ready wtaps
            wperm_ready cw_done cw_ready circ_ready circ_rest_ready mix_done y2_ready y2_stats agg2_ready
            eps2_ready rstd2_ready x2_ready x2T_done x2T_ready logits_done lg_ready lmax_ready ld_ready lex_ready
            lsum_ready gate_ready eq_ready eqr_ready first_ready onehot_ready ranks_done counts_done slot1 slot2
            slot3 slots_ready cnt_ready row_at_ready empties_in route scattered scattered_last ef_ready e_ready
            gathered0 gathered1 gathered2 gathered3 gathered4 gathered5 token_taken gxT_done gxT_ready up_done
            hid_ready gel_ready gelT_done gelT_ready down_done z_a z_st z_agg z_eps z_rs z_ready row_used out_st0
            out_st1 out_st2 out_st3 out_st4 out_st5
        """.split()}

        x_in = [S[f"x_in{r}"] for r in range(4)]

        def count_first(eng, *values):
            values = [v if isinstance(v, int) else eng.to_reg(v) for v in values]
            eng.wait_ge(S["consts_in"], 16)
            return values if len(values) > 1 else values[0]

        class Experts:

            def __init__(self, eng):
                self.eng = eng
                self.regs = [eng.alloc_register(f"expert{r}") for r in range(RING)]

            def load(self, t):
                self.eng.reg_load(self.regs[t.ring(RING)], e_i[0:1, bass.ds(t.n, 1)])

            def of(self, t):
                return nc.snap(self.regs[t.ring(RING)], min_val=0, max_val=E - 1)

        def circulants(engine, g):
            shape = [P, 4, 16, 8]
            engine.tensor_tensor(circ[:, 4 * g:4 * g + 4, :].rearrange("p t (a r) -> p t a r", r=8),
                                 const("band").rearrange("p (a r) -> p a r", r=8).unsqueeze(1).to_broadcast(shape),
                                 w_perm[:, :].rearrange("p (t r) -> p t r", r=8)[:, 4 * g:4 * g + 4, :].unsqueeze(2).to_broadcast(shape),
                                 ALU.mult).then_inc(S["circ_ready" if g == 0 else "circ_rest_ready"], 1)

        def add_empties(eng, experts_here):
            eng.wait_ge(S["cnt_ready"], 1)
            for e in experts_here:
                count = eng.value_load(cnt_i[0:1, e:e + 1], min_val=0, max_val=NT * P)
                eng.dma_start(rows_dram[bass.ds(count + e * REGION, P), :], pad_row[:, :]).then_inc(S["empties_in"], 16)

        scored, used, max_a, maxed, exped = ([S[f"{k}{half}"] for half in range(2)] for k in ("scored", "used", "max_a", "max", "exp"))
        probsT_done = [S["probsT_done0"], S["probsT_done1"]]
        gathered = [S[f"gathered{r}"] for r in range(RING)]
        stored = [S[f"out_st{r}"] for r in range(RING)]

        scores_ps = [ps[:, half, :].rearrange("p (h k) -> p h k", k=T) for half in range(2)]
        nullT_ps, wo_ps = ps[0:16, 2, 0:P], ps[:, 2, 128:256]
        probsT_ps = [ps[:, 4 + half, :] for half in range(2)]
        attn_ps, attnT_ps = ps[:, 6, 0:H * (HD + 1)], ps[:, 6, 256:384]
        proj_ps, null_ps = ps[:, 3, 0:256], ps[:, 3, 256:256 + H]
        qkT_ps, v_ps = ps[:, 7, 0:256], ps[:, 7, 256:512]

        block = ctx.enter_context(nc.Block())

        @block.sync
        def _(sp):
            def load_x(t):
                if t.i is not None or t.c >= 4:
                    sp.wait_ge(S["v_done"], t.n - 3)
                sp.dma_start(xT[:, t.ring(4), :], a["xT"][:, bass.ds(t.n * P, P)]).then_inc(x_in[t.ring(4)], 16)

            sp.dma_start(wqk[:, :], a["wqk"]).then_inc(S["wqk_in"], 16)
            load_x(Tile(0))
            sp.dma_start(consts[:, 0:FIRST_CONSTS], a["consts"][:, 0:FIRST_CONSTS]).then_inc(S["consts_in"], 16)
            sp.dma_start(wv[:, :], a["wv"]).then_inc(S["attn_in"], 16)
            load_x(Tile(1))
            sp.dma_start(cols[:, :], a["cols"]).then_inc(S["attn_in"], 16)
            sp.dma_start(vnull_bc[:, :], a["v_null"].partition_broadcast(16)).then_inc(S["attn_in"], 16)
            load_x(Tile(2))
            sp.dma_start(wo[:, :], a["wo"]).then_inc(S["attn_in"], 16)
            load_x(Tile(3))
            sp.dma_start(xattn_w[:, :, :], a["xattn_w"]).then_inc(S["weights_in"], 16)
            sp.dma_start(bo_bc[:, :], a["bo"].partition_broadcast(P)).then_inc(S["weights_in"], 16)
            sp.dma_start(ctxT[:, :], a["ctxT"]).then_inc(S["ctxT_in"], 16)
            sp.dma_start(x_all[:, :, :], a["x"].rearrange("(t p) d -> p t d", p=P)).then_inc(S["x_all_in"], 16)
            sp.dma_start(consts[:, FIRST_CONSTS:], a["consts"][:, FIRST_CONSTS:]).then_inc(S["late_consts_in"], 16)
            sp.dma_start(wr[:, :], a["wr"]).then_inc(S["router_in"], 16)
            sp.dma_start(br_bc[:, :], a["br"].partition_broadcast(P)).then_inc(S["router_in"], 16)
            sp.dma_start(token_ids[:, :], a["token_ids"]).then_inc(S["ids_in"], 16)
            sp.dma_start(pad_row[:, :], a["pad_row"].partition_broadcast(P)).then_inc(S["pad_row_in"], 16)
            sp.wait_ge(S["pad_row_in"], 16)
            sp.dma_start(rows_dram[E * REGION:, :], pad_row[:, :]).then_inc(S["empties_in"], 16)
            with sp.Fori(0, NT // 4 - 1) as i:
                for c in range(4, 8):
                    load_x(Tile(c, i, 4))

            sp.dma_start(w1[:, :], a["w1"]).then_inc(S["ffn_in"], 16)
            sp.dma_start(w2[:, :], a["w2"]).then_inc(S["ffn_in"], 16)
            sp.dma_start(b1_bc[:, :], a["b1"].partition_broadcast(P)).then_inc(S["ffn_in"], 16)
            sp.dma_start(b2_bc[:, :], a["b2"].partition_broadcast(P)).then_inc(S["ffn_in"], 16)

            def load_rows(t, static, row=None):
                r = t.ring(RING)
                row = sp.value_load(row_at[0:1, bass.ds(t.n, 1)], min_val=0, max_val=E * REGION) if row is None else row
                if not static or t.c >= RING:
                    sp.wait_ge(S["token_taken"], t.n - (RING - 1))
                sp.dma_start(g_rows[:, r, :], rows_dram[bass.ds(row, P), :]).then_inc(gathered[r], 16)

            add_empties(sp, range(E // 2))
            sp.wait_ge(S["row_at_ready"], 1)
            first_rows = [sp.value_load(row_at[0:1, n:n + 1], min_val=0, max_val=E * REGION) for n in range(RING)]
            sp.wait_ge(S["empties_in"], 16 * (E + 1))
            sp.wait_ge(S["scattered"], 16 * (NT - 4))
            sp.wait_ge(S["scattered_last"], 16 * 4)
            for n in range(RING):
                load_rows(Tile(n), True, first_rows[n])
            n0 = (SLOTS - RING) // RING
            with sp.Fori(0, n0) as i:
                for c in range(RING, 2 * RING):
                    load_rows(Tile(c, i, RING), False)
            for n in range(RING + RING * n0, SLOTS):
                load_rows(Tile(n), True)

        @block.gpsimd
        def _(pool):
            def rope_add(t):
                turn, blocks = count_first(pool, t.n + 1, t.n * 4)
                pool.wait_ge(S["rope_b_done"], turn)
                if t.i is not None or t.c >= 2:
                    pool.wait_ge(S["k4_ready"], blocks)
                r = t.ring(2)
                ra = roped[:, r, :].rearrange("p (h c) -> p h c", c=HD)[:, :, 0:4]
                nc.gpsimd.tensor_tensor(ra, ra, rope_b[:, r, :].rearrange("p (h c) -> p h c", c=4), ALU.add).then_inc(S["rope_done"], 1)

            def qk_blocks(t):
                turn = count_first(pool, t.n + 1)
                pool.wait_ge(S["qkT_ready"], turn)
                pool.wait_ge(S["rope_done"], 2 if t.i is None and t.c == 0 else turn)
                r = t.ring(2)
                for half in range(2):
                    rows_h = slice(64 * half, 64 * half + 64)
                    strips = slice(2 * half, 2 * half + 2)
                    nc.gpsimd.tensor_tensor(q_strips[rows_h, r, strips, :], qkT[rows_h, r, 0:P].unsqueeze(1).to_broadcast([64, 2, P]),
                                            const("strip")[rows_h, strips].unsqueeze(2).to_broadcast([64, 2, P]), ALU.mult).then_inc(S["k4_ready"], 1)
                    src = qkT[rows_h, r, P:2 * P].rearrange("p (b k) -> p b k", b=BPT).unsqueeze(2).to_broadcast([64, BPT, HPS, T])
                    m = const("strip_head")[rows_h, :].unsqueeze(1).unsqueeze(3).to_broadcast([64, BPT, HPS, T])
                    nc.gpsimd.tensor_tensor(k4[rows_h, r, half, :, :, :], src, m, ALU.mult).then_inc(S["k4_ready"], 1)

            rope_add(Tile(0))
            rope_add(Tile(1))
            pool.wait_ge(S["mask_ready"], 1)
            qk_blocks(Tile(0))
            qk_blocks(Tile(1))
            rope_add(Tile(2))
            qk_blocks(Tile(2))
            rope_add(Tile(3))

            def attn_step(t, static):
                qk_blocks(t + 3)
                if not static or t.c + 4 < NT:
                    rope_add(t + 4)

            run_steps(pool, attn_step, NT - 3, 4, 1)

            def inverse_std(k, mean_var, g, ready, eps_done, done):
                tiles = slice(4 * g, 4 * g + 4)
                pool.wait_ge(S[ready], 4 * g + 4)
                nc.gpsimd.tensor_scalar(var_eps[:, k, tiles], mean_var[:, tiles, 1], EPS, None, ALU.add).then_inc(S[eps_done], 1)
                pool.wait_ge(S[eps_done], g + 1)
                nc.gpsimd.tensor_tensor(rstd[:, k, tiles], var_eps[:, k, tiles], const("minus_half")[:, tiles], ALU.pow).then_inc(S[done], 1)

            pool.wait_ge(S["k4_ready"], 4 * NT)
            pool.wait_ge(S["ids_in"], 16)
            nc.gpsimd.tensor_copy(rows[:, :, D + 1:D + 2].bitcast(I32).squeeze(2), token_ids[:, :])
            pool.wait_ge(S["late_consts_in"], 16)
            for g in range(GROUPS):
                inverse_std(0, mv, g, "agg_ready", "eps_ready", "rstd_ready")
            pool.wait_ge(S["wperm_ready"], 1)
            circulants(nc.gpsimd, 1)
            pool.wait_ge(S["wperm_ready"], 2)
            circulants(nc.gpsimd, 2)
            circulants(nc.gpsimd, 3)
            for g in range(GROUPS - 1):
                inverse_std(1, mv2, g, "agg2_ready", "eps2_ready", "rstd2_ready")

            for g in range(GROUPS):
                if g == 1:
                    inverse_std(1, mv2, GROUPS - 1, "agg2_ready", "eps2_ready", "rstd2_ready")
                pool.wait_ge(S["slots_ready"], g + 1)
                pool.wait_ge(S["gate_ready"], g + 1)
                for t in range(4 * g, 4 * g + 4):
                    pool.indirect_dma_start(out=rows_dram, out_offset=bass.IndirectOffsetOnAxis(ap=slots[:, t:t + 1], axis=0),
                                            in_=rows[:, t, :], in_offset=None, bounds_check=E * REGION - 1,
                                            oob_is_err=False).then_inc(S["scattered" if g < GROUPS - 1 else "scattered_last"], 16)

            def deviation(t):
                r = t.ring(2)
                turn = count_first(pool, t.n + 1)
                pool.wait_ge(S["z_agg"], turn)
                nc.gpsimd.tensor_scalar(z_rstd[:, r, 0:1], z_mv[:, r, 1:2], EPS, None, ALU.add).then_inc(S["z_eps"], 1)
                pool.wait_ge(S["z_eps"], t.n + 1)
                nc.gpsimd.tensor_tensor(z_rstd[:, r, 1:2], z_rstd[:, r, 0:1], const("minus_half")[:, 0:1], ALU.pow).then_inc(S["z_rs"], 1)

            def store(t):
                q = t.ring(RING)
                turn = count_first(pool, t.n + 1)
                pool.wait_ge(S["z_ready"], turn)
                pool.indirect_dma_start(out=out, out_offset=bass.IndirectOffsetOnAxis(ap=z_token[:, q, :].bitcast(U32), axis=0),
                                        in_=z_out[:, q, :], in_offset=None, bounds_check=NT * P - 1,
                                        oob_is_err=False).then_inc(stored[q], 16)

            deviation(Tile(0))

            def finish_tile(t, static):
                deviation(t + 1)
                store(t)

            run_steps(pool, finish_tile, SLOTS - 1, RING, 0)
            store(Tile(SLOTS - 1))
            for r in range(RING):
                pool.wait_ge(stored[r], 16 * ((SLOTS - 1 - r) // RING + 1))

        @block.tensor
        def _(pe):
            def project(t):
                pe.wait_ge(x_in[t.ring(4)], (t.turn(4) + 1) * 16)
                if t.i is not None or t.c >= 2:
                    pe.wait_ge(S["null_taken"], 1 if t.i is None and t.c == 2 else t.n - 2)
                nc.tensor.matmul(proj_ps, xT[:, t.ring(4), :], wqk[:, :], start=True, stop=True).then_inc(S["proj_done"], 1)

            def turn_qk(t):
                r = t.ring(2)
                pe.wait_ge(S["rope_done"], t.n + 1)
                if t.i is not None or t.c >= 1:
                    pe.wait_ge(S["v_ready"], t.n)
                nc.tensor.transpose(qkT_ps[:, 0:128], roped[:, r, 0:128], ident)
                nc.tensor.transpose(qkT_ps[:, 128:256], roped[:, r, 128:256], ident)
                for b in range(BPT):
                    for half in range(2):
                        last = nc.tensor.matmul(v_ps[64 * half:64 * half + 64, b * P:(b + 1) * P], xT[:, t.ring(4), b * T:(b + 1) * T],
                                                wv[:, :], start=True, stop=True)
                last.then_inc(S["v_done"], 1)

            def scores(t, half):
                r = t.ring(2)
                if half == 0:
                    pe.wait_ge(S["k4_ready"], (t + 1).n * 4)
                if t.i is not None or t.c >= 1:
                    pe.wait_ge(used[half], t.n)
                for s in range(2):
                    for b in range(BPT):
                        last = nc.tensor.matmul(ps[b * T:(b + 1) * T, half, 256 * s:256 * s + 256],
                                                q_strips[:, r, 2 * half + s, b * T:(b + 1) * T],
                                                k4[:, r, half, b, :, :], start=True, stop=True)
                last.then_inc(scored[half], 1)
                if half == 0:
                    pe.wait_ge(S["rope_b_done"], t.n + 3 if t.i is not None else 2 if t.c == 0 else min(t.c + 3, NT))
                    nc.tensor.matmul(null_ps, qkT[:, r, 0:P], knull[:, :], start=True, stop=True).then_inc(S["null_done"], 1)

            def turn_probs(t, half):
                r = t.ring(2)
                pe.wait_ge(exped[half], t.n + 1)
                if half == 0 and (t.i is not None or t.c >= 1):
                    pe.wait_ge(S["probsT_ready"], t.n)
                for c in range(4 * half, 4 * half + 4):
                    last = nc.tensor.transpose(probsT_ps[half][:, (c % 4) * P:(c % 4 + 1) * P], probs[:, r, c * P:(c + 1) * P], ident)
                if half == 1:
                    if t.i is not None or t.c >= 3:
                        pe.wait_ge(S["wo_used"], t.n - 2)
                    last = nc.tensor.transpose(nullT_ps, probs[:, r, H * T:H * T + H], ident)
                last.then_inc(probsT_done[half], 1)

            def mix_values(t):
                r = t.ring(2)
                pe.wait_ge(S["probsT_ready"], t.n + 1)
                pe.wait_ge(S["v_ready"], t.n + 1)
                if t.i is not None or t.c >= 1:
                    pe.wait_ge(S["attnT_ready"], t.n)
                nc.tensor.matmul(attn_ps, nullT[:, r, :], vnull[:, :], start=True, stop=False, skip_group_check=True)
                for c in range(8):
                    for b in range(BPT):
                        at = PAIR * (8 * b + c)
                        last = nc.tensor.matmul(ps[b * T:(b + 1) * T, 6, PAIR * c:PAIR * (c + 1)], probsT[:, r, c, b * T:(b + 1) * T],
                                                v_blocks[:, t.ring(4), at:at + PAIR], start=False, stop=True, skip_group_check=True)
                last.then_inc(S["attn_done"], 1)

            def turn_attn(t):
                pe.wait_ge(S["attn_ready"], t.n + 1)
                nc.tensor.transpose(attnT_ps, attn[:, t.ring(2), :], ident).then_inc(S["attnT_done"], 1)

            def project_out(t, read):
                pe.wait_ge(S["attnT_ready"], t.n + 1)
                pe.wait_ge(S["probsT_ready"], read.n + 1)
                nc.tensor.matmul(wo_ps, attnT[:, t.ring(2), :], wo[:, :], start=True, stop=True).then_inc(S["wo_done"], 1)

            def context_weights():
                pe.wait_ge(S["weights_in"], 32)
                nc.tensor.matmul(ps[:, 6, 0:128], xattn_w[:, 2, :], xattn_w[:, 3, :], start=True, stop=True)
                pe.wait_ge(S["bv_ready"], 1)
                nc.tensor.matmul(ps[:, 6, 128:256], bv_bc[:, :], xattn_w[:, 3, :], start=True, stop=True).then_inc(S["bvo_done"], 1)

            def context(g):
                bank = 6 if g == 1 else 4 + g
                if g == 0:
                    pe.wait_ge(S["ctxT_in"], 16)
                    pe.wait_ge(S["wvo_ready"], 1)
                    pe.wait_ge(S["bvo_ready"], 1)
                nc.tensor.matmul(ps[:, bank, :], ident, bvo[:, :].unsqueeze(1).to_broadcast([P, 4, P]), start=True, stop=False, skip_group_check=True)
                for c in range(4):
                    t = 4 * g + c
                    last = nc.tensor.matmul(ps[:, bank, c * P:(c + 1) * P], ctxT[:, t * P:(t + 1) * P], wvo[:, :],
                                            start=False, stop=True, skip_group_check=True)
                last.then_inc(S["cw_done"], 1)

            pe.wait_ge(S["wqk_in"], 16)
            project(Tile(0))
            pe.wait_ge(S["consts_in"], 16)
            pe.wait_ge(S["attn_in"], 16 * 4)
            turn_qk(Tile(0))
            project(Tile(1))
            context_weights()
            turn_qk(Tile(1))
            pe.wait_ge(S["knull_ready"], 1)
            scores(Tile(0), 0)
            scores(Tile(0), 1)
            project(Tile(2))
            context(0)
            turn_qk(Tile(2))
            project(Tile(3))
            pe.wait_ge(S["vnull_ready"], 1)
            pe.wait_ge(S["cw_ready"], 1)

            def attn_step(t, static):
                if not static or t.c + 1 < NT:
                    scores(t + 1, 0)
                if not static or t.c >= 2:
                    turn_attn(t + -2)
                turn_probs(t, 0)
                if not static or t.c + 1 < NT:
                    scores(t + 1, 1)
                turn_probs(t, 1)
                if not static or t.c >= 1:
                    mix_values(t + -1)
                if not static or t.c + 3 < NT:
                    turn_qk(t + 3)
                if not static or t.c >= 2:
                    project_out(t + -2, t)
                if not static or t.c + 4 < NT:
                    project(t + 4)

            for n in range(4):
                attn_step(Tile(n), True)
                if n == 0:
                    context(1)
                    pe.wait_ge(S["cw_ready"], 2)
            with pe.Fori(0, (NT - 8) // 4) as i:
                for c in range(4, 8):
                    attn_step(Tile(c, i, 4), False)
            for n in range(NT - 4, NT):
                attn_step(Tile(n), True)
            def sums(g):
                for t in range(4 * g, 4 * g + 4):
                    pe.wait_ge(S["x1_ready"], t + 1)
                    last = nc.tensor.matmul(ps[:, 0, BPT * t:BPT * (t + 1)], y_all[:, t, :], const("batch_ind"), start=True, stop=True)
                last.then_inc(S["sums_ready"], 1)

            pe.wait_ge(S["late_consts_in"], 16)
            turn_attn(Tile(NT - 2))
            mix_values(Tile(NT - 1))
            pe.wait_ge(S["wo_used"], NT - 2)
            project_out(Tile(NT - 2), Tile(NT - 1))
            sums(0)
            turn_attn(Tile(NT - 1))
            pe.wait_ge(S["wo_used"], NT - 1)
            project_out(Tile(NT - 1), Tile(NT - 1))
            for g in range(1, GROUPS):
                sums(g)
            pe.wait_ge(S["sumT_ready"], 1)
            nc.tensor.matmul(ps[:, 2, 0:B], xattn_w[:, 1, :], sumT[:, 0, :], start=True, stop=True)
            nc.tensor.matmul(ps[:, 2, B:2 * B], xattn_w[:, 0, :], sumT[:, 1, :], start=True, stop=True).then_inc(S["sqk_done"], 1)
            pe.wait_ge(S["prod_ready"], 1)
            nc.tensor.matmul(ps[0:B, 3, 0:8], sqk[:, 2, :], const("chan8"), start=True, stop=True).then_inc(S["mean_done"], 1)
            pe.wait_ge(S["wt_ready"], 1)
            nc.tensor.matmul(ps[:, 3, 128:256], const("batch_rows", B), w_tiles[:, :], start=True, stop=True).then_inc(S["wtok_done"], 1)
            context(2)

            for g in range(GROUPS):
                if g == 2:
                    context(3)
                pe.wait_ge(S["cw_ready"], g + 1)
                if g == 0:
                    pe.wait_ge(S["circ_ready"], 1)
                else:
                    pe.wait_ge(S["circ_rest_ready"], g)
                for c in range(4):
                    t = 4 * g + c
                    last = nc.tensor.matmul(ps[:, 4 + g, c * P:(c + 1) * P], circ[:, t, :], cw[:, t, :], start=True, stop=True)
                last.then_inc(S["mix_done"], 1)

            def turn_x2(g):
                for c in range(4):
                    pe.wait_ge(S["x2_ready"], 4 * g + c + 1)
                    last = nc.tensor.transpose(ps[:, 4 + g, c * P:(c + 1) * P], rows[:, 4 * g + c, 0:D], ident)
                last.then_inc(S["x2T_done"], 1)

            def router(g):
                pe.wait_ge(S["x2T_ready"], g + 1)
                for c in range(4):
                    last = nc.tensor.matmul(ps[:, g, c * E:(c + 1) * E], x2T[:, 4 * g + c, :], wr[:, :], start=True, stop=True)
                last.then_inc(S["logits_done"], 1)

            def ranks(g):
                pe.wait_ge(S["onehot_ready"], g + 1)
                ranks_ps = ps[:, g, 64:64 + 4 * E]
                oh = onehot[:, 4 * g:4 * g + 4, :].rearrange("p t e -> p (t e)")
                last = nc.tensor.matmul(ranks_ps, tri_b, oh, start=True, stop=False, skip_group_check=True)
                for s in range(1, 4):
                    last = nc.tensor.matmul(ranks_ps[:, E * s:], ones_b, oh[:, 0:E * (4 - s)], start=False, stop=True, skip_group_check=True)
                for t in range(4 * g):
                    last = nc.tensor.matmul(ranks_ps, ones_b, onehot[:, t:t + 1, :].to_broadcast([P, 4, E]),
                                            start=False, stop=True, skip_group_check=True)
                last.then_inc(S["ranks_done"], 1)

            pe.wait_ge(S["router_in"], 32)
            turn_x2(0)
            router(0)
            turn_x2(1)
            ranks(0)
            router(1)
            for g in range(2, GROUPS):
                turn_x2(g)
                router(g)
                ranks(g - 1)
            ranks(GROUPS - 1)
            pe.wait_ge(S["slots_ready"], 1)
            for t in range(NT):
                last = nc.tensor.matmul(ps[:, 0, 0:E], ones_b, onehot[:, t, :], start=(t == 0), stop=(t == NT - 1))
            last.then_inc(S["counts_done"], 1)

            def gxT_ps(r):
                return ps[:, 4 + r, 0:P]

            def y_ps(r):
                return ps[:, 6 + r, 0:D]

            def turn_rows(t):
                pe.wait_ge(gathered[t.ring(RING)], (t.turn(RING) + 1) * 16)
                nc.tensor.transpose(gxT_ps(t.ring(2)), g_rows[:, t.ring(RING), 0:D], ident).then_inc(S["gxT_done"], 1)

            def up(t):
                r = t.ring(2)
                e = experts.of(t)
                pe.wait_ge(S["gxT_ready"], t.n + 1)
                if t.i is not None or t.c >= 2:
                    pe.wait_ge(S["hid_ready"], t.n - 1)
                nc.tensor.matmul(ps[:, r, :], gxT[:, r, :], w1[:, bass.ds(e * F, F)], start=True, stop=True).then_inc(S["up_done"], 1)
                if t.i is not None or t.c + 1 < SLOTS:
                    experts.load(t + 1)

            def turn_hidden(t):
                r = t.ring(2)
                pe.wait_ge(S["gel_ready"], t.n + 1)
                for c in range(FC):
                    last = nc.tensor.transpose(ps[:, 2 + r, c * P:(c + 1) * P], gel[:, r, c * P:(c + 1) * P], ident)
                last.then_inc(S["gelT_done"], 1)

            def down(t, static):
                r = t.ring(2)
                e = experts.of(t)
                pe.wait_ge(S["gelT_ready"], t.n + 1)
                if not static or t.c >= 2:
                    pe.wait_ge(S["z_a"], t.n - 1)
                for c in range(FC):
                    last = nc.tensor.matmul(y_ps(r), gelT[:, r, c * P:(c + 1) * P], w2[:, bass.ds(e * (FC * D) + c * D, D)],
                                            start=(c == 0), stop=(c == FC - 1))
                last.then_inc(S["down_done"], 1)

            pe.wait_ge(S["e_ready"], 1)
            pe.wait_ge(S["ffn_in"], 64)
            experts = Experts(pe)
            experts.load(Tile(0))
            pe.wait_ge(S["scattered"], 16 * (NT - 4))
            for _ in range(3):
                nc.tensor.matmul(ps[:, 7, :], ident, w1[:, 0:512], start=True, stop=True)
            turn_rows(Tile(0))
            turn_rows(Tile(1))
            up(Tile(0))
            turn_rows(Tile(2))
            up(Tile(1))

            def expert_step(t, static):
                turn_hidden(t)
                if not static or t.c + 2 < SLOTS:
                    up(t + 2)
                if not static or t.c + 3 < SLOTS:
                    turn_rows(t + 3)
                down(t, static)

            expert_step(Tile(0), True)
            expert_step(Tile(1), True)
            n0 = (SLOTS - 2 - 3) // RING
            with pe.Fori(0, n0) as i:
                for c in range(2, 2 + RING):
                    expert_step(Tile(c, i, RING), False)
            for n in range(2 + RING * n0, SLOTS):
                expert_step(Tile(n), True)

        @block.scalar
        def _(act):
            def copy(o, i):
                return nc.scalar.activation(o, i, ACT.Copy)

            def take_probsT(t, half):
                r = t.ring(2)
                act.wait_ge(probsT_done[half], t.n + 1)
                last = copy(probsT[:, r, 4 * half:4 * half + 4, :].rearrange("p a b -> p (a b)"), probsT_ps[half])
                if half == 1:
                    copy(nullT[:, r, :], nullT_ps).then_inc(S["probsT_ready"], 1)

            def take_attnT(t):
                act.wait_ge(S["attnT_done"], t.n + 1)
                copy(attnT[:, t.ring(2), :], attnT_ps).then_inc(S["attnT_ready"], 1)

            def take_qv(t):
                r = t.ring(2)
                act.wait_ge(S["v_done"], t.n + 1)
                copy(qkT[:, r, :], qkT_ps).then_inc(S["qkT_ready"], 1)
                for half in range(2):
                    rows_h = slice(64 * half, 64 * half + 64)
                    dst = v_blocks[rows_h, t.ring(4), :].rearrange("p (g w) -> p g w", w=PAIR)
                    src = v_ps[rows_h, :].rearrange("p (g w) -> p g w", w=2 * HD)
                    last = copy(dst[:, :, half * (HD + 1):half * (HD + 1) + HD], src[:, :, half * HD:half * HD + HD])
                last.then_inc(S["v_ready"], 1)

            def exponent(t, half):
                cols_h = slice(512 * half, 512 * half + 512 + H * half)
                act.wait_ge(used[half], t.n + 1)
                nc.scalar.activation(probs[:, t.ring(2), cols_h], probs[:, t.ring(2), cols_h], ACT.Exp, scale=SCALE).then_inc(exped[half], 1)

            act.wait_ge(S["blocks_zero"], 1)
            def take_group(target, g, bank, done, ready):
                act.wait_ge(S[done], g + 1)
                copy(target[:, 4 * g:4 * g + 4, :].rearrange("p a b -> p (a b)"), ps[:, bank, :]).then_inc(S[ready], 1)

            take_qv(Tile(0))
            take_qv(Tile(1))
            exponent(Tile(0), 0)
            take_group(cw, 0, 4, "cw_done", "cw_ready")
            exponent(Tile(0), 1)
            take_qv(Tile(2))

            def attn_step(t, static):
                if not static or t.c >= 2:
                    take_attnT(t + -2)
                take_probsT(t, 0)
                if not static or t.c + 1 < NT:
                    exponent(t + 1, 0)
                take_probsT(t, 1)
                if not static or t.c + 3 < NT:
                    take_qv(t + 3)
                if not static or t.c + 1 < NT:
                    exponent(t + 1, 1)

            for n in range(4):
                attn_step(Tile(n), True)
                if n == 0:
                    take_group(cw, 1, 6, "cw_done", "cw_ready")
            with act.Fori(0, (NT - 8) // 4) as i:
                for c in range(4, 8):
                    attn_step(Tile(c, i, 4), False)
            for n in range(NT - 4, NT):
                attn_step(Tile(n), True)
            take_attnT(Tile(NT - 2))
            take_attnT(Tile(NT - 1))

            act.wait_ge(S["late_consts_in"], 16)
            act.wait_ge(S["m_sub"], 1)
            nc.scalar.activation(wsm[:, 1, :], wsm[:, 0, :], ACT.Exp).then_inc(S["m_exp"], 1)
            take_group(cw, 2, 6, "cw_done", "cw_ready")
            take_group(cw, 3, 7, "cw_done", "cw_ready")

            def exp_logits(g):
                tiles = slice(4 * g, 4 * g + 4)
                act.wait_ge(S["ld_ready"], g + 1)
                nc.scalar.activation(lex[:, tiles, :], lg[:, tiles, :], ACT.Exp).then_inc(S["lex_ready"], 1)

            take_group(x2T, 0, 4, "x2T_done", "x2T_ready")
            take_group(x2T, 1, 5, "x2T_done", "x2T_ready")
            exp_logits(0)
            take_group(x2T, 2, 6, "x2T_done", "x2T_ready")
            exp_logits(1)
            take_group(x2T, 3, 7, "x2T_done", "x2T_ready")
            exp_logits(2)
            exp_logits(3)
            act.wait_ge(S["pad_row_in"], 16)
            add_empties(act, range(E // 2, E))
            nc.scalar.activation(gelu_first[:, :], const("minus_half")[:, 0:1], ACT.Gelu)

            def take_rows(t):
                act.wait_ge(S["gxT_done"], t.n + 1)
                copy(gxT[:, t.ring(2), :], ps[:, 4 + t.ring(2), 0:P]).then_inc(S["gxT_ready"], 1)

            def gelu(t):
                r = t.ring(2)
                act.wait_ge(S["hid_ready"], t.n + 1)
                nc.scalar.activation(gel[:, r, :], hid[:, r, :], ACT.Gelu).then_inc(S["gel_ready"], 1)

            def take_hidden(t):
                r = t.ring(2)
                act.wait_ge(S["gelT_done"], t.n + 1)
                copy(gelT[:, r, :], ps[:, 2 + r, :]).then_inc(S["gelT_ready"], 1)

            take_rows(Tile(0))
            take_rows(Tile(1))
            take_rows(Tile(2))
            gelu(Tile(0))

            def expert_step(t, static):
                take_hidden(t)
                if not static or t.c + 1 < SLOTS:
                    gelu(t + 1)
                if not static or t.c + 3 < SLOTS:
                    take_rows(t + 3)

            run_steps(act, expert_step, SLOTS, RING, 3)

        @block.vector
        def _(dve):
            v = nc.vector
            route_step = [0]

            def chained(ins, name="route"):
                route_step[0] += 1
                ins.then_inc(S["route"], 1)
                dve.wait_ge(S["route"], route_step[0])

            def rope(t):
                r = t.ring(2)
                dve.wait_ge(S["proj_done"], t.n + 1)
                main = proj_ps[:, 0:256].rearrange("p (h c) -> p h c", c=HD)
                ra = roped[:, r, :].rearrange("p (h c) -> p h c", c=HD)
                rb = rope_b[:, r, :].rearrange("p (h c) -> p h c", c=4)
                v.tensor_tensor(ra, main, const("cos8").unsqueeze(1).to_broadcast([P, 2 * H, HD]), ALU.mult)
                for a in (0, 2):
                    last = v.tensor_tensor(rb[:, :, a:a + 2], main[:, :, 2 - a:4 - a],
                                           const("sin4")[:, a:a + 2].unsqueeze(1).to_broadcast([P, 2 * H, 2]), ALU.mult)
                last.then_inc(S["rope_b_done"], 1)

            def take_null(t):
                dve.wait_ge(S["null_done"], t.n + 1)
                v.tensor_copy(null_s[:, t.ring(2), :], null_ps).then_inc(S["null_taken"], 1)

            def subtract_max(t, half):
                r = t.ring(2)
                heads = slice(8 * half, 8 * half + 8)
                dve.wait_ge(scored[half], t.n + 1)
                v.tensor_reduce(row_max[:, r, heads], scores_ps[half], AX.X, ALU.max).then_inc(max_a[half], 1)
                dve.wait_ge(max_a[half], t.n + 1)
                dve.wait_ge(S["null_taken"], t.n + 1)
                v.tensor_tensor(row_max2[:, r, heads], row_max[:, r, heads], null_s[:, r, heads], ALU.max).then_inc(maxed[half], 1)
                dve.wait_ge(maxed[half], t.n + 1)
                if half == 1:
                    v.tensor_tensor(probs[:, r, H * T:H * T + H], null_s[:, r, :], row_max2[:, r, :], ALU.subtract)
                v.tensor_tensor(probs[:, r, 512 * half:512 * half + 512].rearrange("p (h k) -> p h k", k=T), scores_ps[half],
                                row_max2[:, r, heads].unsqueeze(2).to_broadcast([P, 8, T]), ALU.subtract).then_inc(used[half], 1)

            def normalize(t):
                r = t.ring(2)
                heads = attn_ps.rearrange("p (h w) -> p h w", w=HD + 1)
                dve.wait_ge(S["attn_done"], t.n + 1)
                v.reciprocal(rden[:, r, :], heads[:, :, HD]).then_inc(S["attn_r"], 1)
                dve.wait_ge(S["attn_r"], t.n + 1)
                v.tensor_tensor(attn[:, r, :].rearrange("p (h w) -> p h w", w=HD), heads[:, :, 0:HD],
                                rden[:, r, :].unsqueeze(2).to_broadcast([P, H, HD]), ALU.mult).then_inc(S["attn_ready"], 1)

            def residual(t):
                y = y_all[:, bass.ds(t.n, 1), :].squeeze(1)
                dve.wait_ge(S["wo_done"], t.n + 1)
                v.tensor_tensor(y, wo_ps, x_all[:, bass.ds(t.n, 1), :].squeeze(1), ALU.add).then_inc(S["wo_used"], 1)

            def statistics(t):
                turn = count_first(dve, t.n + 1)
                dve.wait_ge(S["wo_used"], turn)
                v.bn_stats(stats[:, bass.ds(t.n, 1), :].squeeze(1), y_all[:, bass.ds(t.n, 1), :].squeeze(1)).then_inc(S["y_all_ready"], 1)

            v.memset(v_blocks[:, :, :], 0.0).then_inc(S["blocks_clear"], 1)
            dve.wait_ge(S["blocks_clear"], 1)
            for half in range(2):
                ones_at = v_blocks[64 * half:64 * half + 64, :, :].rearrange("p r (g w) -> p (r g) w", w=PAIR)[:, :, half * (HD + 1) + HD]
                last = v.memset(ones_at, 1.0)
            last.then_inc(S["blocks_zero"], 1)
            dve.wait_ge(S["consts_in"], 16)
            dve.wait_ge(S["wqk_in"], 16)
            rope(Tile(0))
            for half in range(2):
                other = slice(64 - 64 * half, 128 - 64 * half)
                v.tensor_copy(k4[other, :, half, :, :, :].rearrange("p r b h k -> p r (b h) k"),
                              const("causal")[other, :].unsqueeze(1).unsqueeze(1).to_broadcast([64, 2, BPT * HPS, T]))
                last = v.tensor_copy(q_strips[other, :, 2 * half:2 * half + 2, :].rearrange("p r s (b k) -> p r (s b) k", k=T),
                                     const("same_pos")[other, :].unsqueeze(1).unsqueeze(1).to_broadcast([64, 2, 2 * BPT, T]))
            last.then_inc(S["mask_ready"], 1)
            rope(Tile(1))
            dve.wait_ge(S["attn_in"], 64)
            v.tensor_scalar(knull[:, :], const("head16"), cols[:, 0:1], None, ALU.mult).then_inc(S["knull_ready"], 1)
            vnull_h = vnull[:, :].rearrange("p (h w) -> p h w", w=HD + 1)
            v.tensor_tensor(vnull_h[:, :, 0:HD], ident[0:H, 0:H].unsqueeze(2).to_broadcast([H, H, HD]),
                            vnull_bc[:, :].rearrange("p (h w) -> p h w", w=HD), ALU.mult)
            v.tensor_copy(vnull_h[:, :, HD], ident[0:H, 0:H]).then_inc(S["vnull_ready"], 1)
            v.tensor_scalar(bv_bc[:, :], ident, 0.0, cols[:, 3:4], ALU.mult, ALU.add).then_inc(S["bv_ready"], 1)
            dve.wait_ge(S["weights_in"], 32)
            dve.wait_ge(S["bvo_done"], 1)
            v.tensor_copy(wvo[:, :], ps[:, 6, 0:128]).then_inc(S["wvo_ready"], 1)
            v.tensor_tensor(bvo[:, :], ps[:, 6, 128:256], bo_bc[:, :], ALU.add).then_inc(S["bvo_ready"], 1)
            take_null(Tile(0))
            subtract_max(Tile(0), 0)
            subtract_max(Tile(0), 1)
            rope(Tile(2))
            dve.wait_ge(S["ctxT_in"], 16)
            v.tensor_reduce(sumT[:, 0, :], ctxT[:, :].rearrange("p (b k) -> p b k", k=T), AX.X, ALU.add)
            dve.wait_ge(S["late_consts_in"], 16)
            v.tensor_copy(tri_b, const("earlier"))
            v.memset(ones_b, 1.0)
            dve.wait_ge(S["x_all_in"], 16)

            def attn_step(t, static):
                if not static or t.c + 3 < NT:
                    rope(t + 3)
                if not static or t.c >= 3:
                    residual(t + -3)
                if not static or t.c + 1 < NT:
                    take_null(t + 1)
                    subtract_max(t + 1, 0)
                    subtract_max(t + 1, 1)
                if not static or t.c >= 3:
                    statistics(t + -3)
                if not static or t.c >= 1:
                    normalize(t + -1)

            for n in range(4):
                attn_step(Tile(n), True)
            with dve.Fori(0, (NT - 8) // 4) as i:
                for c in range(4, 8):
                    attn_step(Tile(c, i, 4), False)

            def aggregate(st, mean_var, g, ready, done):
                dve.wait_ge(S[ready], 4 * g + 4)
                for t in range(4 * g, 4 * g + 4):
                    v.bn_aggr(mean_var[:, t, :], st[:, t, :]).then_inc(S[done], 1)

            def normalized(k, mean_var, source, target, t, done):
                v.tensor_scalar(target, source[:, t, :], mean_var[:, t, 0:1], rstd[:, k, t:t + 1],
                                ALU.subtract, ALU.mult).then_inc(S[done], 1)

            def first_norm(g):
                dve.wait_ge(S["rstd_ready"], g + 1)
                for t in range(4 * g, 4 * g + 4):
                    normalized(0, mv, y_all, y_all[:, t, :], t, "x1_ready")

            for n in range(NT - 4, NT):
                attn_step(Tile(n), True)
                if n < NT - 1:
                    aggregate(stats, mv, n - (NT - 4), "y_all_ready", "agg_ready")
                if n >= NT - 3:
                    first_norm(n - (NT - 3))
            residual(Tile(NT - 3))
            statistics(Tile(NT - 3))
            normalize(Tile(NT - 1))
            for n in (NT - 2, NT - 1):
                residual(Tile(n))
                statistics(Tile(n))
            aggregate(stats, mv, GROUPS - 1, "y_all_ready", "agg_ready")
            first_norm(GROUPS - 1)

            dve.wait_ge(S["sums_ready"], GROUPS)
            v.tensor_copy(sumT[:, 1, :], ps[:, 0, 0:B]).then_inc(S["sumT_ready"], 1)
            v.tensor_scalar(cols[:, 1:3], cols[:, 1:3], float(T), None, ALU.mult).then_inc(S["sk_ready"], 1)
            dve.wait_ge(S["sqk_done"], 1)
            dve.wait_ge(S["sk_ready"], 1)
            v.tensor_scalar(sqk[:, 0, :], ps[:, 2, 0:B], cols[:, 2:3], 1.0 / (H * T), ALU.add, ALU.mult).then_inc(S["sq_ready"], 1)
            dve.wait_ge(S["sq_ready"], 1)
            v.scalar_tensor_tensor(sqk[:, 2, :], ps[:, 2, B:2 * B], cols[:, 1:2], sqk[:, 0, :], ALU.add, ALU.mult).then_inc(S["prod_ready"], 1)
            dve.wait_ge(S["mean_done"], 1)
            mean = ps[0:B, 3, 0:8]
            v.tensor_reduce(wcol[:, 0:1], mean, AX.X, ALU.max).then_inc(S["m_max"], 1)
            dve.wait_ge(S["m_max"], 1)
            v.tensor_scalar(wsm[:, 0, :], mean, wcol[:, 0:1], None, ALU.subtract).then_inc(S["m_sub"], 1)
            dve.wait_ge(S["m_exp"], 1)
            v.tensor_reduce(wcol[:, 1:2], wsm[:, 1, :], AX.X, ALU.add).then_inc(S["m_sum"], 1)
            dve.wait_ge(S["m_sum"], 1)
            v.reciprocal(wcol[:, 2:3], wcol[:, 1:2]).then_inc(S["m_rec"], 1)
            dve.wait_ge(S["m_rec"], 1)
            v.tensor_scalar(wsm[:, 2, :], wsm[:, 1, :], wcol[:, 2:3], None, ALU.mult).then_inc(S["w_ready"], 1)
            dve.wait_ge(S["w_ready"], 1)
            v.tensor_tensor(w_tiles[:, :].rearrange("p (t c) -> p t c", c=8), const("batch_tile", B).rearrange("p (t c) -> p t c", c=8),
                            wsm[:, 2, :].unsqueeze(1).to_broadcast([B, NT, 8]), ALU.mult).then_inc(S["wt_ready"], 1)
            dve.wait_ge(S["wtok_done"], 1)
            v.tensor_copy(w_tok[:, :], ps[:, 3, 128:256]).then_inc(S["wtok_ready"], 1)
            dve.wait_ge(S["wtok_ready"], 1)
            def permute(half):
                n = NT // 2
                tiles = slice(half * n, half * n + n)
                taps = w_taps[:, :].rearrange("p (t r c) -> p t r c", r=8, c=8)[:, tiles, :, :]
                v.tensor_tensor(taps, w_tok[:, :].rearrange("p (t c) -> p t c", c=8)[:, tiles, :].unsqueeze(2).to_broadcast([P, n, 8, 8]),
                                const("tap_of").rearrange("p (r c) -> p r c", c=8).unsqueeze(1).to_broadcast([P, n, 8, 8]),
                                ALU.mult).then_inc(S["wtaps"], 1)
                dve.wait_ge(S["wtaps"], half + 1)
                v.tensor_reduce(w_perm[:, :].rearrange("p (t r) -> p t r", r=8)[:, tiles, :], taps, AX.X, ALU.add).then_inc(S["wperm_ready"], 1)

            permute(0)
            dve.wait_ge(S["wperm_ready"], 1)
            circulants(v, 0)
            permute(1)

            def second_sum(g):
                dve.wait_ge(S["mix_done"], g + 1)
                tiles = slice(4 * g, 4 * g + 4)
                v.tensor_tensor(y2_all[:, tiles, :], ps[:, 4 + g, :].rearrange("p (t d) -> p t d", d=D), y_all[:, tiles, :],
                                ALU.add).then_inc(S["y2_ready"], 1)

            def second_statistics(g):
                dve.wait_ge(S["y2_ready"], g + 1)
                for t in range(4 * g, 4 * g + 4):
                    v.bn_stats(stats2[:, t, :], y2_all[:, t, :]).then_inc(S["y2_stats"], 1)

            def second_norm(g):
                dve.wait_ge(S["rstd2_ready"], g + 1)
                for t in range(4 * g, 4 * g + 4):
                    normalized(1, mv2, y2_all, rows[:, t, 0:D], t, "x2_ready")

            def choose(g):
                tiles = slice(4 * g, 4 * g + 4)
                shape = [P, 4, E]
                lg_g, eqr_g = lg[:, tiles, :], eqr[:, tiles, :]
                dve.wait_ge(S["logits_done"], g + 1)
                v.tensor_tensor(lg_g, ps[:, g, 0:4 * E].rearrange("p (t e) -> p t e", e=E),
                                br_bc[:, :].unsqueeze(1).to_broadcast(shape), ALU.add).then_inc(S["lg_ready"], 1)
                dve.wait_ge(S["lg_ready"], g + 1)
                v.tensor_reduce(lmax[:, tiles], lg_g, AX.X, ALU.max).then_inc(S["lmax_ready"], 1)
                dve.wait_ge(S["lmax_ready"], g + 1)
                v.tensor_tensor(lg_g, lg_g, lmax[:, tiles].unsqueeze(2).to_broadcast(shape), ALU.subtract).then_inc(S["ld_ready"], 1)
                dve.wait_ge(S["ld_ready"], g + 1)
                v.tensor_scalar(eqr_g, lg_g, 0.0, None, ALU.is_equal).then_inc(S["eq_ready"], 1)
                dve.wait_ge(S["eq_ready"], g + 1)
                v.tensor_tensor(eqr_g, eqr_g, const("rev8").unsqueeze(1).to_broadcast(shape), ALU.mult).then_inc(S["eqr_ready"], 1)
                dve.wait_ge(S["eqr_ready"], g + 1)
                v.tensor_reduce(first[:, tiles], eqr_g, AX.X, ALU.max).then_inc(S["first_ready"], 1)
                dve.wait_ge(S["first_ready"], g + 1)
                v.tensor_tensor(onehot[:, tiles, :], eqr_g, first[:, tiles].unsqueeze(2).to_broadcast(shape), ALU.is_equal).then_inc(S["onehot_ready"], 1)
                dve.wait_ge(S["lex_ready"], g + 1)
                v.tensor_reduce(lsum[:, tiles], lex[:, tiles, :], AX.X, ALU.add).then_inc(S["lsum_ready"], 1)
                dve.wait_ge(S["lsum_ready"], g + 1)
                v.reciprocal(rows[:, tiles, D:D + 1].squeeze(2), lsum[:, tiles]).then_inc(S["gate_ready"], 1)

            def place(g):
                tiles = slice(4 * g, 4 * g + 4)
                dve.wait_ge(S["ranks_done"], g + 1)
                v.tensor_tensor(slot_f[:, tiles, :], ps[:, g, 64:64 + 4 * E].rearrange("p (t e) -> p t e", e=E),
                                const("region_at").unsqueeze(1).to_broadcast([P, 4, E]), ALU.add).then_inc(S["slot1"], 1)
                dve.wait_ge(S["slot1"], g + 1)
                v.tensor_tensor(slot_f[:, tiles, :], slot_f[:, tiles, :], onehot[:, tiles, :], ALU.mult).then_inc(S["slot2"], 1)
                dve.wait_ge(S["slot2"], g + 1)
                v.tensor_reduce(slot_a[:, tiles], slot_f[:, tiles, :], AX.X, ALU.add).then_inc(S["slot3"], 1)
                dve.wait_ge(S["slot3"], g + 1)
                v.tensor_copy(slots[:, tiles], slot_a[:, tiles]).then_inc(S["slots_ready"], 1)

            def second_aggregate(g):
                aggregate(stats2, mv2, g, "y2_stats", "agg2_ready")

            second_sum(0)
            second_statistics(0)
            second_aggregate(0)
            second_sum(1)
            second_statistics(1)
            second_norm(0)
            second_aggregate(1)
            second_sum(2)
            second_statistics(2)
            second_aggregate(2)
            second_norm(1)
            dve.wait_ge(S["router_in"], 32)
            choose(0)
            second_sum(3)
            place(0)
            second_norm(2)
            choose(1)
            second_statistics(3)
            second_aggregate(3)
            place(1)
            second_norm(3)
            choose(2)
            place(2)
            choose(3)
            place(3)

            dve.wait_ge(S["counts_done"], 1)
            v.tensor_copy(cnt_i[:, :], ps[:, 0, 0:E]).then_inc(S["cnt_ready"], 1)
            chained(v.tensor_copy(cnt[:, :], ps[:, 0, 0:E]))
            chained(v.tensor_tensor(over[:, :, :], cnt[:, :].unsqueeze(2).to_broadcast([P, E, 16]),
                                    const("thresholds").unsqueeze(1).to_broadcast([P, E, 16]), ALU.is_gt))
            chained(v.tensor_reduce(ntile[:, :], over[:, :, :], AX.X, ALU.add))
            v.tensor_scalar(jump[:, :], ntile[:, :], float(-P), float(REGION), ALU.mult, ALU.add)
            chained(v.tensor_tensor(tmp64[:, :, :], const("upto8").rearrange("p (a b) -> p a b", b=E),
                                    ntile[:, :].unsqueeze(1).to_broadcast([P, E, E]), ALU.mult))
            chained(v.tensor_reduce(end_t[:, :], tmp64[:, :, :], AX.X, ALU.add))
            chained(v.tensor_tensor(ge[:, :, :], const("slot_j").unsqueeze(2).to_broadcast([P, SLOTS, E]),
                                    end_t[:, :].unsqueeze(1).to_broadcast([P, SLOTS, E]), ALU.is_ge))
            chained(v.tensor_tensor(jumps[:, :, :], ge[:, :, :], jump[:, :].unsqueeze(1).to_broadcast([P, SLOTS, E]), ALU.mult))
            chained(v.tensor_reduce(row_f[:, :], jumps[:, :, :], AX.X, ALU.add))
            chained(v.tensor_tensor(row_f[:, :], row_f[:, :], const("slot_row"), ALU.add))
            v.tensor_scalar(row_at[:, :], row_f[:, :], float(E * REGION), None, ALU.min).then_inc(S["row_at_ready"], 1)
            v.tensor_reduce(e_f[:, :], ge[:, :, :], AX.X, ALU.add).then_inc(S["ef_ready"], 1)
            dve.wait_ge(S["ef_ready"], 1)
            v.tensor_scalar(e_i[:, :], e_f[:, :], float(E - 1), None, ALU.min).then_inc(S["e_ready"], 1)

            experts = Experts(dve)

            def add_b1(t):
                r = t.ring(2)
                e = experts.of(t)
                dve.wait_ge(S["up_done"], t.n + 1)
                v.tensor_tensor(hid[:, r, :], ps[:, r, :], b1_bc[:, bass.ds(e * F, F)], ALU.add).then_inc(S["hid_ready"], 1)
                if t.i is not None or t.c + 1 < SLOTS:
                    experts.load(t + 1)

            def combine(t, static):
                e = experts.of(t)
                r, q = t.ring(2), t.ring(RING)
                if not static or t.c >= RING:
                    dve.wait_ge(stored[q], t.turn(RING) * 16)
                if not static or t.c >= 2:
                    dve.wait_ge(S["z_ready"], t.n - 1)
                dve.wait_ge(S["down_done"], t.n + 1)
                v.tensor_tensor(z[:, r, :], ps[:, 6 + r, 0:D], b2_bc[:, bass.ds(e * D, D)], ALU.add).then_inc(S["z_a"], 1)
                dve.wait_ge(S["z_a"], t.n + 1)
                dve.wait_ge(gathered[q], (t.turn(RING) + 1) * 16)
                v.scalar_tensor_tensor(z[:, r, :], z[:, r, :], g_rows[:, q, D:D + 1], g_rows[:, q, 0:D], ALU.mult, ALU.add).then_inc(S["row_used"], 1)
                v.tensor_copy(z_token[:, q, :], g_rows[:, q, D + 1:D + 2].bitcast(I32)).then_inc(S["token_taken"], 1)

            def finish(t):
                r, q = t.ring(2), t.ring(RING)
                dve.wait_ge(S["z_rs"], t.n + 1)
                v.tensor_scalar(z_out[:, q, :], z[:, r, :], z_mv[:, r, 0:1], z_rstd[:, r, 1:2], ALU.subtract, ALU.mult).then_inc(S["z_ready"], 1)

            def z_statistics(t, static):
                r = t.ring(2)
                turn = count_first(dve, t.n + 1)
                dve.wait_ge(S["row_used"], turn)
                v.bn_stats(z_stats[:, r, :], z[:, r, :]).then_inc(S["z_st"], 1)
                if not static or t.c >= 1:
                    finish(t + -1)
                turn = count_first(dve, t.n + 1)
                dve.wait_ge(S["z_st"], turn)
                v.bn_aggr(z_mv[:, r, :], z_stats[:, r, :]).then_inc(S["z_agg"], 1)

            dve.wait_ge(S["e_ready"], 1)
            dve.wait_ge(S["ffn_in"], 64)
            experts.load(Tile(0))
            add_b1(Tile(0))
            add_b1(Tile(1))

            def expert_step(t, static):
                if not static or t.c + 2 < SLOTS:
                    add_b1(t + 2)
                combine(t, static)
                z_statistics(t, static)

            for n in range(RING):
                expert_step(Tile(n), True)
            n0 = (SLOTS - RING - 2) // RING
            with dve.Fori(0, n0) as i:
                for c in range(RING, 2 * RING):
                    expert_step(Tile(c, i, RING), False)
            for n in range(RING + RING * n0, SLOTS):
                expert_step(Tile(n), True)
            finish(Tile(SLOTS - 1))


def shape_constants():
    c = {}
    p = np.arange(P)
    c["ident"] = np.eye(P)
    ang = (p % T).astype(np.float32)[:, None] * (1.0 / 10000.0 ** (np.arange(0, 4, 2, dtype=np.float32) / 4)).astype(np.float32)[None]
    cos, sin = np.cos(ang), np.sin(ang)
    c["cos8"] = np.concatenate([cos, cos, np.ones((P, 4))], 1)
    c["sin4"] = np.concatenate([-sin, sin], 1)
    c["strip"] = (p[:, None] // 32 == np.arange(STRIPS)[None])
    c["strip_head"] = (p[:, None] // HD % HPS == np.arange(HPS)[None])
    c["head16"] = (p[:, None] // HD == np.arange(H)[None])
    c["chan8"] = (p[:, None] % HD == np.arange(8)[None])
    c["batch_rows"] = (p[:, None] % BPT == p[None] // T)
    c["batch_tile"] = (p[:, None] // BPT == p[None] // 8)
    c["tap_of"] = ((p[:, None, None] - np.arange(8)[None, :, None]) % 8 == np.arange(8)[None, None]).reshape(P, 64)
    c["band"] = (p[:, None] // T == p[None] // T) & ((p[:, None] - p[None]) % T < 8)
    c["batch_ind"] = (p[:, None] // T == np.arange(BPT)[None])
    c["rev8"] = np.broadcast_to(8 - np.arange(8)[None], (P, 8))
    c["thresholds"] = np.broadcast_to(P * np.arange(16)[None], (P, 16))
    c["region_at"] = np.broadcast_to(REGION * np.arange(E)[None], (P, E))
    c["slot_row"] = np.broadcast_to(P * np.arange(SLOTS)[None], (P, SLOTS))
    c["upto8"] = np.broadcast_to((np.arange(8)[None] <= np.arange(8)[:, None]).reshape(1, 64), (P, 64))
    c["same_pos"] = p[:, None] % T == np.arange(T)[None]
    c["slot_j"] = np.broadcast_to(np.arange(SLOTS)[None], (P, SLOTS))
    c["minus_half"] = np.full((P, 16), -0.5)
    c["causal"] = np.where(np.arange(T)[None] <= (p % T)[:, None], 0.0, -1e30)
    c["earlier"] = p[:, None] < p[None]
    f32 = np.concatenate([c[n].astype(np.float32) for n, _ in CONSTS], 1)
    ids = (P * np.arange(NT)[None] + p[:, None]).astype(np.int32)
    pad = np.zeros(ROW, np.int32)
    pad[D + 1] = NO_TOKEN
    return f32, ids, pad.view(np.float32)


def kernel(**inputs):
    import concourse.bacc as bacc
    from concourse.bass_utils import run_bass_kernel_spmd

    g = {k: np.asarray(v) for k, v in inputs.items()}
    x = g["x"].reshape(B * T, D)
    L = "L0_attn_"

    def headed(geo, sem):
        return np.concatenate([geo.reshape(-1, H, 4), sem.reshape(-1, H, 4)], 2).reshape(-1, P)

    f32, ids, pad = shape_constants()
    A = "L0_xattn_"
    M = "L0_ffn_"
    knull = headed(g[L + "k_geo_null"][None], g[L + "k_sem_null"][None])[0]
    arrays = {
        "consts": f32, "token_ids": ids, "pad_row": pad,
        "x": x, "xT": x.T, "ctxT": g["ctx_1024"].reshape(B * T, D).T,
        "wqk": np.concatenate([headed(g[L + "wq_geo"], g[L + "wq_sem"]), headed(g[L + "wk_geo"], g[L + "wk_sem"])], 1),
        "wv": g[L + "wv"], "wo": g[L + "wo"], "v_null": g[L + "v_null"],
        "cols": np.stack([knull, g[A + "bq"], g[A + "bk"], g[A + "bv"]], 1),
        "xattn_w": np.stack([g[A + "Wq"].T, g[A + "Wk"].T, g[A + "Wv"], g[A + "Wo"].T], 1),
        "bo": g[A + "bo"], "wr": g[M + "Wr"], "br": g[M + "br"],
        "w1": g[M + "W1"].transpose(1, 0, 2).reshape(P, E * F),
        "w2": g[M + "W2"].reshape(E, FC, P, D).transpose(2, 0, 1, 3).reshape(P, E * FC * D),
        "b1": g[M + "b1"].reshape(-1), "b2": g[M + "b2"].reshape(-1),
    }
    nc = bacc.Bacc("TRN2", target_bir_lowering=False, num_devices=1)
    arrays = {k: np.ascontiguousarray(v) for k, v in arrays.items()}
    aps = {k: nc.dram_tensor("in_" + k, v.shape, mybir.dt.from_np(v.dtype), kind="ExternalInput").ap() for k, v in arrays.items()}
    out = nc.dram_tensor("out_0", (B * T, D), F32, kind="ExternalOutput").ap()
    decoder_layer(nc, aps, out)
    r = run_bass_kernel_spmd(nc, [{"in_" + k: v for k, v in arrays.items()}], core_ids=[0])
    return r.results[0]["out_0"].reshape(B, T, D)
```
